# Optimizing a Trainium2 kernel written in Bass

```python
import numpy as np
import jax
import jax.numpy as jnp

def _softmax(x, axis=-1):
    return jax.nn.softmax(x, axis=axis)

def _gelu(x):
    return jax.nn.gelu(x, approximate=True)

def _silu(x):
    return jax.nn.silu(x)

def _sigmoid(x):
    return jax.nn.sigmoid(x)

def _layernorm(x, axis=-1, eps=1e-05):
    m = jnp.mean(x, axis=axis, keepdims=True)
    v = jnp.var(x, axis=axis, keepdims=True)
    return (x - m) / jnp.sqrt(v + eps)

def _scatter_add(tgt, idx, src, axis=0):
    return tgt.at[idx].add(src)

def _segment_sum(src, seg, n):
    return jax.ops.segment_sum(src, seg, n)
kernel_name = 'mk_decoder_preln_d1_seqx_r2_51509a'

def setup_inputs(seed: int=0):
    np.random.seed(seed)
    _w = jnp.asarray

    def _rec_inputs():
        import jax
        import jax.numpy as jnp
        _rk = jax.random.key(seed)
        x = -0.000125 + 0.9999 * jax.random.normal(jax.random.fold_in(_rk, 1), (2, 2048, 512), jnp.float32)
        _lenS = 2048 - jax.random.randint(jax.random.fold_in(_rk, 7), (2,), 0, max(1, 2048 // 4) + 1, jnp.int32)
        _lenS2 = 154 - jax.random.randint(jax.random.fold_in(_rk, 8), (2,), 0, max(1, 154 // 4) + 1, jnp.int32)
        _ctx_2048P = jax.random.normal(jax.random.fold_in(_rk, 11), (2, 16, 1024), jnp.float32)
        _ctx_2048c = jax.random.dirichlet(jax.random.fold_in(_rk, 511), 0.3 * jnp.ones((16,), jnp.float32), (2, 154))
        _ctx_2048t = jnp.einsum('bsk,bkd->bsd', _ctx_2048c, _ctx_2048P)
        _ctx_2048t = _ctx_2048t * jax.lax.rsqrt(jnp.mean(jnp.square(_ctx_2048t)) + 1e-12) * 0.953939
        ctx_2048 = -1.39393e-06 + 0.999914 * (_ctx_2048t + 0.3 * jax.random.normal(jax.random.fold_in(_rk, 611), (2, 154, 1024), jnp.float32))
        return (x, ctx_2048)
    x, ctx_2048 = _rec_inputs()

    def _L0_attn_setup():
        import jax, jax.numpy as jnp
        import numpy as np
        import math
        HEADS = 16
        SEG = 128
        DIL = 4
        BLOCK_M = 64

        def _hilbert_points(level, x=0, y=0, xi=1, xj=0, yi=0, yj=1):
            if level <= 0:
                yield (x, y)
            else:
                for pt in _hilbert_points(level - 1, x, y, yi // 2, yj // 2, xi // 2, xj // 2):
                    yield pt
                for pt in _hilbert_points(level - 1, x + xi // 2, y + xj // 2, xi // 2, xj // 2, yi // 2, yj // 2):
                    yield pt
                for pt in _hilbert_points(level - 1, x + xi // 2 + yi // 2, y + xj // 2 + yj // 2, xi // 2, xj // 2, yi // 2, yj // 2):
                    yield pt
                for pt in _hilbert_points(level - 1, x + xi // 2 + yi, y + xj // 2 + yj, -yi // 2, -yj // 2, -xi // 2, -xj // 2):
                    yield pt

        def create_hilbert_mapping(seq_len):
            grid = 2 ** int(math.ceil(math.log2(math.sqrt(seq_len))))
            pts = list(_hilbert_points(int(math.log2(grid)), 0, 0, grid, 0, 0, grid))
            m = np.zeros(seq_len, dtype=np.int32)
            for hidx, (x, y) in enumerate(pts[:seq_len]):
                lin = y * grid + x
                if lin < seq_len:
                    m[lin] = hidx
            return jnp.asarray(m)

        def _hilbert_attention(x, Wqkv, bqkv, Wproj, bproj, mapping):
            B, M, dim = x.shape
            H = HEADS
            D = dim // H
            scale = D ** (-0.5)
            qkv = (x @ Wqkv + bqkv).reshape(B, M, 3, H, D)
            qkv = jnp.transpose(qkv, (2, 0, 3, 1, 4))
            q, k, v = (qkv[0], qkv[1], qkv[2])
            nb = M // BLOCK_M
            rm = jnp.arange(M).reshape(nb, BLOCK_M)
            mrm = mapping[rm].astype(jnp.int32)
            seg_idx = mrm // SEG
            offs = jnp.arange(0, SEG, DIL)
            key_pos = seg_idx[:, :, None] * SEG + offs[None, None, :]
            mask_k = key_pos < M
            kp0 = key_pos[:, 0, :]
            mask0 = mask_k[:, 0, :]
            idx0 = jnp.where(mask0, mapping[jnp.clip(kp0, 0, M - 1)], 0)
            Ksel = k[:, :, idx0, :] * mask0[None, None, :, :, None]
            Vsel = v[:, :, idx0, :] * mask0[None, None, :, :, None]
            qm = q[:, :, mrm, :] * scale
            scores = jnp.einsum('bhnmd,bhnsd->bhnms', qm, Ksel)
            scores = jnp.where(mask_k[None, None], scores, -1000000000.0)
            sexp = jnp.exp(scores - jnp.max(scores, axis=3, keepdims=True))
            acc = jnp.einsum('bhnms,bhnsd->bhnmd', sexp, Vsel)
            lsum = 1e-06 + jnp.sum(sexp, axis=-1)
            out = acc / lsum[..., None]
            out = out.reshape(B, H, M, D).transpose(0, 2, 1, 3).reshape(B, M, dim)
            return out @ Wproj + bproj
        key = jax.random.key(seed)
        ks = jax.random.split(key, 5)
        B, M, dim = (2, 2048, 512)
        s = 1.0 / math.sqrt(dim)
        return {'x': jax.random.normal(ks[0], (B, M, dim), jnp.float32), 'Wqkv': jax.random.normal(ks[1], (dim, 3 * dim), jnp.float32) * s, 'bqkv': jax.random.normal(ks[2], (3 * dim,), jnp.float32) * 0.01, 'Wproj': jax.random.normal(ks[3], (dim, dim), jnp.float32) * s, 'bproj': jax.random.normal(ks[4], (dim,), jnp.float32) * 0.01, 'mapping': create_hilbert_mapping(M)}
    _L0_attn_all = _L0_attn_setup()
    _L0_attn_in = {k: v for k, v in _L0_attn_all.items() if k in ('Wqkv', 'bqkv', 'Wproj', 'bproj', 'mapping')}
    del _L0_attn_all

    def _L0_xattn_setup():
        import jax, jax.numpy as jnp
        import numpy as np
        B, N, DIM = (8, 2048, 512)
        M, CTX = (128, 1024)
        HEADS, DH = (16, 64)
        INNER = HEADS * DH
        EPS = 1e-06

        def _split_heads(t):
            b, n, _ = t.shape
            return t.reshape(b, n, HEADS, DH).transpose(0, 2, 1, 3)
        key = jax.random.key(seed)
        ks = jax.random.split(key, 6)
        x = jax.random.normal(ks[0], (B, N, DIM), dtype=jnp.float32)
        context = jax.random.normal(ks[1], (B, M, CTX), dtype=jnp.float32)
        Wq = jax.random.normal(ks[2], (DIM, INNER), dtype=jnp.float32) / np.sqrt(DIM)
        Wkv = jax.random.normal(ks[3], (CTX, 2 * INNER), dtype=jnp.float32) / np.sqrt(CTX)
        null_kv = jax.random.normal(ks[4], (2, DH), dtype=jnp.float32) / np.sqrt(2.0)
        Wout = jax.random.normal(ks[5], (INNER, DIM), dtype=jnp.float32) / np.sqrt(INNER)
        ln_scale = jnp.ones((DIM,), dtype=jnp.float32)
        ln_bias = jnp.zeros((DIM,), dtype=jnp.float32)
        return {'x': x, 'context': context, 'Wq': Wq, 'Wkv': Wkv, 'null_kv': null_kv, 'Wout': Wout, 'ln_scale': ln_scale, 'ln_bias': ln_bias}
    _L0_xattn_all = _L0_xattn_setup()
    _L0_xattn_in = {k: v for k, v in _L0_xattn_all.items() if k in ('Wq', 'Wkv', 'null_kv', 'Wout', 'ln_scale', 'ln_bias')}
    del _L0_xattn_all

    def _L0_ffn_setup():
        import jax, jax.numpy as jnp
        import numpy as np
        key = jax.random.key(seed)
        ks = jax.random.split(key, 5)
        B, T, D, E = (4, 1024, 512, 8)
        inputs = jax.random.normal(ks[0], (B, T, D), dtype=jnp.float32)
        Wr = jax.random.normal(ks[1], (D, E), dtype=jnp.float32) * 0.02
        br = jnp.zeros((E,), dtype=jnp.float32)
        W1 = jax.random.normal(ks[2], (E, D, D), dtype=jnp.float32) * 0.02
        b1 = jnp.zeros((E, D), dtype=jnp.float32)
        W2 = jax.random.normal(ks[3], (E, D, D), dtype=jnp.float32) * 0.02
        b2 = jnp.zeros((E, D), dtype=jnp.float32)
        return {'inputs': inputs, 'Wr': Wr, 'br': br, 'W1': W1, 'b1': b1, 'W2': W2, 'b2': b2}
    _L0_ffn_all = _L0_ffn_setup()
    _L0_ffn_in = {k: v for k, v in _L0_ffn_all.items() if k in ('Wr', 'br', 'W1', 'b1', 'W2', 'b2')}
    del _L0_ffn_all
    return {'x': x, 'ctx_2048': ctx_2048, 'L0_attn_Wqkv': _L0_attn_in['Wqkv'], 'L0_attn_bqkv': _L0_attn_in['bqkv'], 'L0_attn_Wproj': _L0_attn_in['Wproj'], 'L0_attn_bproj': _L0_attn_in['bproj'], 'L0_attn_mapping': _L0_attn_in['mapping'], 'L0_xattn_Wq': _L0_xattn_in['Wq'], 'L0_xattn_Wkv': _L0_xattn_in['Wkv'], 'L0_xattn_null_kv': _L0_xattn_in['null_kv'], 'L0_xattn_Wout': _L0_xattn_in['Wout'], 'L0_xattn_ln_scale': _L0_xattn_in['ln_scale'], 'L0_xattn_ln_bias': _L0_xattn_in['ln_bias'], 'L0_ffn_Wr': _L0_ffn_in['Wr'], 'L0_ffn_br': _L0_ffn_in['br'], 'L0_ffn_W1': _L0_ffn_in['W1'], 'L0_ffn_b1': _L0_ffn_in['b1'], 'L0_ffn_W2': _L0_ffn_in['W2'], 'L0_ffn_b2': _L0_ffn_in['b2']}

def reference(x, ctx_2048, L0_attn_Wqkv, L0_attn_bqkv, L0_attn_Wproj, L0_attn_bproj, L0_attn_mapping, L0_xattn_Wq, L0_xattn_Wkv, L0_xattn_null_kv, L0_xattn_Wout, L0_xattn_ln_scale, L0_xattn_ln_bias, L0_ffn_Wr, L0_ffn_br, L0_ffn_W1, L0_ffn_b1, L0_ffn_W2, L0_ffn_b2):
    import jax
    import jax.numpy as jnp

    def _L0_attn_ref(x, Wqkv, bqkv, Wproj, bproj, mapping):
        import jax, jax.numpy as jnp
        import numpy as np
        import math
        HEADS = 16
        SEG = 128
        DIL = 4
        BLOCK_M = 64

        def _hilbert_points(level, x=0, y=0, xi=1, xj=0, yi=0, yj=1):
            if level <= 0:
                yield (x, y)
            else:
                for pt in _hilbert_points(level - 1, x, y, yi // 2, yj // 2, xi // 2, xj // 2):
                    yield pt
                for pt in _hilbert_points(level - 1, x + xi // 2, y + xj // 2, xi // 2, xj // 2, yi // 2, yj // 2):
                    yield pt
                for pt in _hilbert_points(level - 1, x + xi // 2 + yi // 2, y + xj // 2 + yj // 2, xi // 2, xj // 2, yi // 2, yj // 2):
                    yield pt
                for pt in _hilbert_points(level - 1, x + xi // 2 + yi, y + xj // 2 + yj, -yi // 2, -yj // 2, -xi // 2, -xj // 2):
                    yield pt

        def create_hilbert_mapping(seq_len):
            grid = 2 ** int(math.ceil(math.log2(math.sqrt(seq_len))))
            pts = list(_hilbert_points(int(math.log2(grid)), 0, 0, grid, 0, 0, grid))
            m = np.zeros(seq_len, dtype=np.int32)
            for hidx, (x, y) in enumerate(pts[:seq_len]):
                lin = y * grid + x
                if lin < seq_len:
                    m[lin] = hidx
            return jnp.asarray(m)

        def _hilbert_attention(x, Wqkv, bqkv, Wproj, bproj, mapping):
            B, M, dim = x.shape
            H = HEADS
            D = dim // H
            scale = D ** (-0.5)
            qkv = (x @ Wqkv + bqkv).reshape(B, M, 3, H, D)
            qkv = jnp.transpose(qkv, (2, 0, 3, 1, 4))
            q, k, v = (qkv[0], qkv[1], qkv[2])
            nb = M // BLOCK_M
            rm = jnp.arange(M).reshape(nb, BLOCK_M)
            mrm = mapping[rm].astype(jnp.int32)
            seg_idx = mrm // SEG
            offs = jnp.arange(0, SEG, DIL)
            key_pos = seg_idx[:, :, None] * SEG + offs[None, None, :]
            mask_k = key_pos < M
            kp0 = key_pos[:, 0, :]
            mask0 = mask_k[:, 0, :]
            idx0 = jnp.where(mask0, mapping[jnp.clip(kp0, 0, M - 1)], 0)
            Ksel = k[:, :, idx0, :] * mask0[None, None, :, :, None]
            Vsel = v[:, :, idx0, :] * mask0[None, None, :, :, None]
            qm = q[:, :, mrm, :] * scale
            scores = jnp.einsum('bhnmd,bhnsd->bhnms', qm, Ksel)
            scores = jnp.where(mask_k[None, None], scores, -1000000000.0)
            sexp = jnp.exp(scores - jnp.max(scores, axis=3, keepdims=True))
            acc = jnp.einsum('bhnms,bhnsd->bhnmd', sexp, Vsel)
            lsum = 1e-06 + jnp.sum(sexp, axis=-1)
            out = acc / lsum[..., None]
            out = out.reshape(B, H, M, D).transpose(0, 2, 1, 3).reshape(B, M, dim)
            return out @ Wproj + bproj
        return _hilbert_attention(x, Wqkv, bqkv, Wproj, bproj, mapping)

    def _L0_xattn_ref(x, context, Wq, Wkv, null_kv, Wout, ln_scale, ln_bias):
        import jax, jax.numpy as jnp
        import numpy as np
        B, N, DIM = (8, 2048, 512)
        M, CTX = (128, 1024)
        HEADS, DH = (16, 64)
        INNER = HEADS * DH
        EPS = 1e-06

        def _split_heads(t):
            b, n, _ = t.shape
            return t.reshape(b, n, HEADS, DH).transpose(0, 2, 1, 3)
        scale = DH ** (-0.5)
        b = x.shape[0]
        q = _split_heads(jnp.einsum('bnd,df->bnf', x, Wq))
        kv = jnp.einsum('bmc,cf->bmf', context, Wkv)
        k, v = jnp.split(kv, 2, axis=-1)
        k, v = (_split_heads(k), _split_heads(v))
        nk = jnp.broadcast_to(null_kv[0], (b, HEADS, 1, DH))
        nv = jnp.broadcast_to(null_kv[1], (b, HEADS, 1, DH))
        k = jnp.concatenate((nk, k), axis=-2)
        v = jnp.concatenate((nv, v), axis=-2)
        q = q * scale
        sim = jnp.einsum('bhid,bhjd->bhij', q, k)
        attn = jax.nn.softmax(sim, axis=-1)
        out = jnp.einsum('bhij,bhjd->bhid', attn, v)
        out = out.transpose(0, 2, 1, 3).reshape(b, -1, INNER)
        out = jnp.einsum('bnf,fd->bnd', out, Wout)
        mu = jnp.mean(out, axis=-1, keepdims=True)
        var = jnp.var(out, axis=-1, keepdims=True)
        out = (out - mu) * jax.lax.rsqrt(var + EPS) * ln_scale + ln_bias
        return out

    def _L0_ffn_ref(inputs, Wr, br, W1, b1, W2, b2):
        import jax, jax.numpy as jnp
        import numpy as np
        B, T, D = inputs.shape
        E = Wr.shape[1]
        x = inputs.reshape(B * T, D)
        N = x.shape[0]
        C = N // E
        logits = x @ Wr + br
        probs = jax.nn.softmax(logits, axis=-1)
        gate = jnp.max(probs, axis=-1, keepdims=True)
        idx = jnp.argmax(probs, axis=-1)
        mask = jax.nn.one_hot(idx, E, dtype=jnp.float32)
        pos = (jnp.cumsum(mask, axis=0) * mask).astype(jnp.int32)
        mask = mask * (pos < C).astype(jnp.float32)
        mask_flat = jnp.sum(mask, axis=-1, keepdims=True)
        gate = gate * mask_flat
        combine = (gate * mask_flat * jax.nn.one_hot(idx, E, dtype=jnp.float32))[..., None] * jax.nn.one_hot(pos, C, dtype=jnp.float32)
        dispatch = combine
        expert_in = jnp.einsum('nd,nec->ecd', x, dispatch)
        h = jax.nn.relu(jnp.einsum('ecd,edf->ecf', expert_in, W1) + b1[:, None, :])
        eo = jnp.einsum('ecf,efd->ecd', h, W2) + b2[:, None, :]
        out = jnp.einsum('ecd,nec->nd', eo, combine)
        return out.reshape(B, T, D)
    x = x + _L0_attn_ref(_layernorm(x, axis=-1), L0_attn_Wqkv, L0_attn_bqkv, L0_attn_Wproj, L0_attn_bproj, L0_attn_mapping)
    x = x + _L0_xattn_ref(_layernorm(x, axis=-1), ctx_2048, L0_xattn_Wq, L0_xattn_Wkv, L0_xattn_null_kv, L0_xattn_Wout, L0_xattn_ln_scale, L0_xattn_ln_bias)
    x = x + _L0_ffn_ref(_layernorm(x, axis=-1), L0_ffn_Wr, L0_ffn_br, L0_ffn_W1, L0_ffn_b1, L0_ffn_W2, L0_ffn_b2)
    return x

_drawn_inputs = setup_inputs


def setup_inputs(seed=0):
    import zlib

    import numpy as np

    out = dict(_drawn_inputs(seed))
    spreads = {'L0_xattn_ln_scale': (1.0, 0.2),
     'L0_xattn_ln_bias': (0.0, 0.1),
     'L0_ffn_br': (0.0, 0.742),
     'L0_ffn_b1': (0.0, 0.8),
     'L0_ffn_b2': (0.0, 0.628)}
    factors = {'L0_attn_bqkv': 7.32,
     'L0_attn_bproj': 7.68,
     'L0_xattn_null_kv': 5.819,
     'L0_ffn_Wr': 4.21,
     'L0_ffn_W1': 8.0,
     'L0_ffn_W2': 8.0}
    for name, (base, spread) in spreads.items():
        noise = np.random.default_rng([zlib.crc32(name.encode()), seed]).standard_normal(out[name].shape)
        drawn = base * np.exp(spread * noise) if base else spread * noise
        out[name] = jnp.asarray(drawn.astype(out[name].dtype))
    for name, factor in factors.items():
        out[name] = (out[name] * factor).astype(out[name].dtype)
    return out
```

```python
import concourse.bass as bass
from concourse import mybir
from concourse.alu_op_type import AluOpType as ALU
from contextlib import ExitStack

F32 = mybir.dt.float32
F32R = mybir.dt.float32r
I32 = mybir.dt.int32
ACT = mybir.ActivationFunctionType
AX = mybir.AxisListType

P = 128
B, M, D = 2, 2048, 512
T = B * M
NT = T // P
G = 4
NG = NT // G
KD = D // P
H1, D1, SEG, DIL, BLK = 16, 32, 128, 4, 64
NSEG = M // SEG
NKEY = SEG // DIL
SCALE1 = float(D1) ** -0.5
EPS_SUM = 1e-6
EPS1 = 1e-5
H2, D2, CTX, LC = 16, 64, 1024, 154
KC = CTX // P
REM = LC - P
L2 = LC + 1
PW = 160
INNER = H2 * D2
KI = INNER // P
SCALE2 = float(D2) ** -0.5
EPS2 = 1e-6
E = 8
CAP = T // E
ROW = D + 2
NOBODY = 2 * T


def need(eng, sem, value):
    if not isinstance(value, int) or value > 0:
        eng.wait_ge(sem, value)


def hold(eng, sem, value):
    if not isinstance(value, int) or value > 0:
        eng.wait_ge(sem, value)
        eng.nop(nofuse=True)


def product(pe, out, lhs, rhs, first, last):
    (lh, ll), (rh, rl) = lhs, rhs
    pe.matmul(out, lh, rh, start=first, stop=False)
    pe.matmul(out, lh, rl, start=False, stop=False)
    return pe.matmul(out, ll, rh, start=False, stop=last)


def decoder_kernel(nc, x, ctx, wqkv, bqkv, wproj, bproj, mapping, wq2, wkv2, null_kv, wout, ln_scale, ln_bias,
                   wr, br, w1, b1, w2, b2, out):
    x_rows = x.rearrange("b t d -> (b t) d")
    x_tiles = x_rows.rearrange("(n p) d -> p n d", p=P)
    out_rows = out.rearrange("b t d -> (b t) d")
    out_tiles = out_rows.rearrange("(n p) d -> p n d", p=P)
    x1_dram = nc.dram_tensor("x1_scratch", (T, D), F32, kind="Internal").ap()
    x1_tiles = x1_dram.rearrange("(n p) d -> p n d", p=P)
    slots_dram = nc.dram_tensor("slot_rows", (2 * T, ROW), F32, kind="Internal").ap()
    slot_tiles = slots_dram.rearrange("(n p) d -> p n d", p=P)

    with ExitStack() as keep:
        def sb(name, shape, dt=F32, stack=keep):
            return stack.enter_context(nc.sbuf_tensor(name, shape, dt))

        taken = []

        def sem(name):
            taken.append(nc.alloc_semaphore(name=name))
            return taken[-1]

        def release_sems():
            nc.clear_and_free_semaphores(taken)
            nc.all_engine_barrier()
            taken.clear()

        bank = [keep.enter_context(nc.psum_tensor(f"bank{n}", [P, 512], F32)) for n in range(8)]

        ident = sb("ident", [P, P])
        upper = sb("upper", [P, P])
        ones = sb("ones", [P, P])
        head_mask = sb("head_mask", [P, 4])
        minus_half = sb("minus_half", [P, 4])
        rev = sb("rev", [P, E])
        token_int = sb("token_int", [P, NT], I32)
        token_f = sb("token_f", [P, NT])
        lns_b = sb("lns_b", [P, D])
        lnb_b = sb("lnb_b", [P, D])
        br_b = sb("br_b", [P, E])
        wr_sb = sb("wr_sb", [P, KD, E])
        k2 = sb("k2", [P, B, KI, 2, L2])
        v2_main = sb("v2_main", [P, B, INNER])
        v2_rest = sb("v2_rest", [P, B, 4, 4 * D2])

        stage_a = ExitStack()
        with stage_a:
            wq_h = sb("wq_h", [P, KD, D], F32R, stage_a)
            wq_l = sb("wq_l", [P, KD, D], F32R, stage_a)
            wp_h = sb("wp_h", [P, KD, D], F32R, stage_a)
            wp_l = sb("wp_l", [P, KD, D], F32R, stage_a)
            bproj_b = sb("bproj_b", [P, D], F32, stage_a)
            bq_col = sb("bq_col", [P, KD], F32, stage_a)
            k1 = sb("k1", [P, KD, B * NSEG, NKEY], F32, stage_a)
            v1 = sb("v1", [P, B * NSEG, KD * D1], F32, stage_a)
            idx_all = sb("idx_all", [P, NT], I32, stage_a)
            head_ones = sb("head_ones", [P, P], F32, stage_a)
            seg_tab = sb("seg_tab", [1, T // BLK], I32, stage_a)
            with ExitStack() as st:
                setup(nc, sem, lambda *a: sb(*a, stack=st), bank, x_rows, ctx, wqkv, bqkv, wproj, bproj, mapping, wkv2,
                      null_kv, ln_scale, ln_bias, wr, br, slot_tiles, ident, upper, ones, head_mask, minus_half, rev,
                      token_int, token_f, bproj_b, lns_b, lnb_b, br_b, wr_sb, k2, v2_main, v2_rest,
                      wq_h, wq_l, wp_h, wp_l, bq_col, k1, v1, idx_all, head_ones, seg_tab)
            release_sems()
            with ExitStack() as st:
                self_attention(nc, sem, lambda *a: sb(*a, stack=st), bank, x_rows, x_tiles, x1_tiles, ident, head_mask,
                               minus_half, bproj_b, wq_h, wq_l, wp_h, wp_l, bq_col, k1, v1, idx_all, head_ones,
                               seg_tab)
        release_sems()
        with ExitStack() as st:
            cross_attention(nc, sem, lambda *a: sb(*a, stack=st), bank, x1_tiles, out_tiles, slots_dram, wq2, wout,
                            ident, upper, ones, minus_half, rev, token_int, token_f, lns_b, lnb_b, br_b, wr_sb, k2,
                            v2_main, v2_rest)
        release_sems()
        with ExitStack() as st:
            experts(nc, sem, lambda *a: sb(*a, stack=st), bank, slot_tiles, out_rows, w1, b1, w2, b2, ident,
                    minus_half)


def setup(nc, sem, sb, bank, x_rows, ctx, wqkv, bqkv, wproj, bproj, mapping, wkv2, null_kv, ln_scale, ln_bias, wr, br,
          slot_tiles, ident, upper, ones, head_mask, minus_half, rev, token_int, token_f, bproj_b, lns_b, lnb_b, br_b,
          wr_sb, k2, v2_main, v2_rest, wq_h, wq_l, wp_h, wp_l, bq_col, k1, v1, idx_all, head_ones, seg_tab):
    CB = 256
    NC = 2 * INNER // CB
    KB, HB = NC // 2, CB // P
    raw = sb("raw", [P, 2, 2048])
    wc_h = sb("wc_h", [P, 2, 8, CB], F32R)
    wc_l = sb("wc_l", [P, 2, 8, CB], F32R)
    ctx_sb = sb("ctx_sb", [P, 3, CTX])
    ct_h = sb("ct_h", [P, KC, 3 * P], F32R)
    ct_l = sb("ct_l", [P, KC, 3 * P], F32R)
    xk = ctx_sb[:, 0:2, :].rearrange("p a (b d) -> p (a b) d", d=D)
    xkt_h = ct_h[:, :, :].rearrange("p k t -> p (k t)")[:, 0:KD * 512].rearrange("p (k t) -> p k t", k=KD)
    xkt_l = ct_l[:, :, :].rearrange("p k t -> p (k t)")[:, 0:KD * 512].rearrange("p (k t) -> p k t", k=KD)
    v_tmp = sb("v_tmp", [P, 2, D])
    v_last = v_tmp[:, :, :].rearrange("p a d -> p (a d)")
    bk_col = sb("bk_col", [P, KD])
    bv_b = sb("bv_b", [P, D])
    null_k = sb("null_k", [P, 1])
    map_raw = sb("map_raw", [P, NT], I32)
    kmap = sb("kmap", [P, 4], I32)
    kidx = sb("kidx", [P, B, 4], I32)
    seg_raw = sb("seg_raw", [1, T // BLK], I32)
    empty_row = sb("empty_row", [P, ROW])
    stats = sb("stats", [P, 4, 6])
    mv = sb("mv", [P, 4, 2])
    var_eps = sb("var_eps", [P, 4])
    rstd = sb("rstd", [P, 4])

    maps_loaded, ctx_loaded, biases_loaded = sem("maps_loaded"), sem("ctx_loaded"), sem("biases_loaded")
    raw_loaded = [sem("raw_loaded0"), sem("raw_loaded1")]
    raw_high, raw_low = sem("raw_high"), sem("raw_low")
    zeroed, masks, tables = sem("zeroed"), sem("masks"), sem("tables")
    ctx_zeroed, null_k_loaded, null_v_loaded = sem("ctx_zeroed"), sem("null_k_loaded"), sem("null_v_loaded")
    prefilled, empty_made, rest_placed = sem("prefilled"), sem("empty_made"), sem("rest_placed")
    turned, turned_high, turned_low = sem("turned"), sem("turned_high"), sem("turned_low")
    kv_done, block_done, kv_evac = sem("kv_done"), sem("block_done"), sem("kv_evac")
    xk_loaded, xk_stats, xk_aggr, xk_eps = sem("xk_loaded"), sem("xk_stats"), sem("xk_aggr"), sem("xk_eps")
    xk_rstd, xk_norm, v_done, v_biased = sem("xk_rstd"), sem("xk_norm"), sem("v_done"), sem("v_biased")
    v_copied, v_copied_act = sem("v_copied"), sem("v_copied_act")

    units = []
    for n in range(NC):
        units.append((wkv2[:, n * CB:(n + 1) * CB], 8, wc_h[:, n % 2, :, :], wc_l[:, n % 2, :, :]))
    for part in range(2):
        units.append((wqkv[:, (part + 1) * D:(part + 2) * D], 4,
                      *(a[:, part, :, :].rearrange("p k n -> p (k n)").rearrange("p (k n) -> p k n", k=4)
                        for a in (wc_h, wc_l))))
    wkv_a = [(units[NC + part][2], units[NC + part][3]) for part in range(2)]
    units.append((wqkv[:, 0:D], 4, wq_h[:, :, :], wq_l[:, :, :]))
    units.append((wproj[:, :], 4, wp_h[:, :, :], wp_l[:, :, :]))
    NU = len(units)
    CR = 3 * 2
    NR = CR + 4 * B

    block = nc.Block()
    with block as block:
        @block.sync
        def _(sp):
            with nc.allow_non_contiguous_dma(reason="small tables by column"):
                for b in range(B):
                    sp.dma_start(map_raw[:, b * 16:(b + 1) * 16],
                                 mapping.rearrange("(n p) -> p n", p=P)).then_inc(maps_loaded, 16)
                    sp.dma_start(seg_raw[0:1, b * 32:(b + 1) * 32],
                                 mapping.rearrange("(a n f) -> a n f", a=1, f=BLK)[:, :, 0]).then_inc(maps_loaded, 16)
                sp.dma_start(kmap[:, :], mapping.rearrange("(n p f) -> p n f", p=P, f=DIL)[:, :, 0])\
                    .then_inc(maps_loaded, 16)
            for b in range(B):
                sp.dma_start(ctx_sb[:, b, :], ctx[b, 0:P, :]).then_inc(ctx_loaded, 16)
            sp.wait_ge(ctx_zeroed, 1)
            for b in range(B):
                sp.dma_start(ctx_sb[32 * b:32 * b + REM, 2, :], ctx[b, P:LC, :]).then_inc(ctx_loaded, 16)
            for u, (src, chunks, _, _) in enumerate(units):
                need(sp, raw_low, u - 1)
                sp.dma_start(raw[:, u % 2, :].rearrange("p (k n) -> p k n", k=chunks),
                             src.rearrange("(k p) n -> p k n", p=P))\
                    .then_inc(raw_loaded[u % 2], 16)
            sp.wait_ge(kv_evac, KB * HB + KB * 3)
            sp.wait_ge(zeroed, 1)
            for b in range(B):
                for h in range(4):
                    sp.dma_start(v2_rest[h:h + 4 * (REM - 1) + 1:4, b, :, h * D2:(h + 1) * D2],
                                 v_last[32 * b:32 * b + REM, :].rearrange("p (g h d) -> p g h d", g=4, h=4)
                                 [:, :, h, :]).then_inc(rest_placed, 16)
            sp.wait_ge(empty_made, 2)
            sp.dma_start(slot_tiles[:, 0:NT, :],
                         empty_row[:, :].rearrange("p (a d) -> p a d", a=1).to_broadcast([P, NT, ROW]))\
                .then_inc(prefilled, 16)
            sp.wait_ge(prefilled, 16)
            sp.wait_ge(rest_placed, 16 * 4 * B)

        @block.gpsimd
        def _(pool):
            pool.memset(ctx_sb[:, 2, :], 0.0).then_inc(ctx_zeroed, 1)
            pool.memset(ident[:, :], 0.0).then_inc(masks, 1)
            pool.memset(upper[:, :], 1.0).then_inc(masks, 1)
            pool.memset(head_mask[:, :], 1.0).then_inc(masks, 1)
            pool.memset(ones[:, :], 1.0).then_inc(masks, 1)
            pool.memset(minus_half[:, :], -0.5).then_inc(masks, 1)
            pool.wait_ge(masks, 5)
            pool.affine_select(out=ident[:, :], in_=ident[:, :], compare_op=ALU.not_equal, fill=1.0, base=0,
                               pattern=[[-1, P]], channel_multiplier=1).then_inc(masks, 1)
            pool.affine_select(out=upper[:, :], in_=upper[:, :], compare_op=ALU.is_ge, fill=0.0, base=0,
                               pattern=[[1, P]], channel_multiplier=-1).then_inc(masks, 1)
            pool.affine_select(out=head_mask[:, :], in_=head_mask[:, :], compare_op=ALU.is_ge, fill=0.0, base=0,
                               pattern=[[-32, 4]], channel_multiplier=1).then_inc(masks, 1)
            pool.wait_ge(masks, 8)
            pool.affine_select(out=head_mask[:, :], in_=head_mask[:, :], compare_op=ALU.is_ge, fill=0.0, base=31,
                               pattern=[[32, 4]], channel_multiplier=-1).then_inc(masks, 1)
            pool.iota(token_int[:, :], pattern=[[P, NT]], base=0, channel_multiplier=1).then_inc(masks, 1)
            pool.wait_ge(tables, 1)
            for b in range(B):
                pool.wait_ge(turned, CR + 4 * b)
                for n in range(4):
                    pool.indirect_dma_start(out=xk[:, n, :], out_offset=None, in_=x_rows,
                                            in_offset=bass.IndirectOffsetOnAxis(ap=kidx[:, b, n:n + 1], axis=0))\
                        .then_inc(xk_loaded, 16)
                pool.wait_ge(xk_eps, b + 1)
                pool.tensor_tensor(rstd[:, :], var_eps[:, :], minus_half[:, :], ALU.pow).then_inc(xk_rstd, 1)

        @block.scalar
        def _(act):
            with nc.allow_non_contiguous_dma(reason="small biases by column"):
                act.dma_start(bq_col[:, :], bqkv[0:D].rearrange("(c p) -> p c", p=P)).then_inc(biases_loaded, 16)
                act.dma_start(bk_col[:, :], bqkv[D:2 * D].rearrange("(c p) -> p c", p=P)).then_inc(biases_loaded, 16)
                act.dma_start(bv_b[:, :], bqkv[2 * D:3 * D].partition_broadcast(P)).then_inc(biases_loaded, 16)
                act.dma_start(bproj_b[:, :], bproj.partition_broadcast(P)).then_inc(biases_loaded, 16)
                act.dma_start(lns_b[:, :], ln_scale.partition_broadcast(P)).then_inc(biases_loaded, 16)
                act.dma_start(lnb_b[:, :], ln_bias.partition_broadcast(P)).then_inc(biases_loaded, 16)
                act.dma_start(br_b[:, :], br.partition_broadcast(P)).then_inc(biases_loaded, 16)
                act.dma_start(wr_sb[:, :, :], wr.rearrange("(k p) e -> p k e", p=P)).then_inc(biases_loaded, 16)
                for s in range(2):
                    act.dma_start(null_k[s * D2:(s + 1) * D2, :], null_kv[0, :].rearrange("(d a) -> d a", a=1))\
                        .then_inc(null_k_loaded, 16)
                act.wait_ge(zeroed, 1)
                for b in range(B):
                    for h in range(4):
                        act.dma_start(v2_rest[4 * REM + h:4 * REM + h + 1, b, :, h * D2:(h + 1) * D2],
                                      null_kv[1:2, :].rearrange("a (o d) -> a o d", o=1).to_broadcast([1, 4, D2]))\
                            .then_inc(null_v_loaded, 16)

            def split(u):
                if 2 <= u < NC + 2:
                    act.wait_ge(block_done, u - 1)
                act.wait_ge(raw_loaded[u % 2], 16 * (u // 2 + 1))
                act.activation(units[u][2], raw[:, u % 2, :].rearrange("p (k n) -> p k n", k=units[u][1]), ACT.Copy).then_inc(raw_high, 1)

            def turn(r):
                act.wait_ge(turned, r + 1)
                if r < CR:
                    dst = ct_h[:, 4 * (r % 2):4 * (r % 2) + 4, (r // 2) * P:(r // 2 + 1) * P]
                else:
                    dst = xkt_h[:, :, ((r - CR) % 4) * P:((r - CR) % 4 + 1) * P]
                act.activation(dst, bank[r % 2][:, :].rearrange("p (k t) -> p k t", k=4), ACT.Copy)\
                    .then_inc(turned_high, 1)

            for r in range(CR):
                turn(r)
            split(0)
            m = 0
            for n in range(NC):
                split(n + 1)
                for c in range(HB if n < KB else 3):
                    act.wait_ge(kv_done, m + 1)
                    src = bank[2 + m % 3]
                    if n < KB:
                        act.wait_ge(zeroed, 2)
                        for s in range(2):
                            rows = slice(s * D2, (s + 1) * D2)
                            act.activation(k2[rows, :, HB * n + c, s, 0:P],
                                           src[rows, 0:2 * P].rearrange("p (b k) -> p b k", b=B), ACT.Copy,
                                           scale=SCALE2)
                            last = act.activation(
                                k2[rows, :, HB * n + c, s, P:LC],
                                src[rows, 2 * P:2 * P + 64].rearrange("p (b k) -> p b k", b=B)[:, :, 0:REM],
                                ACT.Copy, scale=SCALE2)
                    elif c < 2:
                        last = act.activation(v2_main[:, c, (n - KB) * CB:(n - KB + 1) * CB], src[:, 0:CB], ACT.Copy)
                    else:
                        last = act.activation(v_last[0:64, (n - KB) * CB:(n - KB + 1) * CB], src[0:64, 0:CB], ACT.Copy)
                    last.then_inc(kv_evac, 1)
                    m += 1
            split(NC + 1)
            act.wait_ge(null_k_loaded, 32)
            for s in range(2):
                rows = slice(s * D2, (s + 1) * D2)
                act.activation(k2[rows, :, :, s, LC:L2],
                               null_k[rows, 0:1].rearrange("p (a b c) -> p a b c", a=1, b=1)
                               .to_broadcast([D2, B, KI, 1]), ACT.Copy, scale=SCALE2)
            for u in range(NC + 2, NU):
                split(u)
            act.wait_ge(biases_loaded, 16 * 8)
            for b in range(B):
                for n in range(4):
                    turn(CR + 4 * b + n)
                for c in range(KD):
                    act.wait_ge(kv_done, m + 1)
                    act.activation(k1[:, c, b * NSEG:b * NSEG + NSEG, :],
                                   bank[2 + m % 3][:, :].rearrange("p (s k) -> p s k", s=NSEG), ACT.Identity,
                                   bias=bk_col[:, c:c + 1]).then_inc(kv_evac, 1)
                    m += 1
                for n in range(4):
                    i = 4 * b + n
                    act.wait_ge(v_biased, i + 1)
                    for s in range(4):
                        for h in (2, 3):
                            last = act.activation(
                                v1[32 * h:32 * h + 32, b * NSEG + 4 * n + s, :].rearrange("p (c d) -> p c d", c=KD),
                                v_tmp[32 * s:32 * s + 32, i % 2, :].rearrange("p (c h d) -> p c h d", c=KD, h=4)
                                [:, :, h, :], ACT.Copy)
                    last.then_inc(v_copied_act, 1)
            act.wait_ge(null_v_loaded, 16 * 4 * B)

        @block.vector
        def _(dve):
            dve.memset(v2_rest[:, :, :, :], 0.0).then_inc(zeroed, 1)
            dve.memset(k2[:, :, :, :, :], 0.0).then_inc(zeroed, 1)
            dve.memset(empty_row[:, :], 0.0).then_inc(empty_made, 1)
            dve.wait_ge(empty_made, 1)
            dve.memset(empty_row[:, D + 1:D + 2].bitcast(I32), NOBODY).then_inc(empty_made, 1)
            dve.wait_ge(maps_loaded, 16 * (2 * B + 1))
            for b in range(B):
                last = dve.tensor_scalar(kidx[:, b, :], kmap[:, :], M - 1, b * M, ALU.min, ALU.add)
            last.then_inc(tables, 1)
            for b in range(B):
                dve.tensor_scalar(idx_all[:, 16 * b:16 * b + 16], map_raw[:, 16 * b:16 * b + 16], M - 1, b * M,
                                  ALU.min, ALU.add)
            dve.tensor_scalar(seg_raw[:, :], seg_raw[:, :], 7, None, ALU.arith_shift_right).then_inc(tables, 1)
            dve.wait_ge(tables, 2)
            for b in range(B):
                dve.tensor_scalar(seg_tab[:, 32 * b:32 * b + 32], seg_raw[:, 32 * b:32 * b + 32], NSEG - 1, b * NSEG,
                                  ALU.min, ALU.add)
            for e in range(E):
                dve.memset(rev[:, e:e + 1], float(E - e))
            dve.wait_ge(masks, 10)
            dve.tensor_copy(token_f[:, :], token_int[:, :])
            dve.tensor_copy(head_ones[:, :].rearrange("p (h d) -> p h d", h=4),
                            head_mask[:, :].rearrange("p (h d) -> p h d", d=1).to_broadcast([P, 4, 32]))

            def split(u):
                dve.wait_ge(raw_high, u + 1)
                dve.tensor_tensor(units[u][3], raw[:, u % 2, :].rearrange("p (k n) -> p k n", k=units[u][1]),
                                  units[u][2].bitcast(F32), ALU.subtract)\
                    .then_inc(raw_low, 1)

            def turn(r):
                dve.wait_ge(turned_high, r + 1)
                if r < CR:
                    cols = (slice(None), slice(4 * (r % 2), 4 * (r % 2) + 4), slice((r // 2) * P, (r // 2 + 1) * P))
                    high, low = ct_h[cols], ct_l[cols]
                else:
                    cols = (slice(None), slice(None), slice(((r - CR) % 4) * P, ((r - CR) % 4 + 1) * P))
                    high, low = xkt_h[cols], xkt_l[cols]
                dve.tensor_tensor(low, bank[r % 2][:, :].rearrange("p (k t) -> p k t", k=4), high.bitcast(F32),
                                  ALU.subtract).then_inc(turned_low, 1)

            for r in range(CR):
                turn(r)
            for u in range(NU):
                split(u)
            dve.wait_ge(biases_loaded, 16 * 8)
            dve.wait_ge(rest_placed, 16 * 4 * B)
            for b in range(B):
                dve.wait_ge(xk_loaded, 64 * (b + 1))
                for n in range(4):
                    last = dve.bn_stats(stats[:, n, :], xk[:, n, :])
                last.then_inc(xk_stats, 1)
                dve.wait_ge(xk_stats, b + 1)
                for n in range(4):
                    last = dve.bn_aggr(mv[:, n, :], stats[:, n, :])
                last.then_inc(xk_aggr, 1)
                dve.wait_ge(xk_aggr, b + 1)
                dve.tensor_scalar(var_eps[:, :], mv[:, :, 1], EPS1, None, ALU.add).then_inc(xk_eps, 1)
                dve.wait_ge(xk_rstd, b + 1)
                for n in range(4):
                    dve.tensor_scalar(xk[:, n, :], xk[:, n, :], mv[:, n, 0:1], rstd[:, n:n + 1], ALU.subtract,
                                      ALU.mult).then_inc(xk_norm, 1)
                for n in range(4):
                    turn(CR + 4 * b + n)
                for n in range(4):
                    i = 4 * b + n
                    dve.wait_ge(v_done, i + 1)
                    need(dve, v_copied, i - 1)
                    need(dve, v_copied_act, i - 1)
                    dve.tensor_tensor(v_tmp[:, i % 2, :], bank[5 + i % 2][:, :], bv_b[:, :], ALU.add)\
                        .then_inc(v_biased, 1)
                    dve.wait_ge(v_biased, i + 1)
                    for s in range(4):
                        for h in (0, 1):
                            last = dve.tensor_copy(
                                v1[32 * h:32 * h + 32, b * NSEG + 4 * n + s, :].rearrange("p (c d) -> p c d", c=KD),
                                v_tmp[32 * s:32 * s + 32, i % 2, :].rearrange("p (c h d) -> p c h d", c=KD, h=4)
                                [:, :, h, :])
                    last.then_inc(v_copied, 1)

        @block.tensor
        def _(pe):
            pe.wait_ge(masks, 9)

            def turn(r, src):
                need(pe, turned_low, r - 1)
                for k in range(4):
                    last = pe.transpose(bank[r % 2][:, k * P:(k + 1) * P], src(k), ident[:, :])
                last.then_inc(turned, 1)

            pe.wait_ge(ctx_loaded, 64)
            for r in range(CR):
                turn(r, lambda k, r=r: ctx_sb[:, r // 2, (4 * (r % 2) + k) * P:(4 * (r % 2) + k + 1) * P])
            pe.wait_ge(turned_low, CR)
            m = 0
            for n in range(NC):
                pe.wait_ge(raw_low, n + 1)
                for c in range(HB if n < KB else 3):
                    need(pe, kv_evac, m - 2)
                    for k in range(KC):
                        if n < KB:
                            w = [a[:, n % 2, k, c * P:(c + 1) * P] for a in (wc_h, wc_l)]
                            last = product(pe, bank[2 + m % 3][:, 0:3 * P], w, [a[:, k, :] for a in (ct_h, ct_l)],
                                           k == 0, k == KC - 1)
                        else:
                            t = [a[:, k, c * P:(c + 1) * P] for a in (ct_h, ct_l)]
                            last = product(pe, bank[2 + m % 3][:, 0:CB], t,
                                           [a[:, n % 2, k, :] for a in (wc_h, wc_l)], k == 0, k == KC - 1)
                    last.then_inc(kv_done, 1)
                    m += 1
                pe.wait_ge(kv_done, m)
                pe.sem_inc(block_done, 1)
            pe.wait_ge(raw_low, NC + 2)
            for b in range(B):
                for n in range(4):
                    pe.wait_ge(xk_norm, 4 * b + n + 1)
                    turn(CR + 4 * b + n, lambda k, n=n: xk[:, n, k * P:(k + 1) * P])
                pe.wait_ge(turned_low, CR + 4 * b + 4)
                for c in range(KD):
                    need(pe, kv_evac, m - 2)
                    for k in range(KD):
                        w = [a[:, k, c * P:(c + 1) * P] for a in wkv_a[0]]
                        last = product(pe, bank[2 + m % 3][:, :], w, [a[:, k, :] for a in (xkt_h, xkt_l)], k == 0,
                                       k == KD - 1)
                    last.then_inc(kv_done, 1)
                    m += 1
                for n in range(4):
                    i = 4 * b + n
                    need(pe, v_biased, i - 1)
                    for k in range(KD):
                        t = [a[:, k, n * P:(n + 1) * P] for a in (xkt_h, xkt_l)]
                        last = product(pe, bank[5 + i % 2][:, :], t,
                                       [a[:, k, :] for a in wkv_a[1]], k == 0, k == KD - 1)
                    last.then_inc(v_done, 1)


def self_attention(nc, sem, sb, bank, x_rows, x_tiles, x1_tiles, ident, head_mask, minus_half, bproj_b, wq_h, wq_l,
                   wp_h, wp_l, bq_col, k1, v1, idx_all, head_ones, seg_tab):
    idx = sb("a_idx", [P, G], I32)
    xg = sb("a_xg", [P, G, D])
    xt_h = sb("a_xt_h", [P, KD, G * P], F32R)
    xt_l = sb("a_xt_l", [P, KD, G * P], F32R)
    qt = sb("a_qt", [P, KD, G * P])
    k_block = sb("a_k_block", [P, 4, KD, 4, NKEY])
    v_block = sb("a_v_block", [P, 4, KD, 4, D1])
    prob = sb("a_prob", [P, G, D])
    top = sb("a_top", [P, G, 2 * KD])
    recip = sb("a_recip", [P, D])
    mixed = sb("a_mixed", [P, D])
    at_h = sb("a_at_h", [P, 2, KD, P], F32R)
    at_l = sb("a_at_l", [P, 2, KD, P], F32R)
    xr = sb("a_xr", [P, G, D])
    stats = sb("a_stats", [P, G, 6])
    mv = sb("a_mv", [P, G, 2])
    var_eps = sb("a_var_eps", [P, G])
    rstd = sb("a_rstd", [P, G])

    names = ("slot_tables gathered0 gathered1 gathered2 gathered3 stats_done aggr_done eps_done rstd_done normed "
             "x_turned x_high x_low q_done q_evac k_ready v_ready s_done s_top s_shifted s_exp a_done sum_done "
             "sum_eps sum_recip a_norm a_high a_low proj_done x1_made res_biased").split()
    s = {n: sem("a_" + n) for n in names}
    xr_loaded = [sem(f"a_xr_loaded{t}") for t in range(G)]
    x1_stored = [sem(f"a_x1_stored{t}") for t in range(G)]
    x_bank, q_bank, s_bank, sum_bank, a_bank, o_bank = bank[0], bank[1:3], bank[3:5], bank[5], bank[6], bank[7]

    def run(eng, step):
        step(-1)
        step(0)
        with eng.Fori(1, NG - 2) as i:
            step(i)
        step(NG - 2)
        step(NG - 1)

    def tile0(i, t):
        return G * i + t

    def has(i, n=0):
        return not isinstance(i, int) or 0 <= i + n < NG

    block = nc.Block()
    with block as block:
        @block.sync
        def _(sp):
            def step(i):
                for t in range(G):
                    if has(i):
                        tile = G * i + t
                        need(sp, s["x1_made"], tile + 1)
                        sp.dma_start(x1_tiles[:, tile, :], xr[:, t, :]).then_inc(x1_stored[t], 16)
                    if has(i, 1):
                        need(sp, x1_stored[t], 16 * (i + 1))
                        sp.dma_start(xr[:, t, :], x_tiles[:, G * (i + 1) + t, :]).then_inc(xr_loaded[t], 16)
            run(sp, step)
            for t in range(G):
                sp.wait_ge(x1_stored[t], 16 * NG)

        @block.gpsimd
        def _(pool):
            def gather(i):
                hold(pool, s["x_turned"], G * i)
                hold(pool, s["slot_tables"], i + 1)
                for t in range(G):
                    pool.indirect_dma_start(out=xg[:, t, :], out_offset=None, in_=x_rows,
                                            in_offset=bass.IndirectOffsetOnAxis(ap=idx[:, t:t + 1], axis=0))\
                        .then_inc(s[f"gathered{t}"], 16)

            def power(i):
                hold(pool, s["eps_done"], i + 1)
                pool.tensor_tensor(rstd[:, :], var_eps[:, :], minus_half[:, :], ALU.pow).then_inc(s["rstd_done"], 1)

            def spread(dst, src):
                return pool.tensor_tensor(dst, src, head_mask[:, :].rearrange("p (a h d) -> p a h d", a=1, d=1)
                                          .to_broadcast([P, KD, 4, 32]), ALU.mult)

            def step(i):
                for t in range(G):
                    if has(i, 1):
                        hold(pool, s["s_done"], G * (i + 1) + t - 1)
                        for j in range(2):
                            n = 2 * (G * (i + 1) + t) + j
                            g = pool.value_load(seg_tab[0:1, bass.ds(n, 1)], min_val=0, max_val=B * NSEG - 1)
                            ins = spread(k_block[:, 2 * (t % 2) + j, :, :, :],
                                         k1[:, :, bass.ds(g, 1), :].to_broadcast([P, KD, 4, NKEY]))
                        ins.then_inc(s["k_ready"], 1)
                    if has(i):
                        hold(pool, s["a_done"], G * i + t - 1)
                        for j in range(2):
                            n = 2 * (G * i + t) + j
                            g = pool.value_load(seg_tab[0:1, bass.ds(n, 1)], min_val=0, max_val=B * NSEG - 1)
                            ins = spread(v_block[:, 2 * (t % 2) + j, :, :, :],
                                         v1[:, bass.ds(g, 1), :].rearrange("p a (c d) -> p c a d", c=KD)
                                         .to_broadcast([P, KD, 4, D1]))
                        ins.then_inc(s["v_ready"], 1)
                        hold(pool, xr_loaded[t], 16 * (i + 1))
                        pool.tensor_tensor(xr[:, t, :], xr[:, t, :], bproj_b[:, :], ALU.add)\
                            .then_inc(s["res_biased"], 1)
                    if t == 0 and has(i, 2):
                        gather(i + 2)
                if has(i, 2):
                    power(i + 2)

            gather(0)
            power(0)
            run(pool, step)

        @block.scalar
        def _(act):
            def step(i):
                if has(i, 1):
                    for t in range(G):
                        need(act, s["x_turned"], G * (i + 1) + t + 1)
                        act.activation(xt_h[:, :, t * P:(t + 1) * P],
                                       x_bank[:, :].rearrange("p (k t) -> p k t", k=KD), ACT.Copy)\
                            .then_inc(s["x_high"], 1)
                    for c in range(KD):
                        need(act, s["q_done"], KD * (i + 1) + c + 1)
                        act.activation(qt[:, c, :], q_bank[c % 2][:, :], ACT.Identity, bias=bq_col[:, c:c + 1])\
                            .then_inc(s["q_evac"], 1)
                for t in range(G):
                    if has(i):
                        tile = G * i + t
                        need(act, s["sum_done"], tile + 1)
                        need(act, s["a_norm"], tile)
                        act.activation(recip[:, :], sum_bank[:, :], ACT.Copy, bias=EPS_SUM).then_inc(s["sum_eps"], 1)
                    if has(i, 1):
                        tile = G * (i + 1) + t
                        need(act, s["s_shifted"], tile + 1)
                        act.activation(prob[:, t, :], prob[:, t, :], ACT.Exp, scale=SCALE1).then_inc(s["s_exp"], 1)
                    if has(i):
                        need(act, s["a_norm"], tile0(i, t) + 1)
                        need(act, s["proj_done"], tile0(i, t) - 1)
                        act.activation(at_h[:, t % 2, :, :], mixed[:, :].rearrange("p (c t) -> p c t", c=KD),
                                       ACT.Copy).then_inc(s["a_high"], 1)
            run(act, step)

        @block.vector
        def _(dve):
            def tables(i):
                need(dve, s["gathered3"], 16 * i)
                for t in range(G - 1):
                    need(dve, s[f"gathered{t}"], 16 * i)
                dve.tensor_scalar(idx[:, :], idx_all[:, bass.ds(G * i, G)], 0, None, ALU.add)\
                    .then_inc(s["slot_tables"], 1)

            def norm(i):
                for t in range(G):
                    need(dve, s[f"gathered{t}"], 16 * (i + 1))
                    last = dve.bn_stats(stats[:, t, :], xg[:, t, :])
                last.then_inc(s["stats_done"], 1)
                hold(dve, s["stats_done"], i + 1)
                for t in range(G):
                    last = dve.bn_aggr(mv[:, t, :], stats[:, t, :])
                last.then_inc(s["aggr_done"], 1)
                need(dve, s["aggr_done"], i + 1)
                dve.tensor_scalar(var_eps[:, :], mv[:, :, 1], EPS1, None, ALU.add).then_inc(s["eps_done"], 1)
                need(dve, s["rstd_done"], i + 1)
                for t in range(G):
                    dve.tensor_scalar(xg[:, t, :], xg[:, t, :], mv[:, t, 0:1], rstd[:, t:t + 1], ALU.subtract,
                                      ALU.mult).then_inc(s["normed"], 1)

            def residual(tile, t):
                need(dve, s["proj_done"], tile + 1)
                need(dve, s["res_biased"], tile + 1)
                dve.tensor_tensor(xr[:, t, :], o_bank[:, :], xr[:, t, :], ALU.add).then_inc(s["x1_made"], 1)

            def step(i):
                if has(i, 2):
                    tables(i + 2)
                if has(i, 1):
                    for t in range(G):
                        need(dve, s["x_high"], G * (i + 1) + t + 1)
                        dve.tensor_tensor(xt_l[:, :, t * P:(t + 1) * P],
                                          x_bank[:, :].rearrange("p (k t) -> p k t", k=KD),
                                          xt_h[:, :, t * P:(t + 1) * P].bitcast(F32), ALU.subtract)\
                            .then_inc(s["x_low"], 1)
                for t in range(G):
                    if has(i):
                        tile = G * i + t
                        need(dve, s["sum_eps"], tile + 1)
                        dve.reciprocal(recip[:, :], recip[:, :]).then_inc(s["sum_recip"], 1)
                        need(dve, s["sum_recip"], tile + 1)
                        need(dve, s["a_low"], tile)
                        dve.tensor_tensor(mixed[:, :], a_bank[:, :], recip[:, :], ALU.mult).then_inc(s["a_norm"], 1)
                    if has(i, 1):
                        tile = G * (i + 1) + t
                        s3 = s_bank[t % 2][:, :].rearrange("p (c q) -> p c q", q=BLK)
                        need(dve, s["s_done"], tile + 1)
                        dve.tensor_reduce(top[:, t, :], s3, AX.X, ALU.max).then_inc(s["s_top"], 1)
                        need(dve, s["s_top"], tile + 1)
                        need(dve, s["sum_done"], tile - G + 1)
                        dve.tensor_tensor(prob[:, t, :].rearrange("p (c q) -> p c q", q=BLK), s3,
                                          top[:, t, :].rearrange("p (c q) -> p c q", q=1)
                                          .to_broadcast([P, 2 * KD, BLK]), ALU.subtract).then_inc(s["s_shifted"], 1)
                    if has(i):
                        tile = G * i + t
                        need(dve, s["a_high"], tile + 1)
                        dve.tensor_tensor(at_l[:, t % 2, :, :], mixed[:, :].rearrange("p (c t) -> p c t", c=KD),
                                          at_h[:, t % 2, :, :].bitcast(F32), ALU.subtract).then_inc(s["a_low"], 1)
                    if has(i) and t:
                        residual(G * i + t - 1, t - 1)
                if has(i):
                    residual(G * i + G - 1, G - 1)
                if has(i, 2):
                    norm(i + 2)

            tables(0)
            norm(0)
            run(dve, step)

        @block.tensor
        def _(pe):
            def project(i, t):
                tile = G * i + t
                need(pe, s["a_low"], tile + 1)
                need(pe, s["x1_made"], tile)
                for c in range(KD):
                    last = product(pe, o_bank[:, :], [a[:, t % 2, c, :] for a in (at_h, at_l)],
                                   [a[:, c, :] for a in (wp_h, wp_l)], c == 0, c == KD - 1)
                last.then_inc(s["proj_done"], 1)

            def step(i):
                if has(i, 1):
                    for t in range(G):
                        tile = G * (i + 1) + t
                        need(pe, s["normed"], tile + 1)
                        need(pe, s["x_low"], tile)
                        for k in range(KD):
                            last = pe.transpose(x_bank[:, k * P:(k + 1) * P], xg[:, t, k * P:(k + 1) * P], ident[:, :])
                        last.then_inc(s["x_turned"], 1)
                    need(pe, s["x_low"], G * (i + 2))
                    for c in range(KD):
                        need(pe, s["q_evac"], KD * (i + 1) + c - 1)
                        for k in range(KD):
                            last = product(pe, q_bank[c % 2][:, :],
                                           [a[:, k, c * P:(c + 1) * P] for a in (wq_h, wq_l)],
                                           [a[:, k, :] for a in (xt_h, xt_l)], k == 0, k == KD - 1)
                        last.then_inc(s["q_done"], 1)
                for t in range(G):
                    if has(i):
                        tile = G * i + t
                        need(pe, s["s_exp"], tile + 1)
                        need(pe, s["v_ready"], tile + 1)
                        need(pe, s["a_norm"], tile)
                        for c in range(KD):
                            for j in range(2):
                                o = c * P + BLK * j
                                last = pe.matmul(a_bank[:, o:o + BLK], v_block[:, 2 * (t % 2) + j, c, :, :],
                                                 prob[:, t, o:o + BLK], start=True, stop=True)
                        last.then_inc(s["a_done"], 1)
                        pe.matmul(sum_bank[:, :], head_ones[:, :], prob[:, t, :], start=True, stop=True)\
                            .then_inc(s["sum_done"], 1)
                    if has(i, 1):
                        tile = G * (i + 1) + t
                        if t == 0:
                            need(pe, s["q_evac"], KD * (i + 2))
                        need(pe, s["k_ready"], tile + 1)
                        need(pe, s["s_shifted"], tile - 1)
                        for c in range(KD):
                            for j in range(2):
                                o = c * P + BLK * j
                                last = pe.matmul(s_bank[t % 2][:, o:o + BLK], k_block[:, 2 * (t % 2) + j, c, :, :],
                                                 qt[:, c, t * P + BLK * j:t * P + BLK * (j + 1)], start=True,
                                                 stop=True)
                        last.then_inc(s["s_done"], 1)
                    if has(i) and t:
                        project(i, t - 1)
                if has(i):
                    project(i, G - 1)
            run(pe, step)


def cross_attention(nc, sem, sb, bank, x1_tiles, out_tiles, slots_dram, wq2, wout, ident, upper, ones, minus_half, rev,
                    token_int, token_f, lns_b, lnb_b, br_b, wr_sb, k2, v2_main, v2_rest):
    wq_h, wq_l = sb("b_wq_h", [P, KD, INNER], F32R), sb("b_wq_l", [P, KD, INNER], F32R)
    wo_h, wo_l = sb("b_wo_h", [P, KI, D], F32R), sb("b_wo_l", [P, KI, D], F32R)
    xn = sb("b_xn", [P, G, D])
    xt_h, xt_l = sb("b_xt_h", [P, KD, G * P], F32R), sb("b_xt_l", [P, KD, G * P], F32R)
    qt = sb("b_qt", [P, KI, G * P])
    prob = sb("b_prob", [P, 2, 4, PW, 4])
    raw = prob[:, :, :, :, :].rearrange("p a g k h -> p (a g k h)")[:, 0:2 * 2048].rearrange("p (a n) -> p a n", a=2)
    pt = sb("b_pt", [P, 4 + H2, P])
    o_sb = sb("b_o", [P, INNER])
    ot_h, ot_l = sb("b_ot_h", [P, KI, P], F32R), sb("b_ot_l", [P, KI, P], F32R)
    xr = sb("b_xr", [P, D])
    x2 = sb("b_x2", [P, 2, D])
    y = sb("b_y", [P, D])
    yt = sb("b_yt", [P, KD, P])
    rows = sb("b_rows", [P, G, ROW])
    neg_top, total, recip = sb("b_neg_top", [P, 2, H2]), sb("b_total", [P, 2, H2]), sb("b_recip", [P, H2])
    kinds = ("x", "w", "y")
    stats = {k: sb(f"b_{k}_stats", [P, 6]) for k in kinds}
    mv = {k: sb(f"b_{k}_mv", [P, 2]) for k in kinds}
    var_eps = {k: sb(f"b_{k}_var", [P, 1]) for k in kinds}
    rstd = {k: sb(f"b_{k}_rstd", [P, 1]) for k in kinds}
    logit = sb("b_logit", [P, G, E])
    p_e, q_e = sb("b_p_e", [P, G, E]), sb("b_q_e", [P, G, E])
    onehot = sb("b_onehot", [P, G, E])
    before = sb("b_before", [P, G + 1, E])
    c4 = {k: sb(f"b_{k}", [P, G]) for k in ("top4", "sum4", "rec4", "gate4", "rank4", "pos4", "keep4", "slot4")}
    slot_idx = sb("b_slot_idx", [P, G], I32)

    names = ("raw_high raw_low padded x_loaded0 x_loaded1 x_loaded2 x_loaded3 x_normed x_turned x_high x_low q_done "
             "q_evac s_done s_max s_exp s_recip pt_turned pt_evac o_done o_evac ot_turned ot_high ot_low w_done "
             "w_normed xr_loaded xr_biased w_scaled x2_made y_normed y_turned y_evac l_done l_evac rows_loaded "
             "route_step route_exp onehot_made counted routed scattered").split()
    s = {n: sem("b_" + n) for n in names}
    raw_loaded = [sem("b_raw_loaded0"), sem("b_raw_loaded1")]
    x2_stored = [sem("b_x2_stored0"), sem("b_x2_stored1")]
    ln = {k: {n: sem(f"b_{k}_{n}") for n in ("stats", "aggr", "eps", "rstd")} for k in kinds}
    pt_bank, s_bank, q_bank, o_bank, w_bank, x_bank = bank[0:2], bank[2:4], bank[4], bank[5], bank[6], bank[7]
    PS = H2 // 2
    QUERIES = ((2, 1), (3, 0))
    RS1, RS2 = 10, 13

    units = [(wq2[:, n * 512:(n + 1) * 512], wq_h[:, :, n * 512:(n + 1) * 512], wq_l[:, :, n * 512:(n + 1) * 512])
             for n in range(2)]
    units += [(wout[n * 512:(n + 1) * 512, :], wo_h[:, 4 * n:4 * n + 4, :], wo_l[:, 4 * n:4 * n + 4, :])
              for n in range(2)]
    NU = len(units)

    def run(eng, step):
        for i in (-2, -1, 0, 1):
            step(i)
        with eng.Fori(2, NG - 2) as i:
            step(i)
        for i in (NG - 2, NG - 1, NG):
            step(i)

    def there(i):
        return not isinstance(i, int) or 0 <= i < NG

    def tiled(n):
        return not isinstance(n, int) or 0 <= n < NT

    def capped(v, most):
        return min(v, most) if isinstance(v, int) else v

    block = nc.Block()
    with block as block:
        @block.sync
        def _(sp):
            for u, (src, _, _) in enumerate(units):
                need(sp, s["raw_low"], u - 1)
                sp.dma_start(raw[:, u % 2, :].rearrange("p (k n) -> p k n", k=4),
                             src.rearrange("(k p) n -> p k n", p=P)).then_inc(raw_loaded[u % 2], 16)

            def step(i):
                for t in range(G):
                    n = G * i + t
                    if there(i + 2):
                        need(sp, s["x_turned"], G * (i + 1) + t + 1)
                        sp.dma_start(xn[:, t, :], x1_tiles[:, G * (i + 2) + t, :]).then_inc(s[f"x_loaded{t}"], 16)
                    if tiled(n - 2):
                        need(sp, s["x2_made"], n - 1)
                        sp.dma_start(out_tiles[:, n - 2, :], x2[:, t % 2, :]).then_inc(x2_stored[t % 2], 16)
                    if t == 2 and there(i - 1):
                        need(sp, x2_stored[0], 32 * i)
                        need(sp, x2_stored[1], 32 * i)
                        need(sp, s["scattered"], 64 * (i - 1))
                        sp.dma_start(rows[:, :, 0:D], out_tiles[:, bass.ds(G * (i - 1), G), :])\
                            .then_inc(s["rows_loaded"], 16)
                    if tiled(n):
                        need(sp, s["x2_made"], n)
                        sp.dma_start(xr[:, :], x1_tiles[:, n, :]).then_inc(s["xr_loaded"], 16)
            run(sp, step)
            for par in range(2):
                sp.wait_ge(x2_stored[par], 16 * NT // 2)

        @block.gpsimd
        def _(pool):
            def power(kind, count):
                hold(pool, ln[kind]["eps"], count)
                pool.tensor_tensor(rstd[kind][:, :], var_eps[kind][:, :], minus_half[:, 0:1], ALU.pow)\
                    .then_inc(ln[kind]["rstd"], 1)

            def step(i):
                for t in range(G):
                    n = G * i + t
                    if there(i + 2):
                        power("x", G * (i + 2) + t + 1)
                    if tiled(n - 1):
                        hold(pool, s["xr_loaded"], 16 * n)
                        pool.tensor_tensor(xr[:, :], xr[:, :], lnb_b[:, :], ALU.add).then_inc(s["xr_biased"], 1)
                    if tiled(n - 2):
                        power("y", n - 1)
                    if t == 3 and there(i - 1):
                        hold(pool, s["routed"], i)
                        for k in range(G):
                            pool.indirect_dma_start(out=slots_dram, out_offset=bass.IndirectOffsetOnAxis(
                                ap=slot_idx[:, k:k + 1], axis=0), in_=rows[:, k, :], in_offset=None)\
                                .then_inc(s["scattered"], 16)
                    if tiled(n - 1):
                        power("w", n)
                        x2t = x2[:, (t + 1) % 2, :]
                        hold(pool, s["w_normed"], n)
                        pool.tensor_tensor(x2t, x2t, lns_b[:, :], ALU.mult).then_inc(s["w_scaled"], 1)
                        hold(pool, s["w_scaled"], n)
                        hold(pool, s["xr_biased"], n)
                        pool.tensor_tensor(x2t, x2t, xr[:, :], ALU.add).then_inc(s["x2_made"], 1)
            run(pool, step)
            pool.wait_ge(s["scattered"], 64 * NG)

        @block.scalar
        def _(act):
            for u in range(NU):
                act.wait_ge(raw_loaded[u % 2], 16 * (u // 2 + 1))
                act.activation(units[u][1], raw[:, u % 2, :].rearrange("p (k n) -> p k n", k=4), ACT.Copy)\
                    .then_inc(s["raw_high"], 1)
            act.wait_ge(s["padded"], 1)

            def expo(n, t, j):
                need(act, s["s_max"], PS * n + j + 1)
                for h in range(2):
                    last = act.activation(prob[:, t % 2, j // 2, 0:L2, 2 * (j % 2) + h], s_bank[j % 2][:, h * L2:(h + 1) * L2],
                                          ACT.Exp, bias=neg_top[:, t % 2, 2 * j + h:2 * j + h + 1],
                                          accum_out=total[:, t % 2, 2 * j + h:2 * j + h + 1])
                last.then_inc(s["s_exp"], 1)

            def q_copy(i, c):
                need(act, s["q_done"], KI * i + c + 1)
                act.activation(qt[:, c, :], q_bank[:, :], ACT.Copy).then_inc(s["q_evac"], 1)

            def ot_copy(n, u):
                need(act, s["ot_turned"], 2 * n + u + 1)
                act.activation(ot_h[:, 4 * u:4 * u + 4, :], x_bank[:, :].rearrange("p (c t) -> p c t", c=4), ACT.Copy)\
                    .then_inc(s["ot_high"], 1)

            def step(i):
                for t in range(G):
                    n = G * i + t
                    for j in range(PS):
                        if tiled(n + 1):
                            expo(n + 1, t + 1, j)
                        if (t, j % 2) in QUERIES and there(i + 1):
                            q_copy(i + 1, 4 * (t - 2) + j // 2)
                        if j == PS - 2:
                            if tiled(n):
                                ot_copy(n, 0)
                            if t == 3 and there(i + 2):
                                for k in range(G):
                                    need(act, s["x_turned"], G * (i + 2) + k + 1)
                                    act.activation(xt_h[:, :, k * P:(k + 1) * P],
                                                   x_bank[:, :].rearrange("p (k t) -> p k t", k=KD), ACT.Copy)\
                                        .then_inc(s["x_high"], 1)
                    if tiled(n):
                        ot_copy(n, 1)
                    if t == 1 and there(i - 1):
                        need(act, s["route_step"], (RS1 + RS2) * (i - 1) + 2)
                        act.activation(p_e[:, :, :], q_e[:, :, :], ACT.Exp).then_inc(s["route_exp"], 1)
            run(act, step)

        @block.vector
        def _(dve):
            for u in range(NU):
                dve.wait_ge(s["raw_high"], u + 1)
                dve.tensor_tensor(units[u][2], raw[:, u % 2, :].rearrange("p (k n) -> p k n", k=4),
                                  units[u][1].bitcast(F32), ALU.subtract).then_inc(s["raw_low"], 1)
            dve.wait_ge(s["raw_low"], NU)
            dve.memset(before[:, :, :], 0.0)
            dve.memset(prob[:, :, :, L2:PW, :], 0.0).then_inc(s["padded"], 1)

            def norm_stats(kind, count, src, eps):
                dve.bn_stats(stats[kind][:, :], src).then_inc(ln[kind]["stats"], 1)
                hold(dve, ln[kind]["stats"], count)
                dve.bn_aggr(mv[kind][:, :], stats[kind][:, :]).then_inc(ln[kind]["aggr"], 1)
                need(dve, ln[kind]["aggr"], count)
                dve.tensor_scalar(var_eps[kind][:, :], mv[kind][:, 1:2], eps, None, ALU.add)\
                    .then_inc(ln[kind]["eps"], 1)

            def norm(kind, count, dst, src):
                need(dve, ln[kind]["rstd"], count)
                return dve.tensor_scalar(dst, src, mv[kind][:, 0:1], rstd[kind][:, :], ALU.subtract, ALU.mult)

            def pt_copy(n, t, u):
                need(dve, s["pt_turned"], 5 * n + u + 1)
                dve.tensor_copy(pt[:, 4 * u:4 * u + 4, :],
                                pt_bank[(5 * t + u) % 2][:, :].rearrange("p (c t) -> p c t", c=4))\
                    .then_inc(s["pt_evac"], 1)

            def o_copy(n, u):
                need(dve, s["o_done"], 2 * n + u + 1)
                need(dve, s["s_recip"], n + 1)
                dve.tensor_tensor(o_sb[:, 512 * u:512 * u + 512].rearrange("p (h d) -> p h d", h=8),
                                  o_bank[:, :].rearrange("p (h d) -> p h d", h=8),
                                  recip[:, 8 * u:8 * u + 8].rearrange("p (h d) -> p h d", d=1)
                                  .to_broadcast([P, 8, D2]), ALU.mult).then_inc(s["o_evac"], 1)

            def ot_copy(n, u):
                need(dve, s["ot_high"], 2 * n + u + 1)
                dve.tensor_tensor(ot_l[:, 4 * u:4 * u + 4, :], x_bank[:, :].rearrange("p (c t) -> p c t", c=4),
                                  ot_h[:, 4 * u:4 * u + 4, :].bitcast(F32), ALU.subtract).then_inc(s["ot_low"], 1)

            def router(i, first, steps):
                for k, op in enumerate(steps):
                    if first + k:
                        need(dve, s["route_step"], (RS1 + RS2) * i + first + k)
                    op().then_inc(s["route_step"], 1)

            def b8(a):
                return a.rearrange("p (t e) -> p t e", e=1).to_broadcast([P, G, E])

            def route_experts(i):
                revb = rev[:, :].rearrange("p (t e) -> p t e", t=1).to_broadcast([P, G, E])
                need(dve, s["l_evac"], G * (i + 1))
                router(i, 0, [
                    lambda: dve.tensor_reduce(c4["top4"][:, :], logit[:, :, :], AX.X, ALU.max),
                    lambda: dve.tensor_tensor(q_e[:, :, :], logit[:, :, :], b8(c4["top4"][:, :]), ALU.subtract),
                ])
                need(dve, s["route_exp"], i + 1)
                router(i, 2, [
                    lambda: dve.tensor_reduce(c4["sum4"][:, :], p_e[:, :, :], AX.X, ALU.add),
                    lambda: dve.reciprocal(c4["rec4"][:, :], c4["sum4"][:, :]),
                    lambda: dve.tensor_tensor(p_e[:, :, :], p_e[:, :, :], b8(c4["rec4"][:, :]), ALU.mult),
                    lambda: dve.tensor_reduce(c4["gate4"][:, :], p_e[:, :, :], AX.X, ALU.max),
                    lambda: dve.tensor_tensor(q_e[:, :, :], p_e[:, :, :], b8(c4["gate4"][:, :]), ALU.is_ge),
                    lambda: dve.tensor_tensor(q_e[:, :, :], q_e[:, :, :], revb, ALU.mult),
                    lambda: dve.tensor_reduce(c4["rank4"][:, :], q_e[:, :, :], AX.X, ALU.max),
                    lambda: dve.tensor_tensor(onehot[:, :, :], revb, b8(c4["rank4"][:, :]), ALU.is_equal),
                ])

            def route_slots(i):
                need(dve, s["counted"], i + 1)
                need(dve, s["scattered"], 64 * i)
                cum = q_bank[:, 64:64 + G * E].rearrange("p (t e) -> p t e", t=G)
                tot = q_bank[:, 128:128 + G * E].rearrange("p (t e) -> p t e", t=G)
                pos, keep, slot = c4["pos4"][:, :], c4["keep4"][:, :], c4["slot4"][:, :]
                spare = token_f[:, bass.ds(G * i, G)]
                steps = [lambda k=k: dve.tensor_tensor(before[:, k + 1, :], before[:, k, :], tot[:, k, :], ALU.add)
                         for k in range(G)]
                steps += [
                    lambda: dve.tensor_tensor(q_e[:, :, :], cum, before[:, 0:G, :], ALU.add),
                    lambda: dve.tensor_tensor(q_e[:, :, :], q_e[:, :, :], onehot[:, :, :], ALU.mult),
                    lambda: dve.tensor_reduce(pos, q_e[:, :, :], AX.X, ALU.add),
                    lambda: dve.tensor_scalar(keep, pos, float(CAP), None, ALU.is_lt),
                    lambda: dve.tensor_scalar(slot, c4["rank4"][:, :], -float(CAP), float(CAP * E - T), ALU.mult,
                                              ALU.add),
                    lambda: dve.tensor_tensor(slot, slot, pos, ALU.add),
                    lambda: dve.tensor_tensor(slot, slot, spare, ALU.subtract),
                    lambda: dve.tensor_tensor(slot, slot, keep, ALU.mult),
                    lambda: dve.tensor_copy(before[:, 0, :], before[:, G, :]),
                ]
                assert len(steps) == RS2
                router(i, RS1, steps)
                need(dve, s["route_step"], (RS1 + RS2) * (i + 1))
                dve.scalar_tensor_tensor(slot_idx[:, :], slot, float(T), spare, ALU.add, ALU.add)
                need(dve, s["rows_loaded"], 16 * (i + 1))
                dve.tensor_copy(rows[:, :, D:D + 1], c4["gate4"][:, :].rearrange("p (t a) -> p t a", a=1))
                dve.tensor_scalar(rows[:, :, D + 1:D + 2].bitcast(I32),
                                  token_int[:, bass.ds(G * i, G)].rearrange("p (t a) -> p t a", a=1), 0, None,
                                  ALU.add).then_inc(s["routed"], 1)

            def step(i):
                for t in range(G):
                    n = G * i + t

                    def top(j):
                        if tiled(n + 1):
                            need(dve, s["s_done"], PS * (n + 1) + j + 1)
                            dve.tensor_reduce(neg_top[:, (t + 1) % 2, 2 * j:2 * j + 2],
                                              s_bank[j % 2][:, 0:2 * L2].rearrange("p (h k) -> p h k", h=2), AX.X,
                                              ALU.max, negate=True).then_inc(s["s_max"], 1)

                    if tiled(n):
                        need(dve, s["s_exp"], PS * (n + 1))
                        need(dve, s["o_evac"], 2 * n)
                        dve.reciprocal(recip[:, :], total[:, t % 2, :]).then_inc(s["s_recip"], 1)
                        pt_copy(n, t, 0)
                        pt_copy(n, t, 1)
                    top(0)
                    if tiled(n):
                        pt_copy(n, t, 2)
                    top(1)
                    if there(i + 2):
                        need(dve, s[f"x_loaded{t}"], 16 * (i + 3))
                        norm_stats("x", G * (i + 2) + t + 1, xn[:, t, :], EPS1)
                    if tiled(n):
                        pt_copy(n, t, 3)
                    top(2)
                    if tiled(n):
                        o_copy(n, 0)
                    if tiled(n - 2):
                        need(dve, s["x2_made"], n - 1)
                        norm_stats("y", n - 1, x2[:, t % 2, :], EPS1)
                    if tiled(n):
                        pt_copy(n, t, 4)
                    top(3)
                    if there(i + 2):
                        norm("x", G * (i + 2) + t + 1, xn[:, t, :], xn[:, t, :]).then_inc(s["x_normed"], 1)
                    top(4)
                    if tiled(n):
                        o_copy(n, 1)
                    if tiled(n - 2):
                        need(dve, s["y_turned"], n - 2)
                        norm("y", n - 1, y[:, :], x2[:, t % 2, :]).then_inc(s["y_normed"], 1)
                    top(5)
                    if tiled(n - 2):
                        need(dve, s["y_turned"], n - 1)
                        need(dve, s["l_done"], n - 2)
                        dve.tensor_copy(yt[:, :, :], x_bank[:, :].rearrange("p (c t) -> p c t", c=KD))\
                            .then_inc(s["y_evac"], 1)
                    if tiled(n - 1):
                        need(dve, s["w_done"], n)
                        norm_stats("w", n, w_bank[:, :], EPS2)
                    top(6)
                    if tiled(n - 1):
                        need(dve, x2_stored[(t + 1) % 2], 16 * (2 * i + (t - 3) // 2 + 1))
                        norm("w", n, x2[:, (t + 1) % 2, :], w_bank[:, :]).then_inc(s["w_normed"], 1)
                    if tiled(n):
                        ot_copy(n, 0)
                    if t == 3 and there(i + 2):
                        for k in range(G):
                            need(dve, s["x_high"], G * (i + 2) + k + 1)
                            dve.tensor_tensor(xt_l[:, :, k * P:(k + 1) * P],
                                              x_bank[:, :].rearrange("p (k t) -> p k t", k=KD),
                                              xt_h[:, :, k * P:(k + 1) * P].bitcast(F32), ALU.subtract)\
                                .then_inc(s["x_low"], 1)
                    top(7)
                    if tiled(n):
                        ot_copy(n, 1)
                    if tiled(n - 2):
                        need(dve, s["l_done"], n - 1)
                        dve.tensor_tensor(logit[:, (t + 2) % 4, :], q_bank[:, 0:E], br_b[:, :], ALU.add)\
                            .then_inc(s["l_evac"], 1)
                    if t == 1 and there(i - 1):
                        route_experts(i - 1)
                    if t == 2 and there(i - 1):
                        route_slots(i - 1)
            run(dve, step)

        @block.tensor
        def _(pe):
            pe.wait_ge(s["raw_low"], NU)

            def turn_p(n, t, u):
                if u < 2:
                    need(pe, s["s_exp"], PS * (n + 1))
                need(pe, s["pt_evac"], 5 * n + u - 1)
                for k in range(4):
                    src = prob[:, t % 2, k, P:PW, :].rearrange("p k h -> p (k h)") if u == 0 else \
                        prob[:, t % 2, u - 1, 0:P, k]
                    last = pe.transpose(pt_bank[(5 * t + u) % 2][:, k * P:(k + 1) * P], src, ident[:, :])
                last.then_inc(s["pt_turned"], 1)

            def scores(n, t, b, j):
                need(pe, s["s_exp"], PS * n + j - 1)
                if t % G == 0:
                    need(pe, s["q_evac"], 2 * n + j + 1)
                pe.matmul(s_bank[j % 2][:, 0:2 * L2], qt[:, j, (t % G) * P:(t % G + 1) * P],
                          k2[:, bass.ds(b, 1), j, :, :].rearrange("p a h k -> p (a h k)"), start=True, stop=True)\
                    .then_inc(s["s_done"], 1)

            def values(n, b, g):
                need(pe, s["pt_evac"], 5 * n + g + 2)
                if g % 2 == 0:
                    need(pe, s["o_evac"], 2 * n + g // 2)
                o = (g % 2) * 256
                pe.matmul(o_bank[:, o:o + 256], pt[:, g, :], v2_rest[:, bass.ds(b, 1), g, :]
                          .rearrange("p a n -> p (a n)"), start=True, stop=False)
                for h in range(4):
                    last = pe.matmul(o_bank[:, o + h * D2:o + (h + 1) * D2], pt[:, 4 + 4 * g + h, :],
                                     v2_main[:, bass.ds(b, 1), (4 * g + h) * D2:(4 * g + h + 1) * D2]
                                     .rearrange("p a n -> p (a n)"), start=False, stop=h == 3)
                if g % 2:
                    last.then_inc(s["o_done"], 1)

            def queries(i, c):
                need(pe, s["x_low"], G * (i + 1))
                need(pe, s["q_evac"], KI * i + c)
                need(pe, s["l_evac"], capped(G * (i - 1) + (0 if c < 4 else 1), NT))
                if c >= 4:
                    need(pe, s["route_step"], (RS1 + RS2) * (i - 1))
                for k in range(KD):
                    last = product(pe, q_bank[:, :], [a[:, k, c * P:(c + 1) * P] for a in (wq_h, wq_l)],
                                   [a[:, k, :] for a in (xt_h, xt_l)], k == 0, k == KD - 1)
                last.then_inc(s["q_done"], 1)

            def output(n, half):
                if half == 0:
                    need(pe, s["ot_low"], 2 * (n + 1))
                    need(pe, s["w_normed"], n)
                for c in range(4 * half, 4 * half + 4):
                    last = product(pe, w_bank[:, :], [a[:, c, :] for a in (ot_h, ot_l)],
                                   [a[:, c, :] for a in (wo_h, wo_l)], c == 0, c == KI - 1)
                if half:
                    last.then_inc(s["w_done"], 1)

            def turn_o(n, u):
                need(pe, s["o_evac"], 2 * n + u + 1)
                for k in range(4):
                    last = pe.transpose(x_bank[:, k * P:(k + 1) * P], o_sb[:, (4 * u + k) * P:(4 * u + k + 1) * P],
                                        ident[:, :])
                last.then_inc(s["ot_turned"], 1)

            def batch(i):
                if isinstance(i, int):
                    return i // G
                return nc.s_assert_within(i >> 2, 0, B - 1, skip_runtime_bounds_check_because="groups end at NG - 1")

            def step(i):
                for t in range(G):
                    n = G * i + t
                    b = batch(i)
                    bn = b if t < 3 else batch(i + 1)

                    def sc(j):
                        if tiled(n + 1):
                            scores(n + 1, t + 1, bn, j)
                        if (t, j % 2) in QUERIES and there(i + 1):
                            queries(i + 1, 4 * (t - 2) + j // 2)

                    if tiled(n):
                        turn_p(n, t, 0)
                        turn_p(n, t, 1)
                    sc(0)
                    if tiled(n):
                        turn_p(n, t, 2)
                    sc(1)
                    if tiled(n):
                        values(n, b, 0)
                        turn_p(n, t, 3)
                    sc(2)
                    if tiled(n):
                        values(n, b, 1)
                        turn_p(n, t, 4)
                    sc(3)
                    if tiled(n):
                        values(n, b, 2)
                    sc(4)
                    if tiled(n):
                        values(n, b, 3)
                    if tiled(n - 1):
                        output(n - 1, 0)
                    sc(5)
                    if tiled(n - 2):
                        need(pe, s["y_normed"], n - 1)
                        need(pe, s["ot_low"], capped(2 * n, 2 * NT))
                        need(pe, s["y_evac"], n - 2)
                        for k in range(KD):
                            last = pe.transpose(x_bank[:, k * P:(k + 1) * P], y[:, k * P:(k + 1) * P], ident[:, :])
                        last.then_inc(s["y_turned"], 1)
                    if tiled(n - 1):
                        output(n - 1, 1)
                    sc(6)
                    if tiled(n):
                        need(pe, s["y_evac"], n - 1)
                        if t == 0:
                            need(pe, s["x_low"], capped(G * (i + 2), NT))
                        turn_o(n, 0)
                    if t == 3 and there(i + 2):
                        need(pe, s["ot_low"], capped(2 * n + 1, 2 * NT))
                        for k in range(G):
                            need(pe, s["x_normed"], G * (i + 2) + k + 1)
                            need(pe, s["x_low"], G * (i + 2) + k)
                            for c in range(KD):
                                last = pe.transpose(x_bank[:, c * P:(c + 1) * P], xn[:, k, c * P:(c + 1) * P],
                                                    ident[:, :])
                            last.then_inc(s["x_turned"], 1)
                    sc(7)
                    if tiled(n):
                        need(pe, s["ot_low"], 2 * n + 1)
                        if t == 3:
                            need(pe, s["x_low"], capped(G * (i + 3), NT))
                        turn_o(n, 1)
                    if tiled(n - 2):
                        need(pe, s["y_evac"], n - 1)
                        need(pe, s["l_evac"], n - 2)
                        if t == 3:
                            need(pe, s["route_step"], (RS1 + RS2) * i)
                        need(pe, s["q_evac"], capped(KI * (i + 1) if t < 2 else KI * (i + 1) + 4 * (t - 1), KI * NG))
                        for k in range(KD):
                            last = pe.matmul(q_bank[:, 0:E], yt[:, k, :], wr_sb[:, k, :], start=k == 0,
                                             stop=k == KD - 1)
                        last.then_inc(s["l_done"], 1)
                    if t == 2 and there(i - 1):
                        need(pe, s["route_step"], (RS1 + RS2) * (i - 1) + RS1)
                        need(pe, s["l_evac"], capped(G * (i - 1) + 5, NT))
                        oh = onehot[:, :, :].rearrange("p t e -> p (t e)")
                        pe.matmul(q_bank[:, 64:64 + G * E], upper[:, :], oh, start=True, stop=True)
                        pe.matmul(q_bank[:, 128:128 + G * E], ones[:, :], oh, start=True, stop=True)\
                            .then_inc(s["counted"], 1)
            run(pe, step)


def experts(nc, sem, sb, bank, slot_tiles, out_rows, w1, b1, w2, b2, ident, minus_half):
    raw = sb("c_raw", [P, 2, 2048])
    w_h = sb("c_w_h", [P, 2, 2, KD, D], F32R)
    w_l = sb("c_w_l", [P, 2, 2, KD, D], F32R)
    b1_col = sb("c_b1", [P, 2, KD])
    b2_b = sb("c_b2", [P, 2, D])
    rows = sb("c_rows", [P, 2, G, ROW])
    y = sb("c_y", [P, G, D])
    base = sb("c_base", [P, G, D])
    xt_h, xt_l = sb("c_xt_h", [P, KD, G * P], F32R), sb("c_xt_l", [P, KD, G * P], F32R)
    h = sb("c_h", [P, 2, G * P])
    ht_h, ht_l = sb("c_ht_h", [P, KD, G * P], F32R), sb("c_ht_l", [P, KD, G * P], F32R)
    res = sb("c_res", [P, G, D])
    stats, mv = sb("c_stats", [P, G, 6]), sb("c_mv", [P, G, 2])
    var_eps, rstd, gain = sb("c_var", [P, G]), sb("c_rstd", [P, G]), sb("c_gain", [P, G])

    names = ("w_loaded0 w_loaded1 w_high w_low b_loaded0 b_loaded1 rows_loaded0 rows_loaded1 stats_done aggr_done "
             "eps_done rstd_done gain_done normed scaled based x_turned x_high x_low h_done h_relu h_high h_low "
             "o_done res_made scattered0 scattered1 scattered2 scattered3").split()
    s = {n: sem("c_" + n) for n in names}
    h_bank, x_bank, o_bank = bank[0:2], bank[2:4], bank[4:6]

    def run(eng, ahead, work):
        def pair(p, last):
            for k in range(2):
                work(2 * p + k, k)
                if not (last and k):
                    ahead(2 * p + k + 1, 1 - k)
        ahead(0, 0)
        pair(0, False)
        with eng.Fori(1, E // 2 - 1) as p:
            pair(p, False)
        pair(E // 2 - 1, True)

    def times(e, par):
        return (e - par) // 2 if isinstance(e, int) else (e - par) >> 1

    block = nc.Block()
    with block as block:
        @block.sync
        def _(sp):
            def load(e, par):
                for k in range(G):
                    need(sp, s[f"scattered{k}"], 16 * (e - 1))
                sp.dma_start(rows[:, par, :, :], slot_tiles[:, bass.ds(G * e, G), :])\
                    .then_inc(s[f"rows_loaded{par}"], 16)
                for m, w in enumerate((w1, w2)):
                    need(sp, s["w_low"], 2 * e + m - 1)
                    sp.dma_start(raw[:, m, :].rearrange("p (k n) -> p k n", k=KD),
                                 w[bass.ds(e, 1), :, :].rearrange("a (k p) n -> p (a k) n", p=P))\
                        .then_inc(s[f"w_loaded{m}"], 16)
                need(sp, s["h_relu"], KD * (e - 1))
                need(sp, s["scaled"], G * (e - 1))
                with nc.allow_non_contiguous_dma(reason="a bias by column"):
                    sp.dma_start(b1_col[:, par, :], b1[bass.ds(e, 1), :].rearrange("a (c p) -> p (a c)", p=P))\
                        .then_inc(s[f"b_loaded{par}"], 16)
                sp.dma_start(b2_b[:, par, :], b2[bass.ds(e, 1), :].to_broadcast([P, D]))\
                    .then_inc(s[f"b_loaded{par}"], 16)
            run(sp, load, lambda e, par: None)

        @block.gpsimd
        def _(pool):
            def ahead(e, par):
                hold(pool, s["eps_done"], e + 1)
                pool.tensor_tensor(rstd[:, :], var_eps[:, :], minus_half[:, :], ALU.pow).then_inc(s["rstd_done"], 1)

            def work(e, par):
                hold(pool, s[f"b_loaded{par}"], 32 * (times(e, par) + 1))
                hold(pool, s["res_made"], G * e)
                for k in range(G):
                    pool.tensor_scalar(base[:, k, :], b2_b[:, par, :], rows[:, par, k, D:D + 1], None, ALU.mult)\
                        .then_inc(s["scaled"], 1)
                for k in range(G):
                    hold(pool, s["scaled"], G * e + k + 1)
                    pool.tensor_tensor(base[:, k, :], base[:, k, :], rows[:, par, k, 0:D], ALU.add)\
                        .then_inc(s["based"], 1)

            def send(e, par):
                for k in range(G):
                    hold(pool, s["res_made"], G * e + k + 1)
                    pool.indirect_dma_start(
                        out=out_rows,
                        out_offset=bass.IndirectOffsetOnAxis(ap=rows[:, par, k, D + 1:D + 2].bitcast(I32), axis=0),
                        in_=res[:, k, :], in_offset=None, bounds_check=T - 1, oob_is_err=False)\
                        .then_inc(s[f"scattered{k}"], 16)

            def ahead_then_send(e, par):
                ahead(e, par)
                if not isinstance(e, int) or e > 0:
                    send(e - 1, 1 - par)
            run(pool, ahead_then_send, work)
            send(E - 1, 1)
            for k in range(G):
                pool.wait_ge(s[f"scattered{k}"], 16 * E)

        @block.scalar
        def _(act):
            def ahead(e, par):
                for m in range(2):
                    need(act, s[f"w_loaded{m}"], 16 * (e + 1))
                    act.activation(w_h[:, par, m, :, :], raw[:, m, :].rearrange("p (k n) -> p k n", k=KD), ACT.Copy)\
                        .then_inc(s["w_high"], 1)
                for k in range(G):
                    need(act, s["x_turned"], G * e + k + 1)
                    act.activation(xt_h[:, :, k * P:(k + 1) * P],
                                   x_bank[k % 2][:, :].rearrange("p (k t) -> p k t", k=KD), ACT.Copy)\
                        .then_inc(s["x_high"], 1)

            def work(e, par):
                hold(act, s[f"b_loaded{par}"], 32 * (times(e, par) + 1))
                for c in range(KD):
                    need(act, s["h_done"], KD * e + c + 1)
                    need(act, s["h_low"], KD * e + c - 1)
                    act.activation(h[:, c % 2, :], h_bank[c % 2][:, :], ACT.Relu, bias=b1_col[:, par, c:c + 1])\
                        .then_inc(s["h_relu"], 1)
                    need(act, s["h_relu"], KD * e + c + 1)
                    act.activation(ht_h[:, c, :], h[:, c % 2, :], ACT.Copy).then_inc(s["h_high"], 1)
            run(act, ahead, work)

        @block.vector
        def _(dve):
            def ahead(e, par):
                need(dve, s[f"rows_loaded{par}"], 16 * (times(e, par) + 1))
                for k in range(G):
                    last = dve.bn_stats(stats[:, k, :], rows[:, par, k, 0:D])
                last.then_inc(s["stats_done"], 1)
                hold(dve, s["stats_done"], e + 1)
                for k in range(G):
                    last = dve.bn_aggr(mv[:, k, :], stats[:, k, :])
                last.then_inc(s["aggr_done"], 1)
                need(dve, s["aggr_done"], e + 1)
                dve.tensor_scalar(var_eps[:, :], mv[:, :, 1], EPS1, None, ALU.add).then_inc(s["eps_done"], 1)
                for m in range(2):
                    need(dve, s["w_high"], 2 * e + m + 1)
                    dve.tensor_tensor(w_l[:, par, m, :, :], raw[:, m, :].rearrange("p (k n) -> p k n", k=KD),
                                      w_h[:, par, m, :, :].bitcast(F32), ALU.subtract).then_inc(s["w_low"], 1)
                    if m == 0:
                        need(dve, s["rstd_done"], e + 1)
                        dve.tensor_tensor(gain[:, :], rstd[:, :], rows[:, par, :, D], ALU.mult)\
                            .then_inc(s["gain_done"], 1)
                        need(dve, s["gain_done"], e + 1)
                        need(dve, s["x_turned"], G * e)
                        for k in range(G):
                            dve.tensor_scalar(y[:, k, :], rows[:, par, k, 0:D], mv[:, k, 0:1], gain[:, k:k + 1],
                                              ALU.subtract, ALU.mult).then_inc(s["normed"], 1)
                for k in range(G):
                    need(dve, s["x_high"], G * e + k + 1)
                    dve.tensor_tensor(xt_l[:, :, k * P:(k + 1) * P],
                                      x_bank[k % 2][:, :].rearrange("p (k t) -> p k t", k=KD),
                                      xt_h[:, :, k * P:(k + 1) * P].bitcast(F32), ALU.subtract)\
                        .then_inc(s["x_low"], 1)
                if not isinstance(e, int) or e > 0:
                    finish(e - 1, 1 - par)

            def work(e, par):
                for c in range(KD):
                    need(dve, s["h_high"], KD * e + c + 1)
                    dve.tensor_tensor(ht_l[:, c, :], h[:, c % 2, :], ht_h[:, c, :].bitcast(F32), ALU.subtract)\
                        .then_inc(s["h_low"], 1)

            def finish(e, par):
                for k in range(G):
                    need(dve, s["o_done"], G * e + k + 1)
                    need(dve, s["based"], G * e + k + 1)
                    need(dve, s[f"scattered{k}"], 16 * e)
                    dve.scalar_tensor_tensor(res[:, k, :], o_bank[k % 2][:, :], rows[:, par, k, D:D + 1],
                                             base[:, k, :], ALU.mult, ALU.add).then_inc(s["res_made"], 1)
            run(dve, ahead, work)
            finish(E - 1, 1)

        @block.tensor
        def _(pe):
            def ahead(e, par):
                for k in range(G):
                    need(pe, s["normed"], G * e + k + 1)
                    need(pe, s["x_low"], G * e + k - 1)
                    for c in range(KD):
                        last = pe.transpose(x_bank[k % 2][:, c * P:(c + 1) * P], y[:, k, c * P:(c + 1) * P],
                                            ident[:, :])
                    last.then_inc(s["x_turned"], 1)
                if not isinstance(e, int) or e > 0:
                    second(e - 1, 1 - par)

            def work(e, par):
                need(pe, s["w_low"], 2 * e + 1)
                need(pe, s["x_low"], G * (e + 1))
                for c in range(KD):
                    need(pe, s["h_relu"], KD * e + c - 1)
                    for k in range(KD):
                        last = product(pe, h_bank[c % 2][:, :],
                                       [a[:, par, 0, k, c * P:(c + 1) * P] for a in (w_h, w_l)],
                                       [a[:, k, :] for a in (xt_h, xt_l)], k == 0, k == KD - 1)
                    last.then_inc(s["h_done"], 1)

            def second(e, par):
                need(pe, s["w_low"], 2 * e + 2)
                need(pe, s["h_low"], KD * (e + 1))
                for k in range(G):
                    need(pe, s["res_made"], G * e + k - 1)
                    for c in range(KD):
                        last = product(pe, o_bank[k % 2][:, :], [a[:, c, k * P:(k + 1) * P] for a in (ht_h, ht_l)],
                                       [a[:, par, 1, c, :] for a in (w_h, w_l)], c == 0, c == KD - 1)
                    last.then_inc(s["o_done"], 1)
            run(pe, ahead, work)
            second(E - 1, 1)


_INS = ['x', 'ctx_2048', 'L0_attn_Wqkv', 'L0_attn_bqkv', 'L0_attn_Wproj', 'L0_attn_bproj', 'L0_attn_mapping',
        'L0_xattn_Wq', 'L0_xattn_Wkv', 'L0_xattn_null_kv', 'L0_xattn_Wout', 'L0_xattn_ln_scale', 'L0_xattn_ln_bias',
        'L0_ffn_Wr', 'L0_ffn_br', 'L0_ffn_W1', 'L0_ffn_b1', 'L0_ffn_W2', 'L0_ffn_b2']


def kernel(**inputs):
    import numpy as _np
    import concourse.bacc as _bacc
    from concourse import mybir as _mybir
    from concourse.bass_utils import run_bass_kernel_spmd as _run

    nc = _bacc.Bacc("TRN2", target_bir_lowering=False, num_devices=1)
    arrays, args = {}, []
    for name in _INS:
        a = _np.ascontiguousarray(inputs[name])
        arrays[f"in_{name}_dram"] = a
        args.append(nc.dram_tensor(f"in_{name}_dram", a.shape, _mybir.dt.from_np(a.dtype), kind="ExternalInput").ap())
    args.append(nc.dram_tensor("out_0_dram", (B, M, D), F32, kind="ExternalOutput").ap())
    decoder_kernel(nc, *args)
    r = _run(nc, [arrays], core_ids=[0])
    return r.results[0]["out_0_dram"]
```

```python
import concourse.bass as bass
from concourse import mybir
from concourse.alu_op_type import AluOpType as ALU
from contextlib import ExitStack

F32 = mybir.dt.float32
F32R = mybir.dt.float32r
I32 = mybir.dt.int32
ACT = mybir.ActivationFunctionType
AX = mybir.AxisListType

P = 128
B, M, D = 2, 2048, 512
T = B * M
NT = T // P
G = 4
NG = NT // G
KD = D // P
H1, D1, SEG, DIL, BLK = 16, 32, 128, 4, 64
NSEG = M // SEG
NKEY = SEG // DIL
SCALE1 = float(D1) ** -0.5
EPS_SUM = 1e-6
EPS1 = 1e-5
H2, D2, CTX, LC = 16, 64, 1024, 154
KC = CTX // P
REM = LC - P
L2 = LC + 1
PW = 160
INNER = H2 * D2
KI = INNER // P
SCALE2 = float(D2) ** -0.5
EPS2 = 1e-6
E = 8
CAP = T // E
ROW = D + 2
NOBODY = 2 * T


def need(eng, sem, value):
    if not isinstance(value, int) or value > 0:
        eng.wait_ge(sem, value)


def hold(eng, sem, value):
    if not isinstance(value, int) or value > 0:
        eng.wait_ge(sem, value)
        eng.nop(nofuse=True)


def product(pe, out, lhs, rhs, first, last):
    (lh, ll), (rh, rl) = lhs, rhs
    pe.matmul(out, lh, rh, start=first, stop=False)
    pe.matmul(out, lh, rl, start=False, stop=False)
    return pe.matmul(out, ll, rh, start=False, stop=last)


def decoder_kernel(nc, x, ctx, wqkv, bqkv, wproj, bproj, mapping, wq2, wkv2, null_kv, wout, ln_scale, ln_bias,
                   wr, br, w1, b1, w2, b2, out):
    x_rows = x.rearrange("b t d -> (b t) d")
    x_tiles = x_rows.rearrange("(n p) d -> p n d", p=P)
    out_rows = out.rearrange("b t d -> (b t) d")
    out_tiles = out_rows.rearrange("(n p) d -> p n d", p=P)
    x1_dram = nc.dram_tensor("x1_scratch", (T, D), F32, kind="Internal").ap()
    x1_tiles = x1_dram.rearrange("(n p) d -> p n d", p=P)
    slots_dram = nc.dram_tensor("slot_rows", (2 * T, ROW), F32, kind="Internal").ap()
    slot_tiles = slots_dram.rearrange("(n p) d -> p n d", p=P)

    with ExitStack() as keep:
        def sb(name, shape, dt=F32, stack=keep):
            return stack.enter_context(nc.sbuf_tensor(name, shape, dt))

        taken = []

        def sem(name):
            taken.append(nc.alloc_semaphore(name=name))
            return taken[-1]

        def release_sems():
            nc.clear_and_free_semaphores(taken)
            nc.all_engine_barrier()
            taken.clear()

        bank = [keep.enter_context(nc.psum_tensor(f"bank{n}", [P, 512], F32)) for n in range(8)]

        ident = sb("ident", [P, P])
        upper = sb("upper", [P, P])
        ones = sb("ones", [P, P])
        head_mask = sb("head_mask", [P, 4])
        minus_half = sb("minus_half", [P, 4])
        rev = sb("rev", [P, E])
        token_int = sb("token_int", [P, NT], I32)
        token_f = sb("token_f", [P, NT])
        lns_b = sb("lns_b", [P, D])
        lnb_b = sb("lnb_b", [P, D])
        br_b = sb("br_b", [P, E])
        wr_sb = sb("wr_sb", [P, KD, E])
        keys_values = ExitStack()
        k2 = sb("k2", [P, B, KI, 2, L2], F32, keys_values)
        v2_main = sb("v2_main", [P, B, INNER], F32, keys_values)
        v2_rest = sb("v2_rest", [P, B, 4, 4 * D2], F32, keys_values)

        stage_a = ExitStack()
        with stage_a:
            wq_h = sb("wq_h", [P, KD, D], F32R, stage_a)
            wq_l = sb("wq_l", [P, KD, D], F32R, stage_a)
            wp_h = sb("wp_h", [P, KD, D], F32R, stage_a)
            wp_l = sb("wp_l", [P, KD, D], F32R, stage_a)
            bproj_b = sb("bproj_b", [P, D], F32, stage_a)
            bq_col = sb("bq_col", [P, KD], F32, stage_a)
            k1 = sb("k1", [P, KD, B * NSEG, NKEY], F32, stage_a)
            v1 = sb("v1", [P, B * NSEG, KD * D1], F32, stage_a)
            idx_all = sb("idx_all", [P, NT], I32, stage_a)
            head_ones = sb("head_ones", [P, P], F32, stage_a)
            seg_tab = sb("seg_tab", [1, T // BLK], I32, stage_a)
            with ExitStack() as st:
                setup(nc, sem, lambda *a: sb(*a, stack=st), bank, x_rows, ctx, wqkv, bqkv, wproj, bproj, mapping, wkv2,
                      null_kv, ln_scale, ln_bias, wr, br, slot_tiles, ident, upper, ones, head_mask, minus_half, rev,
                      token_int, token_f, bproj_b, lns_b, lnb_b, br_b, wr_sb, k2, v2_main, v2_rest,
                      wq_h, wq_l, wp_h, wp_l, bq_col, k1, v1, idx_all, head_ones, seg_tab)
            release_sems()
            with ExitStack() as st:
                self_attention(nc, sem, lambda *a: sb(*a, stack=st), bank, x_rows, x_tiles, x1_tiles, ident, head_mask,
                               minus_half, bproj_b, wq_h, wq_l, wp_h, wp_l, bq_col, k1, v1, idx_all, head_ones,
                               seg_tab)
        release_sems()
        with ExitStack() as st:
            cross_attention(nc, sem, lambda *a: sb(*a, stack=st), bank, x1_tiles, out_tiles, slots_dram, wq2, wout,
                            ident, upper, ones, minus_half, rev, token_int, token_f, lns_b, lnb_b, br_b, wr_sb, k2,
                            v2_main, v2_rest)
        keys_values.close()
        release_sems()
        with ExitStack() as st:
            experts(nc, sem, lambda *a: sb(*a, stack=st), bank, slot_tiles, out_rows, w1, b1, w2, b2, ident,
                    minus_half)


def setup(nc, sem, sb, bank, x_rows, ctx, wqkv, bqkv, wproj, bproj, mapping, wkv2, null_kv, ln_scale, ln_bias, wr, br,
          slot_tiles, ident, upper, ones, head_mask, minus_half, rev, token_int, token_f, bproj_b, lns_b, lnb_b, br_b,
          wr_sb, k2, v2_main, v2_rest, wq_h, wq_l, wp_h, wp_l, bq_col, k1, v1, idx_all, head_ones, seg_tab):
    CB = 256
    NC = 2 * INNER // CB
    KB, HB = NC // 2, CB // P
    raw = sb("raw", [P, 2, 2048])
    wc_h = sb("wc_h", [P, 2, 8, CB], F32R)
    wc_l = sb("wc_l", [P, 2, 8, CB], F32R)
    ctx_sb = sb("ctx_sb", [P, 3, CTX])
    ct_h = sb("ct_h", [P, KC, 3 * P], F32R)
    ct_l = sb("ct_l", [P, KC, 3 * P], F32R)
    xk = ctx_sb[:, 0:2, :].rearrange("p a (b d) -> p (a b) d", d=D)
    xkt_h = ct_h[:, :, :].rearrange("p k t -> p (k t)")[:, 0:KD * 512].rearrange("p (k t) -> p k t", k=KD)
    xkt_l = ct_l[:, :, :].rearrange("p k t -> p (k t)")[:, 0:KD * 512].rearrange("p (k t) -> p k t", k=KD)
    v_tmp = sb("v_tmp", [P, 2, D])
    v_last = v_tmp[:, :, :].rearrange("p a d -> p (a d)")
    bk_col = sb("bk_col", [P, KD])
    bv_b = sb("bv_b", [P, D])
    null_k = sb("null_k", [P, 1])
    map_raw = sb("map_raw", [P, NT], I32)
    kmap = sb("kmap", [P, 4], I32)
    kidx = sb("kidx", [P, B, 4], I32)
    seg_raw = sb("seg_raw", [1, T // BLK], I32)
    empty_row = sb("empty_row", [P, ROW])
    stats = sb("stats", [P, 4, 6])
    mv = sb("mv", [P, 4, 2])
    var_eps = sb("var_eps", [P, 4])
    rstd = sb("rstd", [P, 4])

    maps_loaded, ctx_loaded, biases_loaded = sem("maps_loaded"), sem("ctx_loaded"), sem("biases_loaded")
    raw_loaded = [sem("raw_loaded0"), sem("raw_loaded1")]
    raw_high, raw_low = sem("raw_high"), sem("raw_low")
    zeroed, masks, tables = sem("zeroed"), sem("masks"), sem("tables")
    ctx_zeroed, null_k_loaded, null_v_loaded = sem("ctx_zeroed"), sem("null_k_loaded"), sem("null_v_loaded")
    prefilled, empty_made, rest_placed = sem("prefilled"), sem("empty_made"), sem("rest_placed")
    turned, turned_high, turned_low = sem("turned"), sem("turned_high"), sem("turned_low")
    kv_done, block_done, kv_evac = sem("kv_done"), sem("block_done"), sem("kv_evac")
    xk_loaded, xk_stats, xk_aggr, xk_eps = sem("xk_loaded"), sem("xk_stats"), sem("xk_aggr"), sem("xk_eps")
    xk_rstd, xk_norm, v_done, v_biased = sem("xk_rstd"), sem("xk_norm"), sem("v_done"), sem("v_biased")
    v_copied, v_copied_act = sem("v_copied"), sem("v_copied_act")

    units = []
    for n in range(NC):
        units.append((wkv2[:, n * CB:(n + 1) * CB], 8, wc_h[:, n % 2, :, :], wc_l[:, n % 2, :, :]))
    for part in range(2):
        units.append((wqkv[:, (part + 1) * D:(part + 2) * D], 4,
                      *(a[:, part, :, :].rearrange("p k n -> p (k n)").rearrange("p (k n) -> p k n", k=4)
                        for a in (wc_h, wc_l))))
    wkv_a = [(units[NC + part][2], units[NC + part][3]) for part in range(2)]
    units.append((wqkv[:, 0:D], 4, wq_h[:, :, :], wq_l[:, :, :]))
    units.append((wproj[:, :], 4, wp_h[:, :, :], wp_l[:, :, :]))
    NU = len(units)
    CR = 3 * 2
    NR = CR + 4 * B

    block = nc.Block()
    with block as block:
        @block.sync
        def _(sp):
            with nc.allow_non_contiguous_dma(reason="small tables by column"):
                for b in range(B):
                    sp.dma_start(map_raw[:, b * 16:(b + 1) * 16],
                                 mapping.rearrange("(n p) -> p n", p=P)).then_inc(maps_loaded, 16)
                    sp.dma_start(seg_raw[0:1, b * 32:(b + 1) * 32],
                                 mapping.rearrange("(a n f) -> a n f", a=1, f=BLK)[:, :, 0]).then_inc(maps_loaded, 16)
                sp.dma_start(kmap[:, :], mapping.rearrange("(n p f) -> p n f", p=P, f=DIL)[:, :, 0])\
                    .then_inc(maps_loaded, 16)
            for b in range(B):
                sp.dma_start(ctx_sb[:, b, :], ctx[b, 0:P, :]).then_inc(ctx_loaded, 16)
            sp.wait_ge(ctx_zeroed, 1)
            for b in range(B):
                sp.dma_start(ctx_sb[32 * b:32 * b + REM, 2, :], ctx[b, P:LC, :]).then_inc(ctx_loaded, 16)
            for u, (src, chunks, _, _) in enumerate(units):
                need(sp, raw_low, u - 1)
                sp.dma_start(raw[:, u % 2, :].rearrange("p (k n) -> p k n", k=chunks),
                             src.rearrange("(k p) n -> p k n", p=P))\
                    .then_inc(raw_loaded[u % 2], 16)
            sp.wait_ge(kv_evac, KB * HB + KB * 3)
            sp.wait_ge(zeroed, 1)
            for b in range(B):
                for h in range(4):
                    sp.dma_start(v2_rest[h:h + 4 * (REM - 1) + 1:4, b, :, h * D2:(h + 1) * D2],
                                 v_last[32 * b:32 * b + REM, :].rearrange("p (g h d) -> p g h d", g=4, h=4)
                                 [:, :, h, :]).then_inc(rest_placed, 16)
            sp.wait_ge(empty_made, 2)
            sp.dma_start(slot_tiles[:, 0:NT, :],
                         empty_row[:, :].rearrange("p (a d) -> p a d", a=1).to_broadcast([P, NT, ROW]))\
                .then_inc(prefilled, 16)
            sp.wait_ge(prefilled, 16)
            sp.wait_ge(rest_placed, 16 * 4 * B)

        @block.gpsimd
        def _(pool):
            pool.memset(ctx_sb[:, 2, :], 0.0).then_inc(ctx_zeroed, 1)
            pool.memset(ident[:, :], 0.0).then_inc(masks, 1)
            pool.memset(upper[:, :], 1.0).then_inc(masks, 1)
            pool.memset(head_mask[:, :], 1.0).then_inc(masks, 1)
            pool.memset(ones[:, :], 1.0).then_inc(masks, 1)
            pool.memset(minus_half[:, :], -0.5).then_inc(masks, 1)
            pool.wait_ge(masks, 5)
            pool.affine_select(out=ident[:, :], in_=ident[:, :], compare_op=ALU.not_equal, fill=1.0, base=0,
                               pattern=[[-1, P]], channel_multiplier=1).then_inc(masks, 1)
            pool.affine_select(out=upper[:, :], in_=upper[:, :], compare_op=ALU.is_ge, fill=0.0, base=0,
                               pattern=[[1, P]], channel_multiplier=-1).then_inc(masks, 1)
            pool.affine_select(out=head_mask[:, :], in_=head_mask[:, :], compare_op=ALU.is_ge, fill=0.0, base=0,
                               pattern=[[-32, 4]], channel_multiplier=1).then_inc(masks, 1)
            pool.wait_ge(masks, 8)
            pool.affine_select(out=head_mask[:, :], in_=head_mask[:, :], compare_op=ALU.is_ge, fill=0.0, base=31,
                               pattern=[[32, 4]], channel_multiplier=-1).then_inc(masks, 1)
            pool.iota(token_int[:, :], pattern=[[P, NT]], base=0, channel_multiplier=1).then_inc(masks, 1)
            pool.wait_ge(tables, 1)
            for b in range(B):
                pool.wait_ge(turned, CR + 4 * b)
                for n in range(4):
                    pool.indirect_dma_start(out=xk[:, n, :], out_offset=None, in_=x_rows,
                                            in_offset=bass.IndirectOffsetOnAxis(ap=kidx[:, b, n:n + 1], axis=0))\
                        .then_inc(xk_loaded, 16)
                pool.wait_ge(xk_eps, b + 1)
                pool.tensor_tensor(rstd[:, :], var_eps[:, :], minus_half[:, :], ALU.pow).then_inc(xk_rstd, 1)

        @block.scalar
        def _(act):
            with nc.allow_non_contiguous_dma(reason="small biases by column"):
                act.dma_start(bq_col[:, :], bqkv[0:D].rearrange("(c p) -> p c", p=P)).then_inc(biases_loaded, 16)
                act.dma_start(bk_col[:, :], bqkv[D:2 * D].rearrange("(c p) -> p c", p=P)).then_inc(biases_loaded, 16)
                act.dma_start(bv_b[:, :], bqkv[2 * D:3 * D].partition_broadcast(P)).then_inc(biases_loaded, 16)
                act.dma_start(bproj_b[:, :], bproj.partition_broadcast(P)).then_inc(biases_loaded, 16)
                act.dma_start(lns_b[:, :], ln_scale.partition_broadcast(P)).then_inc(biases_loaded, 16)
                act.dma_start(lnb_b[:, :], ln_bias.partition_broadcast(P)).then_inc(biases_loaded, 16)
                act.dma_start(br_b[:, :], br.partition_broadcast(P)).then_inc(biases_loaded, 16)
                act.dma_start(wr_sb[:, :, :], wr.rearrange("(k p) e -> p k e", p=P)).then_inc(biases_loaded, 16)
                for s in range(2):
                    act.dma_start(null_k[s * D2:(s + 1) * D2, :], null_kv[0, :].rearrange("(d a) -> d a", a=1))\
                        .then_inc(null_k_loaded, 16)
                act.wait_ge(zeroed, 1)
                for b in range(B):
                    for h in range(4):
                        act.dma_start(v2_rest[4 * REM + h:4 * REM + h + 1, b, :, h * D2:(h + 1) * D2],
                                      null_kv[1:2, :].rearrange("a (o d) -> a o d", o=1).to_broadcast([1, 4, D2]))\
                            .then_inc(null_v_loaded, 16)

            def split(u):
                if 2 <= u < NC + 2:
                    act.wait_ge(block_done, u - 1)
                act.wait_ge(raw_loaded[u % 2], 16 * (u // 2 + 1))
                act.activation(units[u][2], raw[:, u % 2, :].rearrange("p (k n) -> p k n", k=units[u][1]), ACT.Copy).then_inc(raw_high, 1)

            def turn(r):
                act.wait_ge(turned, r + 1)
                if r < CR:
                    dst = ct_h[:, 4 * (r % 2):4 * (r % 2) + 4, (r // 2) * P:(r // 2 + 1) * P]
                else:
                    dst = xkt_h[:, :, ((r - CR) % 4) * P:((r - CR) % 4 + 1) * P]
                act.activation(dst, bank[r % 2][:, :].rearrange("p (k t) -> p k t", k=4), ACT.Copy)\
                    .then_inc(turned_high, 1)

            for r in range(CR):
                turn(r)
            split(0)
            m = 0
            for n in range(NC):
                split(n + 1)
                for c in range(HB if n < KB else 3):
                    act.wait_ge(kv_done, m + 1)
                    src = bank[2 + m % 3]
                    if n < KB:
                        act.wait_ge(zeroed, 2)
                        for s in range(2):
                            rows = slice(s * D2, (s + 1) * D2)
                            act.activation(k2[rows, :, HB * n + c, s, 0:P],
                                           src[rows, 0:2 * P].rearrange("p (b k) -> p b k", b=B), ACT.Copy,
                                           scale=SCALE2)
                            last = act.activation(
                                k2[rows, :, HB * n + c, s, P:LC],
                                src[rows, 2 * P:2 * P + 64].rearrange("p (b k) -> p b k", b=B)[:, :, 0:REM],
                                ACT.Copy, scale=SCALE2)
                    elif c < 2:
                        last = act.activation(v2_main[:, c, (n - KB) * CB:(n - KB + 1) * CB], src[:, 0:CB], ACT.Copy)
                    else:
                        last = act.activation(v_last[0:64, (n - KB) * CB:(n - KB + 1) * CB], src[0:64, 0:CB], ACT.Copy)
                    last.then_inc(kv_evac, 1)
                    m += 1
            split(NC + 1)
            act.wait_ge(null_k_loaded, 32)
            for s in range(2):
                rows = slice(s * D2, (s + 1) * D2)
                act.activation(k2[rows, :, :, s, LC:L2],
                               null_k[rows, 0:1].rearrange("p (a b c) -> p a b c", a=1, b=1)
                               .to_broadcast([D2, B, KI, 1]), ACT.Copy, scale=SCALE2)
            for u in range(NC + 2, NU):
                split(u)
            act.wait_ge(biases_loaded, 16 * 8)
            for b in range(B):
                for n in range(4):
                    turn(CR + 4 * b + n)
                for c in range(KD):
                    act.wait_ge(kv_done, m + 1)
                    act.activation(k1[:, c, b * NSEG:b * NSEG + NSEG, :],
                                   bank[2 + m % 3][:, :].rearrange("p (s k) -> p s k", s=NSEG), ACT.Identity,
                                   bias=bk_col[:, c:c + 1]).then_inc(kv_evac, 1)
                    m += 1
                for n in range(4):
                    i = 4 * b + n
                    act.wait_ge(v_biased, i + 1)
                    for s in range(4):
                        for h in (2, 3):
                            last = act.activation(
                                v1[32 * h:32 * h + 32, b * NSEG + 4 * n + s, :].rearrange("p (c d) -> p c d", c=KD),
                                v_tmp[32 * s:32 * s + 32, i % 2, :].rearrange("p (c h d) -> p c h d", c=KD, h=4)
                                [:, :, h, :], ACT.Copy)
                    last.then_inc(v_copied_act, 1)
            act.wait_ge(null_v_loaded, 16 * 4 * B)

        @block.vector
        def _(dve):
            dve.memset(v2_rest[:, :, :, :], 0.0).then_inc(zeroed, 1)
            dve.memset(k2[:, :, :, :, :], 0.0).then_inc(zeroed, 1)
            dve.memset(empty_row[:, :], 0.0).then_inc(empty_made, 1)
            dve.wait_ge(empty_made, 1)
            dve.memset(empty_row[:, D + 1:D + 2].bitcast(I32), NOBODY).then_inc(empty_made, 1)
            dve.wait_ge(maps_loaded, 16 * (2 * B + 1))
            for b in range(B):
                last = dve.tensor_scalar(kidx[:, b, :], kmap[:, :], M - 1, b * M, ALU.min, ALU.add)
            last.then_inc(tables, 1)
            for b in range(B):
                dve.tensor_scalar(idx_all[:, 16 * b:16 * b + 16], map_raw[:, 16 * b:16 * b + 16], M - 1, b * M,
                                  ALU.min, ALU.add)
            dve.tensor_scalar(seg_raw[:, :], seg_raw[:, :], 7, None, ALU.arith_shift_right).then_inc(tables, 1)
            dve.wait_ge(tables, 2)
            for b in range(B):
                dve.tensor_scalar(seg_tab[:, 32 * b:32 * b + 32], seg_raw[:, 32 * b:32 * b + 32], NSEG - 1, b * NSEG,
                                  ALU.min, ALU.add)
            for e in range(E):
                dve.memset(rev[:, e:e + 1], float(E - e))
            dve.wait_ge(masks, 10)
            dve.tensor_copy(token_f[:, :], token_int[:, :])
            dve.tensor_copy(head_ones[:, :].rearrange("p (h d) -> p h d", h=4),
                            head_mask[:, :].rearrange("p (h d) -> p h d", d=1).to_broadcast([P, 4, 32]))

            def split(u):
                dve.wait_ge(raw_high, u + 1)
                dve.tensor_tensor(units[u][3], raw[:, u % 2, :].rearrange("p (k n) -> p k n", k=units[u][1]),
                                  units[u][2].bitcast(F32), ALU.subtract)\
                    .then_inc(raw_low, 1)

            def turn(r):
                dve.wait_ge(turned_high, r + 1)
                if r < CR:
                    cols = (slice(None), slice(4 * (r % 2), 4 * (r % 2) + 4), slice((r // 2) * P, (r // 2 + 1) * P))
                    high, low = ct_h[cols], ct_l[cols]
                else:
                    cols = (slice(None), slice(None), slice(((r - CR) % 4) * P, ((r - CR) % 4 + 1) * P))
                    high, low = xkt_h[cols], xkt_l[cols]
                dve.tensor_tensor(low, bank[r % 2][:, :].rearrange("p (k t) -> p k t", k=4), high.bitcast(F32),
                                  ALU.subtract).then_inc(turned_low, 1)

            for r in range(CR):
                turn(r)
            for u in range(NU):
                split(u)
            dve.wait_ge(biases_loaded, 16 * 8)
            dve.wait_ge(rest_placed, 16 * 4 * B)
            for b in range(B):
                dve.wait_ge(xk_loaded, 64 * (b + 1))
                for n in range(4):
                    last = dve.bn_stats(stats[:, n, :], xk[:, n, :])
                last.then_inc(xk_stats, 1)
                dve.wait_ge(xk_stats, b + 1)
                for n in range(4):
                    last = dve.bn_aggr(mv[:, n, :], stats[:, n, :])
                last.then_inc(xk_aggr, 1)
                dve.wait_ge(xk_aggr, b + 1)
                dve.tensor_scalar(var_eps[:, :], mv[:, :, 1], EPS1, None, ALU.add).then_inc(xk_eps, 1)
                dve.wait_ge(xk_rstd, b + 1)
                for n in range(4):
                    dve.tensor_scalar(xk[:, n, :], xk[:, n, :], mv[:, n, 0:1], rstd[:, n:n + 1], ALU.subtract,
                                      ALU.mult).then_inc(xk_norm, 1)
                for n in range(4):
                    turn(CR + 4 * b + n)
                for n in range(4):
                    i = 4 * b + n
                    dve.wait_ge(v_done, i + 1)
                    need(dve, v_copied, i - 1)
                    need(dve, v_copied_act, i - 1)
                    dve.tensor_tensor(v_tmp[:, i % 2, :], bank[5 + i % 2][:, :], bv_b[:, :], ALU.add)\
                        .then_inc(v_biased, 1)
                    dve.wait_ge(v_biased, i + 1)
                    for s in range(4):
                        for h in (0, 1):
                            last = dve.tensor_copy(
                                v1[32 * h:32 * h + 32, b * NSEG + 4 * n + s, :].rearrange("p (c d) -> p c d", c=KD),
                                v_tmp[32 * s:32 * s + 32, i % 2, :].rearrange("p (c h d) -> p c h d", c=KD, h=4)
                                [:, :, h, :])
                    last.then_inc(v_copied, 1)

        @block.tensor
        def _(pe):
            pe.wait_ge(masks, 9)

            def turn(r, src):
                need(pe, turned_low, r - 1)
                for k in range(4):
                    last = pe.transpose(bank[r % 2][:, k * P:(k + 1) * P], src(k), ident[:, :])
                last.then_inc(turned, 1)

            pe.wait_ge(ctx_loaded, 64)
            for r in range(CR):
                turn(r, lambda k, r=r: ctx_sb[:, r // 2, (4 * (r % 2) + k) * P:(4 * (r % 2) + k + 1) * P])
            pe.wait_ge(turned_low, CR)
            m = 0
            for n in range(NC):
                pe.wait_ge(raw_low, n + 1)
                for c in range(HB if n < KB else 3):
                    need(pe, kv_evac, m - 2)
                    for k in range(KC):
                        if n < KB:
                            w = [a[:, n % 2, k, c * P:(c + 1) * P] for a in (wc_h, wc_l)]
                            last = product(pe, bank[2 + m % 3][:, 0:3 * P], w, [a[:, k, :] for a in (ct_h, ct_l)],
                                           k == 0, k == KC - 1)
                        else:
                            t = [a[:, k, c * P:(c + 1) * P] for a in (ct_h, ct_l)]
                            last = product(pe, bank[2 + m % 3][:, 0:CB], t,
                                           [a[:, n % 2, k, :] for a in (wc_h, wc_l)], k == 0, k == KC - 1)
                    last.then_inc(kv_done, 1)
                    m += 1
                pe.wait_ge(kv_done, m)
                pe.sem_inc(block_done, 1)
            pe.wait_ge(raw_low, NC + 2)
            for b in range(B):
                for n in range(4):
                    pe.wait_ge(xk_norm, 4 * b + n + 1)
                    turn(CR + 4 * b + n, lambda k, n=n: xk[:, n, k * P:(k + 1) * P])
                pe.wait_ge(turned_low, CR + 4 * b + 4)
                for c in range(KD):
                    need(pe, kv_evac, m - 2)
                    for k in range(KD):
                        w = [a[:, k, c * P:(c + 1) * P] for a in wkv_a[0]]
                        last = product(pe, bank[2 + m % 3][:, :], w, [a[:, k, :] for a in (xkt_h, xkt_l)], k == 0,
                                       k == KD - 1)
                    last.then_inc(kv_done, 1)
                    m += 1
                for n in range(4):
                    i = 4 * b + n
                    need(pe, v_biased, i - 1)
                    for k in range(KD):
                        t = [a[:, k, n * P:(n + 1) * P] for a in (xkt_h, xkt_l)]
                        last = product(pe, bank[5 + i % 2][:, :], t,
                                       [a[:, k, :] for a in wkv_a[1]], k == 0, k == KD - 1)
                    last.then_inc(v_done, 1)


def self_attention(nc, sem, sb, bank, x_rows, x_tiles, x1_tiles, ident, head_mask, minus_half, bproj_b, wq_h, wq_l,
                   wp_h, wp_l, bq_col, k1, v1, idx_all, head_ones, seg_tab):
    idx = sb("a_idx", [P, G], I32)
    xg = sb("a_xg", [P, G, D])
    xt_h = sb("a_xt_h", [P, KD, G * P], F32R)
    xt_l = sb("a_xt_l", [P, KD, G * P], F32R)
    qt = sb("a_qt", [P, KD, G * P])
    k_block = sb("a_k_block", [P, 4, KD, 4, NKEY])
    v_block = sb("a_v_block", [P, 4, KD, 4, D1])
    prob = sb("a_prob", [P, G, D])
    top = sb("a_top", [P, G, 2 * KD])
    total, recip = sb("a_total", [P, H1]), sb("a_recip", [P, H1])
    recip_wide = sb("a_recip_wide", [P, D])
    recip_t = sb("a_recip_t", [P, D])
    mixed = sb("a_mixed", [P, D])
    at_h = sb("a_at_h", [P, 2, KD, P], F32R)
    at_l = sb("a_at_l", [P, 2, KD, P], F32R)
    xr = sb("a_xr", [P, G, D])
    stats = sb("a_stats", [P, G, 6])
    mv = sb("a_mv", [P, G, 2])
    var_eps = sb("a_var_eps", [P, G])
    rstd = sb("a_rstd", [P, G])

    names = ("slot_tables gathered0 gathered1 gathered2 gathered3 stats_done aggr_done eps_done rstd_done normed "
             "x_turned x_high x_low q_done q_evac k_ready v_ready s_done s_top s_shifted s_exp a_done sum_done "
             "sum_eps sum_recip recip_spread recip_turned recip_evac a_norm a_high a_low proj_done x1_made res_biased").split()
    s = {n: sem("a_" + n) for n in names}
    xr_loaded = [sem(f"a_xr_loaded{t}") for t in range(G)]
    x1_stored = [sem(f"a_x1_stored{t}") for t in range(G)]
    x_bank, q_bank, s_bank, sum_bank, a_bank, o_bank, r_bank = (bank[0], bank[1:3], bank[3], bank[4], bank[5],
                                                                bank[6], bank[7])

    def run(eng, step):
        for i in (-2, -1, 0):
            step(i)
        with eng.Fori(1, NG - 2) as i:
            step(i)
        for i in (NG - 2, NG - 1, NG):
            step(i)

    def there(i):
        return not isinstance(i, int) or 0 <= i < NG

    def tiled(n):
        return not isinstance(n, int) or 0 <= n < NT

    block = nc.Block()
    with block as block:
        @block.sync
        def _(sp):
            def step(i):
                for t in range(G):
                    n = G * i + t
                    k = (t + 2) % G
                    if tiled(n - 2):
                        need(sp, s["x1_made"], n - 1)
                        sp.dma_start(x1_tiles[:, n - 2, :], xr[:, k, :]).then_inc(x1_stored[k], 16)
                    if tiled(n + 2):
                        need(sp, x1_stored[k], 16 * (i if t < 2 else i + 1))
                        sp.dma_start(xr[:, k, :], x_tiles[:, n + 2, :]).then_inc(xr_loaded[k], 16)
            run(sp, step)
            for t in range(G):
                sp.wait_ge(x1_stored[t], 16 * NG)

        @block.gpsimd
        def _(pool):
            def spread(dst, src):
                return pool.tensor_tensor(dst, src, head_mask[:, :].rearrange("p (a h d) -> p a h d", a=1, d=1)
                                          .to_broadcast([P, KD, 4, 32]), ALU.mult)

            def segment(n, j):
                return pool.value_load(seg_tab[0:1, bass.ds(2 * n + j, 1)], min_val=0, max_val=B * NSEG - 1)

            def step(i):
                for t in range(G):
                    n = G * i + t
                    m, k = n + 7, (t + 3) % G
                    if tiled(n + 1):
                        hold(pool, s["a_done"], n)
                        for j in range(2):
                            g = segment(n + 1, j)
                            ins = spread(v_block[:, 2 * ((t + 1) % 2) + j, :, :, :],
                                         v1[:, bass.ds(g, 1), :].rearrange("p a (c d) -> p c a d", c=KD)
                                         .to_broadcast([P, KD, 4, D1]))
                        ins.then_inc(s["v_ready"], 1)
                    if tiled(n + 2):
                        hold(pool, s["s_done"], n + 1)
                        for j in range(2):
                            g = segment(n + 2, j)
                            ins = spread(k_block[:, 2 * (t % 2) + j, :, :, :],
                                         k1[:, :, bass.ds(g, 1), :].to_broadcast([P, KD, 4, NKEY]))
                        ins.then_inc(s["k_ready"], 1)
                    if tiled(n):
                        hold(pool, xr_loaded[t], 16 * (i + 1))
                        pool.tensor_tensor(xr[:, t, :], xr[:, t, :], bproj_b[:, :], ALU.add)\
                            .then_inc(s["res_biased"], 1)
                    if there(i + 2):
                        hold(pool, s["x_turned"], G * (i + 1) + t + 1)
                        hold(pool, s["slot_tables"], n + 9)
                        pool.indirect_dma_start(out=xg[:, t, :], out_offset=None, in_=x_rows,
                                                in_offset=bass.IndirectOffsetOnAxis(ap=idx[:, t:t + 1], axis=0))\
                            .then_inc(s[f"gathered{t}"], 16)
                    if there(i + 2 if t else i + 1):
                        hold(pool, s["eps_done"], m + 1)
                        pool.tensor_tensor(rstd[:, k:k + 1], var_eps[:, k:k + 1], minus_half[:, 0:1], ALU.pow)\
                            .then_inc(s["rstd_done"], 1)
            run(pool, step)

        @block.scalar
        def _(act):
            def expo(n, t):
                need(act, s["s_shifted"], n + 1)
                act.activation(prob[:, t % G, :], prob[:, t % G, :], ACT.Exp, scale=SCALE1).then_inc(s["s_exp"], 1)

            def q_copy(i, c):
                need(act, s["q_done"], KD * i + c + 1)
                act.activation(qt[:, c, :], q_bank[c % 2][:, :], ACT.Identity, bias=bq_col[:, c:c + 1])\
                    .then_inc(s["q_evac"], 1)

            def xt_copy(i, k):
                need(act, s["x_turned"], G * i + k + 1)
                act.activation(xt_h[:, :, k * P:(k + 1) * P], x_bank[:, :].rearrange("p (k t) -> p k t", k=KD),
                               ACT.Copy).then_inc(s["x_high"], 1)

            def step(i):
                for t in range(G):
                    n = G * i + t
                    if tiled(n):
                        need(act, s["sum_recip"], n + 1)
                        act.activation(recip_wide[:, :].rearrange("p (h d) -> p h d", h=H1),
                                       recip[:, :].rearrange("p (h d) -> p h d", d=1).to_broadcast([P, H1, D1]),
                                       ACT.Copy).then_inc(s["recip_spread"], 1)
                    if t < 3 and tiled(n + 1):
                        expo(n + 1, t + 1)
                    if there(i + 1):
                        if t < 2:
                            xt_copy(i + 1, 2 * t)
                        else:
                            q_copy(i + 1, 2 * (t - 2))
                    if tiled(n):
                        need(act, s["recip_turned"], n + 1)
                        act.activation(recip_t[:, :], r_bank[:, :], ACT.Copy).then_inc(s["recip_evac"], 1)
                        need(act, s["a_norm"], n + 1)
                        act.activation(at_h[:, t % 2, :, :], mixed[:, :].rearrange("p (c t) -> p c t", c=KD),
                                       ACT.Copy).then_inc(s["a_high"], 1)
                    if there(i + 1):
                        if t < 2:
                            xt_copy(i + 1, 2 * t + 1)
                        else:
                            q_copy(i + 1, 2 * (t - 2) + 1)
                    if t == 3 and tiled(n + 1):
                        expo(n + 1, t + 1)
            run(act, step)

        @block.vector
        def _(dve):
            def shift(n, t):
                s3 = s_bank[:, :].rearrange("p (c q) -> p c q", q=BLK)
                need(dve, s["s_done"], n + 1)
                dve.tensor_reduce(top[:, t % G, :], s3, AX.X, ALU.max).then_inc(s["s_top"], 1)
                need(dve, s["s_top"], n + 1)
                dve.tensor_tensor(prob[:, t % G, :].rearrange("p (c q) -> p c q", q=BLK), s3,
                                  top[:, t % G, :].rearrange("p (c q) -> p c q", q=1)
                                  .to_broadcast([P, 2 * KD, BLK]), ALU.subtract).then_inc(s["s_shifted"], 1)

            def xt_copy(i, k):
                need(dve, s["x_high"], G * i + k + 1)
                dve.tensor_tensor(xt_l[:, :, k * P:(k + 1) * P], x_bank[:, :].rearrange("p (k t) -> p k t", k=KD),
                                  xt_h[:, :, k * P:(k + 1) * P].bitcast(F32), ALU.subtract)\
                    .then_inc(s["x_low"], 1)

            def step(i):
                for t in range(G):
                    n = G * i + t
                    m, k = n + 7, (t + 3) % G
                    if there(i + 2):
                        need(dve, s[f"gathered{t}"], 16 * (i + 2))
                        dve.tensor_scalar(idx[:, t:t + 1], idx_all[:, bass.ds(n + 8, 1)], 0, None, ALU.add)\
                            .then_inc(s["slot_tables"], 1)
                    if tiled(n - 2):
                        need(dve, s["proj_done"], n - 1)
                        need(dve, s["res_biased"], n - 1)
                        r = (t + 2) % G
                        dve.tensor_tensor(xr[:, r, :], o_bank[:, :], xr[:, r, :], ALU.add).then_inc(s["x1_made"], 1)
                    if tiled(n):
                        need(dve, s["sum_done"], n + 1)
                        dve.tensor_scalar(total[:, :], sum_bank[:, 0:H1], EPS_SUM, None, ALU.add)\
                            .then_inc(s["sum_eps"], 1)
                        need(dve, s["sum_eps"], n + 1)
                        dve.reciprocal(recip[:, :], total[:, :]).then_inc(s["sum_recip"], 1)
                    if t < 3 and tiled(n + 1):
                        shift(n + 1, t + 1)
                    if t < 2 and there(i + 1):
                        xt_copy(i + 1, 2 * t)
                    if tiled(n):
                        need(dve, s["a_done"], n + 1)
                        need(dve, s["recip_evac"], n + 1)
                        dve.tensor_tensor(mixed[:, :], a_bank[:, :], recip_t[:, :], ALU.mult).then_inc(s["a_norm"], 1)
                    if there(i + 2 if t else i + 1):
                        need(dve, s[f"gathered{k}"], 16 * ((i + 2 if t else i + 1) + 1))
                        dve.bn_stats(stats[:, k, :], xg[:, k, :]).then_inc(s["stats_done"], 1)
                        hold(dve, s["stats_done"], m + 1)
                        dve.bn_aggr(mv[:, k, :], stats[:, k, :]).then_inc(s["aggr_done"], 1)
                        need(dve, s["aggr_done"], m + 1)
                        dve.tensor_scalar(var_eps[:, k:k + 1], mv[:, k, 1:2], EPS1, None, ALU.add)\
                            .then_inc(s["eps_done"], 1)
                    if tiled(n):
                        need(dve, s["a_high"], n + 1)
                        dve.tensor_tensor(at_l[:, t % 2, :, :], mixed[:, :].rearrange("p (c t) -> p c t", c=KD),
                                          at_h[:, t % 2, :, :].bitcast(F32), ALU.subtract).then_inc(s["a_low"], 1)
                    if t < 2 and there(i + 1):
                        xt_copy(i + 1, 2 * t + 1)
                    if there(i + 2 if t else i + 1):
                        need(dve, s["rstd_done"], m + 1)
                        dve.tensor_scalar(xg[:, k, :], xg[:, k, :], mv[:, k, 0:1], rstd[:, k:k + 1], ALU.subtract,
                                          ALU.mult).then_inc(s["normed"], 1)
                    if t == 3 and tiled(n + 1):
                        shift(n + 1, t + 1)
            run(dve, step)

        @block.tensor
        def _(pe):
            def sums(n, t):
                need(pe, s["s_exp"], n + 1)
                need(pe, s["sum_eps"], n)
                for c in range(KD):
                    last = pe.matmul(sum_bank[:, 4 * c:4 * c + 4], prob[:, t, c * P:(c + 1) * P], head_mask[:, :],
                                     start=True, stop=True)
                last.then_inc(s["sum_done"], 1)

            def scores(n, t):
                need(pe, s["k_ready"], n + 1)
                need(pe, s["s_shifted"], n)
                for c in range(KD):
                    for j in range(2):
                        o = c * P + BLK * j
                        last = pe.matmul(s_bank[:, o:o + BLK], k_block[:, 2 * (t % 2) + j, c, :, :],
                                         qt[:, c, (t % G) * P + BLK * j:(t % G) * P + BLK * (j + 1)], start=True,
                                         stop=True)
                last.then_inc(s["s_done"], 1)

            def values(n, t):
                need(pe, s["v_ready"], n + 1)
                need(pe, s["a_norm"], n)
                for c in range(KD):
                    for j in range(2):
                        o = c * P + BLK * j
                        last = pe.matmul(a_bank[:, o:o + BLK], v_block[:, 2 * (t % 2) + j, c, :, :],
                                         prob[:, t, o:o + BLK], start=True, stop=True)
                last.then_inc(s["a_done"], 1)

            def turn_x(i, k):
                need(pe, s["normed"], G * i + k + 1)
                need(pe, s["x_low"], G * i + k)
                for c in range(KD):
                    last = pe.transpose(x_bank[:, c * P:(c + 1) * P], xg[:, k, c * P:(c + 1) * P], ident[:, :])
                last.then_inc(s["x_turned"], 1)

            def turn_recip(n):
                need(pe, s["recip_spread"], n + 1)
                need(pe, s["recip_evac"], n)
                for c in range(KD):
                    last = pe.transpose(r_bank[:, c * P:(c + 1) * P], recip_wide[:, c * P:(c + 1) * P], ident[:, :])
                last.then_inc(s["recip_turned"], 1)

            def queries(i, c):
                need(pe, s["x_low"], G * (i + 1))
                need(pe, s["q_evac"], KD * i + c - 1)
                for k in range(KD):
                    last = product(pe, q_bank[c % 2][:, :], [a[:, k, c * P:(c + 1) * P] for a in (wq_h, wq_l)],
                                   [a[:, k, :] for a in (xt_h, xt_l)], k == 0, k == KD - 1)
                last.then_inc(s["q_done"], 1)

            def project(n, t, half):
                if half == 0:
                    need(pe, s["a_low"], n + 1)
                    need(pe, s["x1_made"], n)
                for c in range(2 * half, 2 * half + 2):
                    last = product(pe, o_bank[:, :], [a[:, t % 2, c, :] for a in (at_h, at_l)],
                                   [a[:, c, :] for a in (wp_h, wp_l)], c == 0, c == KD - 1)
                if half:
                    last.then_inc(s["proj_done"], 1)

            def step(i):
                for t in range(G):
                    n = G * i + t
                    if tiled(n):
                        sums(n, t)
                    if t < 3 and tiled(n + 1):
                        scores(n + 1, t + 1)
                    if tiled(n):
                        values(n, t)
                    if there(i + 1):
                        if t < 2:
                            turn_x(i + 1, 2 * t)
                        else:
                            queries(i + 1, 2 * (t - 2))
                    if tiled(n):
                        turn_recip(n)
                    if t == 3 and there(i + 1):
                        queries(i + 1, 3)
                    if tiled(n - 1):
                        project(n - 1, t + 1, 0)
                    if t == 3 and tiled(n + 1):
                        need(pe, s["q_evac"], KD * (i + 2))
                        scores(n + 1, t + 1)
                    if tiled(n - 1):
                        project(n - 1, t + 1, 1)
                    if t == 2 and there(i + 1):
                        queries(i + 1, 1)
                    if t < 2 and there(i + 1):
                        turn_x(i + 1, 2 * t + 1)
            run(pe, step)


def cross_attention(nc, sem, sb, bank, x1_tiles, out_tiles, slots_dram, wq2, wout, ident, upper, ones, minus_half, rev,
                    token_int, token_f, lns_b, lnb_b, br_b, wr_sb, k2, v2_main, v2_rest):
    wq_h, wq_l = sb("b_wq_h", [P, KD, INNER], F32R), sb("b_wq_l", [P, KD, INNER], F32R)
    wo_h, wo_l = sb("b_wo_h", [P, KI, D], F32R), sb("b_wo_l", [P, KI, D], F32R)
    xn = sb("b_xn", [P, G, D])
    xt_h, xt_l = sb("b_xt_h", [P, KD, G * P], F32R), sb("b_xt_l", [P, KD, G * P], F32R)
    qt = sb("b_qt", [P, KI, G * P])
    prob = sb("b_prob", [P, 2, 4, PW, 4])
    raw = prob[:, :, :, :, :].rearrange("p a g k h -> p (a g k h)")[:, 0:2 * 2048].rearrange("p (a n) -> p a n", a=2)
    pt = sb("b_pt", [P, 4 + H2, P])
    o_sb = sb("b_o", [P, INNER])
    ot_h, ot_l = sb("b_ot_h", [P, KI, P], F32R), sb("b_ot_l", [P, KI, P], F32R)
    xr = sb("b_xr", [P, D])
    x2 = sb("b_x2", [P, 2, D])
    y = sb("b_y", [P, D])
    yt = sb("b_yt", [P, KD, P])
    rows = sb("b_rows", [P, G, ROW])
    neg_top, total, recip = sb("b_neg_top", [P, 2, H2]), sb("b_total", [P, 2, H2]), sb("b_recip", [P, H2])
    kinds = ("x", "w", "y")
    stats = {k: sb(f"b_{k}_stats", [P, 6]) for k in kinds}
    mv = {k: sb(f"b_{k}_mv", [P, 2]) for k in kinds}
    var_eps = {k: sb(f"b_{k}_var", [P, 1]) for k in kinds}
    rstd = {k: sb(f"b_{k}_rstd", [P, 1]) for k in kinds}
    logit = sb("b_logit", [P, G, E])
    p_e, q_e = sb("b_p_e", [P, G, E]), sb("b_q_e", [P, G, E])
    onehot = sb("b_onehot", [P, G, E])
    before = sb("b_before", [P, G + 1, E])
    c4 = {k: sb(f"b_{k}", [P, G]) for k in ("top4", "sum4", "rec4", "gate4", "rank4", "pos4", "keep4", "slot4")}
    slot_idx = sb("b_slot_idx", [P, G], I32)

    names = ("raw_high raw_low padded x_loaded0 x_loaded1 x_loaded2 x_loaded3 x_normed x_turned x_high x_low q_done "
             "q_evac s_done s_max s_exp s_recip pt_turned pt_evac pt_evac_act o_done o_evac ot_turned ot_high ot_low w_done "
             "w_normed xr_loaded xr_biased w_scaled x2_made y_normed y_turned y_evac l_done l_evac rows_loaded "
             "route_step route_exp onehot_made counted routed scattered").split()
    s = {n: sem("b_" + n) for n in names}
    raw_loaded = [sem("b_raw_loaded0"), sem("b_raw_loaded1")]
    x2_stored = [sem("b_x2_stored0"), sem("b_x2_stored1")]
    ln = {k: {n: sem(f"b_{k}_{n}") for n in ("stats", "aggr", "eps", "rstd")} for k in kinds}
    pt_bank, s_bank, q_bank, o_bank, w_bank, x_bank = bank[0:2], bank[2:4], bank[4], bank[5], bank[6], bank[7]
    PS = H2 // 2
    QUERIES = {(2, 1): 0, (2, 3): 1, (2, 5): 2, (2, 7): 3, (3, 0): 4, (3, 1): 5, (3, 3): 6, (3, 5): 7}
    RS1, RS2, COUNTS = 10, 13, 5

    units = [(wq2[:, n * 512:(n + 1) * 512], wq_h[:, :, n * 512:(n + 1) * 512], wq_l[:, :, n * 512:(n + 1) * 512])
             for n in range(2)]
    units += [(wout[n * 512:(n + 1) * 512, :], wo_h[:, 4 * n:4 * n + 4, :], wo_l[:, 4 * n:4 * n + 4, :])
              for n in range(2)]
    NU = len(units)

    def run(eng, step):
        for i in (-2, -1, 0, 1):
            step(i)
        with eng.Fori(2, NG - 2) as i:
            step(i)
        for i in (NG - 2, NG - 1, NG):
            step(i)

    def there(i):
        return not isinstance(i, int) or 0 <= i < NG

    def tiled(n):
        return not isinstance(n, int) or 0 <= n < NT

    def capped(v, most):
        return min(v, most) if isinstance(v, int) else v

    block = nc.Block()
    with block as block:
        @block.sync
        def _(sp):
            def load_weights():
                for u, (src, _, _) in enumerate(units):
                    need(sp, s["raw_low"], u - 1)
                    sp.dma_start(raw[:, u % 2, :].rearrange("p (k n) -> p k n", k=4),
                                 src.rearrange("(k p) n -> p k n", p=P)).then_inc(raw_loaded[u % 2], 16)

            def step(i):
                if isinstance(i, int) and i == -1:
                    load_weights()
                for t in range(G):
                    n = G * i + t
                    if tiled(n - 2):
                        need(sp, s["x2_made"], n - 1)
                        sp.dma_start(out_tiles[:, n - 2, :], x2[:, t % 2, :]).then_inc(x2_stored[t % 2], 16)
                    if t == 2 and there(i - 1):
                        need(sp, x2_stored[0], 32 * i)
                        need(sp, x2_stored[1], 32 * i)
                        need(sp, s["scattered"], 64 * (i - 1))
                        sp.dma_start(rows[:, :, 0:D], out_tiles[:, bass.ds(G * (i - 1), G), :])\
                            .then_inc(s["rows_loaded"], 16)
                    if there(i + 2):
                        need(sp, s["x_turned"], G * (i + 1) + t + 1)
                        sp.dma_start(xn[:, t, :], x1_tiles[:, G * (i + 2) + t, :]).then_inc(s[f"x_loaded{t}"], 16)
                    if tiled(n):
                        need(sp, s["x2_made"], n)
                        sp.dma_start(xr[:, :], x1_tiles[:, n, :]).then_inc(s["xr_loaded"], 16)
            run(sp, step)
            for par in range(2):
                sp.wait_ge(x2_stored[par], 16 * NT // 2)

        @block.gpsimd
        def _(pool):
            def power(kind, count):
                hold(pool, ln[kind]["eps"], count)
                pool.tensor_tensor(rstd[kind][:, :], var_eps[kind][:, :], minus_half[:, 0:1], ALU.pow)\
                    .then_inc(ln[kind]["rstd"], 1)

            def step(i):
                for t in range(G):
                    n = G * i + t
                    if tiled(n - 2):
                        power("y", n - 1)
                    if tiled(n - 1):
                        hold(pool, s["xr_loaded"], 16 * n)
                        pool.tensor_tensor(xr[:, :], xr[:, :], lnb_b[:, :], ALU.add).then_inc(s["xr_biased"], 1)
                    if tiled(n - 1):
                        power("w", n)
                        x2t = x2[:, (t + 1) % 2, :]
                        hold(pool, s["w_normed"], n)
                        pool.tensor_tensor(x2t, x2t, lns_b[:, :], ALU.mult).then_inc(s["w_scaled"], 1)
                        hold(pool, s["w_scaled"], n)
                        hold(pool, s["xr_biased"], n)
                        pool.tensor_tensor(x2t, x2t, xr[:, :], ALU.add).then_inc(s["x2_made"], 1)
                    if there(i + 2 if t else i + 1):
                        power("x", n + 8)
                    if t == 3 and there(i - 1):
                        hold(pool, s["routed"], i)
                        for k in range(G):
                            pool.indirect_dma_start(out=slots_dram, out_offset=bass.IndirectOffsetOnAxis(
                                ap=slot_idx[:, k:k + 1], axis=0), in_=rows[:, k, :], in_offset=None)\
                                .then_inc(s["scattered"], 16)
            run(pool, step)
            pool.wait_ge(s["scattered"], 64 * NG)

        @block.scalar
        def _(act):
            def split(u):
                act.wait_ge(raw_loaded[u % 2], 16 * (u // 2 + 1))
                act.activation(units[u][1], raw[:, u % 2, :].rearrange("p (k n) -> p k n", k=4), ACT.Copy)\
                    .then_inc(s["raw_high"], 1)

            def expo(n, t, j):
                need(act, s["s_max"], PS * n + j + 1)
                for h in range(2):
                    last = act.activation(prob[:, t % 2, j // 2, 0:L2, 2 * (j % 2) + h], s_bank[j % 2][:, h * L2:(h + 1) * L2],
                                          ACT.Exp, bias=neg_top[:, t % 2, 2 * j + h:2 * j + h + 1],
                                          accum_out=total[:, t % 2, 2 * j + h:2 * j + h + 1])
                last.then_inc(s["s_exp"], 1)

            def q_copy(i, c):
                need(act, s["q_done"], KI * i + c + 1)
                act.activation(qt[:, c, :], q_bank[:, :], ACT.Copy).then_inc(s["q_evac"], 1)

            def pt_copy(n, t, u):
                if u == 1:
                    need(act, s["o_done"], 2 * n)
                need(act, s["pt_turned"], 5 * n + u + 1)
                act.activation(pt[:, 4 * u:4 * u + 4, :],
                               pt_bank[(5 * t + u) % 2][:, :].rearrange("p (c t) -> p c t", c=4), ACT.Copy)\
                    .then_inc(s["pt_evac_act"], 1)

            def xt_copy(i, k):
                need(act, s["x_turned"], G * i + k + 1)
                act.activation(xt_h[:, :, k * P:(k + 1) * P], x_bank[:, :].rearrange("p (k t) -> p k t", k=KD),
                               ACT.Copy).then_inc(s["x_high"], 1)

            def ot_copy(n, u):
                need(act, s["ot_turned"], 2 * n + u + 1)
                act.activation(ot_h[:, 4 * u:4 * u + 4, :], x_bank[:, :].rearrange("p (c t) -> p c t", c=4), ACT.Copy)\
                    .then_inc(s["ot_high"], 1)

            def step(i):
                for t in range(G):
                    n = G * i + t
                    if isinstance(i, int) and i == -1:
                        if t < 2:
                            split(t)
                        elif t == 3:
                            act.wait_ge(s["padded"], 1)
                    if tiled(n):
                        pt_copy(n, t, 1)
                    if t < 2 and there(i + 1):
                        xt_copy(i + 1, 2 * t)
                    for j in range(PS):
                        if tiled(n + 1):
                            expo(n + 1, t + 1, j)
                        if (t, j) in QUERIES and there(i + 1):
                            q_copy(i + 1, QUERIES[t, j])
                        if (t, j) in ((2, 3), (2, 5)) and isinstance(i, int) and i == -1:
                            split(2 + j // 5)
                        if j == 1 and tiled(n):
                            pt_copy(n, t, 3)
                        if j == 2 and t < 2 and there(i + 1):
                            xt_copy(i + 1, 2 * t + 1)
                        if j == 4 and tiled(n):
                            ot_copy(n, 0)
                        if j == 6 and tiled(n):
                            ot_copy(n, 1)
                    if t == 1 and there(i - 1):
                        need(act, s["route_step"], (RS1 + RS2) * (i - 1) + 2)
                        act.activation(p_e[:, :, :], q_e[:, :, :], ACT.Exp).then_inc(s["route_exp"], 1)
            run(act, step)

        @block.vector
        def _(dve):
            dve.memset(before[:, :, :], 0.0)

            def split(u):
                dve.wait_ge(s["raw_high"], u + 1)
                dve.tensor_tensor(units[u][2], raw[:, u % 2, :].rearrange("p (k n) -> p k n", k=4),
                                  units[u][1].bitcast(F32), ALU.subtract).then_inc(s["raw_low"], 1)

            def norm_stats(kind, count, src, eps):
                dve.bn_stats(stats[kind][:, :], src).then_inc(ln[kind]["stats"], 1)
                hold(dve, ln[kind]["stats"], count)
                dve.bn_aggr(mv[kind][:, :], stats[kind][:, :]).then_inc(ln[kind]["aggr"], 1)
                need(dve, ln[kind]["aggr"], count)
                dve.tensor_scalar(var_eps[kind][:, :], mv[kind][:, 1:2], eps, None, ALU.add)\
                    .then_inc(ln[kind]["eps"], 1)

            def norm(kind, count, dst, src):
                need(dve, ln[kind]["rstd"], count)
                return dve.tensor_scalar(dst, src, mv[kind][:, 0:1], rstd[kind][:, :], ALU.subtract, ALU.mult)

            def pt_copy(n, t, u):
                need(dve, s["pt_turned"], 5 * n + u + 1)
                dve.tensor_copy(pt[:, 4 * u:4 * u + 4, :],
                                pt_bank[(5 * t + u) % 2][:, :].rearrange("p (c t) -> p c t", c=4))\
                    .then_inc(s["pt_evac"], 1)

            def xt_copy(i, k):
                need(dve, s["x_high"], G * i + k + 1)
                dve.tensor_tensor(xt_l[:, :, k * P:(k + 1) * P], x_bank[:, :].rearrange("p (k t) -> p k t", k=KD),
                                  xt_h[:, :, k * P:(k + 1) * P].bitcast(F32), ALU.subtract)\
                    .then_inc(s["x_low"], 1)

            def o_copy(n, u):
                need(dve, s["o_done"], 2 * n + u + 1)
                need(dve, s["s_recip"], n + 1)
                dve.tensor_tensor(o_sb[:, 512 * u:512 * u + 512].rearrange("p (h d) -> p h d", h=8),
                                  o_bank[:, :].rearrange("p (h d) -> p h d", h=8),
                                  recip[:, 8 * u:8 * u + 8].rearrange("p (h d) -> p h d", d=1)
                                  .to_broadcast([P, 8, D2]), ALU.mult).then_inc(s["o_evac"], 1)

            def ot_copy(n, u):
                need(dve, s["ot_high"], 2 * n + u + 1)
                dve.tensor_tensor(ot_l[:, 4 * u:4 * u + 4, :], x_bank[:, :].rearrange("p (c t) -> p c t", c=4),
                                  ot_h[:, 4 * u:4 * u + 4, :].bitcast(F32), ALU.subtract).then_inc(s["ot_low"], 1)

            def router(i, first, steps):
                for k, op in enumerate(steps):
                    if first + k:
                        need(dve, s["route_step"], (RS1 + RS2) * i + first + k)
                    op().then_inc(s["route_step"], 1)

            def b8(a):
                return a.rearrange("p (t e) -> p t e", e=1).to_broadcast([P, G, E])

            def route_experts(i):
                revb = rev[:, :].rearrange("p (t e) -> p t e", t=1).to_broadcast([P, G, E])
                need(dve, s["l_evac"], G * (i + 1))
                router(i, 0, [
                    lambda: dve.tensor_reduce(c4["top4"][:, :], logit[:, :, :], AX.X, ALU.max),
                    lambda: dve.tensor_tensor(q_e[:, :, :], logit[:, :, :], b8(c4["top4"][:, :]), ALU.subtract),
                ])
                need(dve, s["route_exp"], i + 1)
                router(i, 2, [
                    lambda: dve.tensor_reduce(c4["sum4"][:, :], p_e[:, :, :], AX.X, ALU.add),
                    lambda: dve.reciprocal(c4["rec4"][:, :], c4["sum4"][:, :]),
                    lambda: dve.tensor_tensor(p_e[:, :, :], p_e[:, :, :], b8(c4["rec4"][:, :]), ALU.mult),
                    lambda: dve.tensor_reduce(c4["gate4"][:, :], p_e[:, :, :], AX.X, ALU.max),
                    lambda: dve.tensor_tensor(q_e[:, :, :], p_e[:, :, :], b8(c4["gate4"][:, :]), ALU.is_ge),
                    lambda: dve.tensor_tensor(q_e[:, :, :], q_e[:, :, :], revb, ALU.mult),
                    lambda: dve.tensor_reduce(c4["rank4"][:, :], q_e[:, :, :], AX.X, ALU.max),
                    lambda: dve.tensor_tensor(onehot[:, :, :], revb, b8(c4["rank4"][:, :]), ALU.is_equal),
                ])

            def route_slots(i):
                need(dve, s["counted"], i + 1)
                need(dve, s["scattered"], 64 * i)
                cum = q_bank[:, 64:64 + G * E].rearrange("p (t e) -> p t e", t=G)
                tot = q_bank[:, 128:128 + G * E].rearrange("p (t e) -> p t e", t=G)
                pos, keep, slot = c4["pos4"][:, :], c4["keep4"][:, :], c4["slot4"][:, :]
                spare = token_f[:, bass.ds(G * i, G)]
                steps = [lambda k=k: dve.tensor_tensor(before[:, k + 1, :], before[:, k, :], tot[:, k, :], ALU.add)
                         for k in range(G)]
                steps += [
                    lambda: dve.tensor_tensor(q_e[:, :, :], cum, before[:, 0:G, :], ALU.add),
                    lambda: dve.tensor_tensor(q_e[:, :, :], q_e[:, :, :], onehot[:, :, :], ALU.mult),
                    lambda: dve.tensor_reduce(pos, q_e[:, :, :], AX.X, ALU.add),
                    lambda: dve.tensor_scalar(keep, pos, float(CAP), None, ALU.is_lt),
                    lambda: dve.tensor_scalar(slot, c4["rank4"][:, :], -float(CAP), float(CAP * E - T), ALU.mult,
                                              ALU.add),
                    lambda: dve.tensor_tensor(slot, slot, pos, ALU.add),
                    lambda: dve.tensor_tensor(slot, slot, spare, ALU.subtract),
                    lambda: dve.tensor_tensor(slot, slot, keep, ALU.mult),
                    lambda: dve.tensor_copy(before[:, 0, :], before[:, G, :]),
                ]
                assert len(steps) == RS2
                router(i, RS1, steps)
                need(dve, s["route_step"], (RS1 + RS2) * (i + 1))
                dve.scalar_tensor_tensor(slot_idx[:, :], slot, float(T), spare, ALU.add, ALU.add)
                need(dve, s["rows_loaded"], 16 * (i + 1))
                dve.tensor_copy(rows[:, :, D:D + 1], c4["gate4"][:, :].rearrange("p (t a) -> p t a", a=1))
                dve.tensor_scalar(rows[:, :, D + 1:D + 2].bitcast(I32),
                                  token_int[:, bass.ds(G * i, G)].rearrange("p (t a) -> p t a", a=1), 0, None,
                                  ALU.add).then_inc(s["routed"], 1)

            def step(i):
                for t in range(G):
                    n = G * i + t
                    if isinstance(i, int) and i == -1:
                        if t < 2:
                            split(t)
                        elif t == 2:
                            split(2)
                            split(3)
                            dve.wait_ge(s["raw_low"], NU)
                            dve.memset(prob[:, :, :, L2:PW, :], 0.0).then_inc(s["padded"], 1)

                    def top(j):
                        if tiled(n + 1):
                            need(dve, s["s_done"], PS * (n + 1) + j + 1)
                            dve.tensor_reduce(neg_top[:, (t + 1) % 2, 2 * j:2 * j + 2],
                                              s_bank[j % 2][:, 0:2 * L2].rearrange("p (h k) -> p h k", h=2), AX.X,
                                              ALU.max, negate=True).then_inc(s["s_max"], 1)

                    if tiled(n):
                        need(dve, s["s_exp"], PS * (n + 1))
                        need(dve, s["o_evac"], 2 * n)
                        dve.reciprocal(recip[:, :], total[:, t % 2, :]).then_inc(s["s_recip"], 1)
                        pt_copy(n, t, 0)
                    if t < 2 and there(i + 1):
                        xt_copy(i + 1, 2 * t)
                    top(0)
                    if tiled(n - 2):
                        need(dve, s["x2_made"], n - 1)
                        norm_stats("y", n - 1, x2[:, t % 2, :], EPS1)
                    if tiled(n - 2):
                        need(dve, s["y_turned"], n - 2)
                        norm("y", n - 1, y[:, :], x2[:, t % 2, :]).then_inc(s["y_normed"], 1)
                    if tiled(n):
                        pt_copy(n, t, 2)
                    top(1)
                    if tiled(n - 1):
                        need(dve, s["w_done"], n)
                        norm_stats("w", n, w_bank[:, :], EPS2)
                    top(2)
                    if t < 2 and there(i + 1):
                        xt_copy(i + 1, 2 * t + 1)
                    if tiled(n):
                        pt_copy(n, t, 4)
                        o_copy(n, 0)
                    top(3)
                    if tiled(n - 2):
                        need(dve, s["y_turned"], n - 1)
                        need(dve, s["l_done"], n - 2)
                        dve.tensor_copy(yt[:, :, :], x_bank[:, :].rearrange("p (c t) -> p c t", c=KD))\
                            .then_inc(s["y_evac"], 1)
                    if tiled(n - 1):
                        need(dve, x2_stored[(t + 1) % 2], 16 * (2 * i + (t - 3) // 2 + 1))
                        norm("w", n, x2[:, (t + 1) % 2, :], w_bank[:, :]).then_inc(s["w_normed"], 1)
                    top(4)
                    if tiled(n):
                        ot_copy(n, 0)
                        o_copy(n, 1)
                    top(5)
                    m, k = n + 7, (t + 3) % G
                    if there(i + 2 if t else i + 1):
                        need(dve, s[f"x_loaded{k}"], 16 * ((i + 2 if t else i + 1) + 1))
                        norm_stats("x", m + 1, xn[:, k, :], EPS1)
                    if tiled(n - 2):
                        need(dve, s["l_done"], n - 1)
                        dve.tensor_tensor(logit[:, (t + 2) % 4, :], w_bank[:, 0:E], br_b[:, :], ALU.add)\
                            .then_inc(s["l_evac"], 1)
                    top(6)
                    if there(i + 2 if t else i + 1):
                        norm("x", m + 1, xn[:, k, :], xn[:, k, :]).then_inc(s["x_normed"], 1)
                    top(7)
                    if tiled(n):
                        ot_copy(n, 1)
                    if t == 1 and there(i - 1):
                        route_experts(i - 1)
                    if t == 2 and there(i - 1):
                        route_slots(i - 1)
            run(dve, step)

        @block.tensor
        def _(pe):
            def turn_p(n, t, u):
                if u < 2:
                    need(pe, s["s_exp"], PS * (n + 1))
                evac, value = ((s["pt_evac_act"], 2 * n), (s["pt_evac"], 3 * n), (s["pt_evac"], 3 * n + 1),
                               (s["pt_evac_act"], 2 * n + 1), (s["pt_evac"], 3 * n + 2))[u]
                need(pe, evac, value)
                for k in range(4):
                    src = prob[:, t % 2, k, P:PW, :].rearrange("p k h -> p (k h)") if u == 0 else \
                        prob[:, t % 2, u - 1, 0:P, k]
                    last = pe.transpose(pt_bank[(5 * t + u) % 2][:, k * P:(k + 1) * P], src, ident[:, :])
                last.then_inc(s["pt_turned"], 1)

            def scores(n, t, b, j):
                need(pe, s["s_exp"], PS * n + j - 1)
                if t % G == 0:
                    need(pe, s["q_evac"], 2 * n + j + 1)
                pe.matmul(s_bank[j % 2][:, 0:2 * L2], qt[:, j, (t % G) * P:(t % G + 1) * P],
                          k2[:, bass.ds(b, 1), j, :, :].rearrange("p a h k -> p (a h k)"), start=True, stop=True)\
                    .then_inc(s["s_done"], 1)

            def values(n, b, g):
                need(pe, s["pt_evac"], 3 * n + 1)
                evac, value = ((s["pt_evac_act"], 2 * n + 1), (s["pt_evac"], 3 * n + 2),
                               (s["pt_evac_act"], 2 * n + 2), (s["pt_evac"], 3 * n + 3))[g]
                need(pe, evac, value)
                if g % 2 == 0:
                    need(pe, s["o_evac"], 2 * n + g // 2)
                o = (g % 2) * 256
                pe.matmul(o_bank[:, o:o + 256], pt[:, g, :], v2_rest[:, bass.ds(b, 1), g, :]
                          .rearrange("p a n -> p (a n)"), start=True, stop=False)
                for h in range(4):
                    last = pe.matmul(o_bank[:, o + h * D2:o + (h + 1) * D2], pt[:, 4 + 4 * g + h, :],
                                     v2_main[:, bass.ds(b, 1), (4 * g + h) * D2:(4 * g + h + 1) * D2]
                                     .rearrange("p a n -> p (a n)"), start=False, stop=h == 3)
                if g % 2:
                    last.then_inc(s["o_done"], 1)

            def queries(i, c):
                need(pe, s["x_low"], G * (i + 1))
                if isinstance(i, int) and i == 0:
                    need(pe, s["raw_low"], 1 + c // 4)
                need(pe, s["q_evac"], KI * i + c)
                if c >= 4:
                    need(pe, s["route_step"], (RS1 + RS2) * (i - 2) + RS1 + COUNTS)
                for k in range(KD):
                    last = product(pe, q_bank[:, :], [a[:, k, c * P:(c + 1) * P] for a in (wq_h, wq_l)],
                                   [a[:, k, :] for a in (xt_h, xt_l)], k == 0, k == KD - 1)
                last.then_inc(s["q_done"], 1)

            def output(n, half):
                need(pe, s["ot_low"], 2 * n + half + 1)
                if isinstance(n, int) and n == 0:
                    need(pe, s["raw_low"], NU)
                if half == 0:
                    need(pe, s["w_normed"], n)
                    need(pe, s["l_evac"], n - 1)
                for c in range(4 * half, 4 * half + 4):
                    last = product(pe, w_bank[:, :], [a[:, c, :] for a in (ot_h, ot_l)],
                                   [a[:, c, :] for a in (wo_h, wo_l)], c == 0, c == KI - 1)
                if half:
                    last.then_inc(s["w_done"], 1)

            def turn_o(n, u):
                need(pe, s["o_evac"], 2 * n + u + 1)
                for k in range(4):
                    last = pe.transpose(x_bank[:, k * P:(k + 1) * P], o_sb[:, (4 * u + k) * P:(4 * u + k + 1) * P],
                                        ident[:, :])
                last.then_inc(s["ot_turned"], 1)

            def batch(i):
                if isinstance(i, int):
                    return i // G
                return nc.s_assert_within(i >> 2, 0, B - 1, skip_runtime_bounds_check_because="groups end at NG - 1")

            def step(i):
                for t in range(G):
                    n = G * i + t
                    b = batch(i)
                    bn = b if t < 3 else batch(i + 1)

                    def sc(j):
                        if tiled(n + 1):
                            scores(n + 1, t + 1, bn, j)
                        if (t, j) in QUERIES and there(i + 1):
                            queries(i + 1, QUERIES[t, j])

                    def turn_x(k):
                        if t < 2 and there(i + 1):
                            need(pe, s["x_normed"], G * (i + 1) + k + 1)
                            need(pe, s["x_low"], G * (i + 1) + k)
                            need(pe, s["ot_low"], 2 * n)
                            need(pe, s["y_evac"], n - 2)
                            for c in range(KD):
                                last = pe.transpose(x_bank[:, c * P:(c + 1) * P], xn[:, k, c * P:(c + 1) * P],
                                                    ident[:, :])
                            last.then_inc(s["x_turned"], 1)

                    def x_read():
                        if there(i + 1):
                            need(pe, s["x_low"], G * (i + 1) + (2 * t + 2 if t < 2 else G))

                    if tiled(n - 1):
                        output(n - 1, 0)
                    if tiled(n):
                        turn_p(n, t, 0)
                        turn_p(n, t, 1)
                    turn_x(2 * t)
                    sc(0)
                    if tiled(n - 1):
                        output(n - 1, 1)
                    if tiled(n):
                        turn_p(n, t, 2)
                    sc(1)
                    if tiled(n):
                        turn_p(n, t, 3)
                        values(n, b, 0)
                    sc(2)
                    turn_x(2 * t + 1)
                    if tiled(n):
                        turn_p(n, t, 4)
                        values(n, b, 1)
                    sc(3)
                    if tiled(n - 2):
                        need(pe, s["y_normed"], n - 1)
                        need(pe, s["ot_low"], capped(2 * n, 2 * NT))
                        x_read()
                        for k in range(KD):
                            last = pe.transpose(x_bank[:, k * P:(k + 1) * P], y[:, k * P:(k + 1) * P], ident[:, :])
                        last.then_inc(s["y_turned"], 1)
                    if tiled(n):
                        values(n, b, 2)
                    sc(4)
                    if tiled(n):
                        need(pe, s["y_evac"], n - 1)
                        x_read()
                        turn_o(n, 0)
                        values(n, b, 3)
                    sc(5)
                    if tiled(n - 2):
                        need(pe, s["y_evac"], n - 1)
                        need(pe, s["w_normed"], capped(n, NT))
                        for k in range(KD):
                            last = pe.matmul(w_bank[:, 0:E], yt[:, k, :], wr_sb[:, k, :], start=k == 0,
                                             stop=k == KD - 1)
                        last.then_inc(s["l_done"], 1)
                    sc(6)
                    if tiled(n):
                        need(pe, s["ot_low"], 2 * n + 1)
                        x_read()
                        turn_o(n, 1)
                    sc(7)
                    if t == 2 and there(i - 1):
                        need(pe, s["route_step"], (RS1 + RS2) * (i - 1) + RS1)
                        need(pe, s["q_evac"], capped(KI * (i + 1) + 4, KI * NG))
                        oh = onehot[:, :, :].rearrange("p t e -> p (t e)")
                        pe.matmul(q_bank[:, 64:64 + G * E], upper[:, :], oh, start=True, stop=True)
                        pe.matmul(q_bank[:, 128:128 + G * E], ones[:, :], oh, start=True, stop=True)\
                            .then_inc(s["counted"], 1)
            run(pe, step)


def experts(nc, sem, sb, bank, slot_tiles, out_rows, w1, b1, w2, b2, ident, minus_half):
    raw = sb("c_raw", [P, 2, 2048])
    w_h = sb("c_w_h", [P, 2, 2, KD, D], F32R)
    w_l = sb("c_w_l", [P, 2, 2, KD, D], F32R)
    b1_col = sb("c_b1", [P, 2, KD])
    b2_b = sb("c_b2", [P, 2, D])
    rows = sb("c_rows", [P, 2, G, ROW])
    gate, token = sb("c_gate", [P, 2, G]), sb("c_token", [P, 2, G], I32)
    y = sb("c_y", [P, G, D])
    base = sb("c_base", [P, 2, G, D])
    xt_h, xt_l = sb("c_xt_h", [P, KD, G * P], F32R), sb("c_xt_l", [P, KD, G * P], F32R)
    h = sb("c_h", [P, 2, G * P])
    ht_h, ht_l = sb("c_ht_h", [P, KD, G * P], F32R), sb("c_ht_l", [P, KD, G * P], F32R)
    res = sb("c_res", [P, G, D])
    stats, mv = sb("c_stats", [P, G, 6]), sb("c_mv", [P, G, 2])
    var_eps, rstd, gain = sb("c_var", [P, G]), sb("c_rstd", [P, G]), sb("c_gain", [P, G])

    names = ("w_loaded0 w_loaded1 w_high w_low b_loaded0 b_loaded1 rows_loaded0 rows_loaded1 stats_done aggr_done "
             "eps_done rstd_done gain_done normed scaled based tails x_turned x_high x_low h_done h_relu h_high h_low "
             "o_done res_made scattered0 scattered1 scattered2 scattered3").split()
    s = {n: sem("c_" + n) for n in names}
    h_bank, x_bank, o_bank = bank[0:2], bank[2:4], bank[4:6]

    def run(eng, prepare, work):
        def pair(p, last):
            for k in range(2):
                work(2 * p + k, k, not (last and k))
        prepare(0, 0)
        pair(0, False)
        with eng.Fori(1, E // 2 - 1) as p:
            pair(p, False)
        pair(E // 2 - 1, True)

    def times(e, par):
        return (e - par) // 2 if isinstance(e, int) else (e - par) >> 1

    block = nc.Block()
    with block as block:
        @block.sync
        def _(sp):
            def load(e, par):
                need(sp, s["based"], G * (e - 1))
                need(sp, s["normed"], G * (e - 1))
                need(sp, s["tails"], e - 1)
                sp.dma_start(rows[:, par, :, :], slot_tiles[:, bass.ds(G * e, G), :])\
                    .then_inc(s[f"rows_loaded{par}"], 16)
                for m, w in enumerate((w1, w2)):
                    need(sp, s["w_low"], 2 * e + m - 1)
                    sp.dma_start(raw[:, m, :].rearrange("p (k n) -> p k n", k=KD),
                                 w[bass.ds(e, 1), :, :].rearrange("a (k p) n -> p (a k) n", p=P))\
                        .then_inc(s[f"w_loaded{m}"], 16)
                need(sp, s["h_relu"], KD * (e - 1))
                need(sp, s["scaled"], G * (e - 1))
                with nc.allow_non_contiguous_dma(reason="a bias by column"):
                    sp.dma_start(b1_col[:, par, :], b1[bass.ds(e, 1), :].rearrange("a (c p) -> p (a c)", p=P))\
                        .then_inc(s[f"b_loaded{par}"], 16)
                sp.dma_start(b2_b[:, par, :], b2[bass.ds(e, 1), :].to_broadcast([P, D]))\
                    .then_inc(s[f"b_loaded{par}"], 16)

            def work(e, par, more):
                if more:
                    load(e + 1, 1 - par)
            run(sp, load, work)

        @block.gpsimd
        def _(pool):
            def prepare(e, par):
                hold(pool, s["eps_done"], e + 1)
                pool.tensor_tensor(rstd[:, :], var_eps[:, :], minus_half[:, :], ALU.pow).then_inc(s["rstd_done"], 1)
                for k in range(G):
                    hold(pool, s["scaled"], G * e + k + 1)
                    pool.tensor_tensor(base[:, par, k, :], base[:, par, k, :], rows[:, par, k, 0:D], ALU.add)\
                        .then_inc(s["based"], 1)

            def work(e, par, more):
                if more:
                    prepare(e + 1, 1 - par)
                for k in range(G):
                    hold(pool, s["res_made"], G * e + k + 1)
                    pool.indirect_dma_start(
                        out=out_rows, out_offset=bass.IndirectOffsetOnAxis(ap=token[:, par, k:k + 1], axis=0),
                        in_=res[:, k, :], in_offset=None, bounds_check=T - 1, oob_is_err=False)\
                        .then_inc(s[f"scattered{k}"], 16)
            run(pool, prepare, work)
            for k in range(G):
                pool.wait_ge(s[f"scattered{k}"], 16 * E)

        @block.scalar
        def _(act):
            def weights(e, par, m):
                need(act, s[f"w_loaded{m}"], 16 * (e + 1))
                act.activation(w_h[:, par, m, :, :], raw[:, m, :].rearrange("p (k n) -> p k n", k=KD), ACT.Copy)\
                    .then_inc(s["w_high"], 1)

            def scale_bias(e, par):
                hold(act, s[f"rows_loaded{par}"], 16 * (times(e, par) + 1))
                hold(act, s[f"b_loaded{par}"], 32 * (times(e, par) + 1))
                hold(act, s["res_made"], G * (e - 1))
                for k in range(G):
                    act.activation(base[:, par, k, :], b2_b[:, par, :], ACT.Copy, scale=rows[:, par, k, D:D + 1])\
                        .then_inc(s["scaled"], 1)

            def xt_copy(e, k):
                need(act, s["x_turned"], G * e + k + 1)
                act.activation(xt_h[:, :, k * P:(k + 1) * P],
                               x_bank[k % 2][:, :].rearrange("p (k t) -> p k t", k=KD), ACT.Copy)\
                    .then_inc(s["x_high"], 1)

            def prepare(e, par):
                weights(e, par, 0)
                for k in range(G):
                    xt_copy(e, k)
                weights(e, par, 1)
                scale_bias(e, par)

            def work(e, par, more):
                hold(act, s[f"b_loaded{par}"], 32 * (times(e, par) + 1))
                for c in range(KD):
                    need(act, s["h_done"], KD * e + c + 1)
                    need(act, s["h_low"], KD * e + c - 1)
                    act.activation(h[:, c % 2, :], h_bank[c % 2][:, :], ACT.Relu, bias=b1_col[:, par, c:c + 1])\
                        .then_inc(s["h_relu"], 1)
                    need(act, s["h_relu"], KD * e + c + 1)
                    act.activation(ht_h[:, c, :], h[:, c % 2, :], ACT.Copy).then_inc(s["h_high"], 1)
                    if c == 1 and more:
                        weights(e + 1, 1 - par, 0)
                if more:
                    scale_bias(e + 1, 1 - par)
                    for k in range(G):
                        xt_copy(e + 1, k)
                    weights(e + 1, 1 - par, 1)
            run(act, prepare, work)

        @block.vector
        def _(dve):
            def row_stats(e, par):
                need(dve, s[f"rows_loaded{par}"], 16 * (times(e, par) + 1))
                for k in range(G):
                    last = dve.bn_stats(stats[:, k, :], rows[:, par, k, 0:D])
                last.then_inc(s["stats_done"], 1)
                hold(dve, s["stats_done"], e + 1)
                for k in range(G):
                    last = dve.bn_aggr(mv[:, k, :], stats[:, k, :])
                last.then_inc(s["aggr_done"], 1)
                need(dve, s["aggr_done"], e + 1)
                dve.tensor_scalar(var_eps[:, :], mv[:, :, 1], EPS1, None, ALU.add).then_inc(s["eps_done"], 1)

            def norm(e, par):
                need(dve, s["rstd_done"], e + 1)
                dve.tensor_tensor(gain[:, :], rstd[:, :], rows[:, par, :, D], ALU.mult).then_inc(s["gain_done"], 1)
                need(dve, s["gain_done"], e + 1)
                need(dve, s["x_turned"], G * e)
                for k in range(G):
                    dve.tensor_scalar(y[:, k, :], rows[:, par, k, 0:D], mv[:, k, 0:1], gain[:, k:k + 1],
                                      ALU.subtract, ALU.mult).then_inc(s["normed"], 1)

            def weights(e, par, m):
                need(dve, s["w_high"], 2 * e + m + 1)
                dve.tensor_tensor(w_l[:, par, m, :, :], raw[:, m, :].rearrange("p (k n) -> p k n", k=KD),
                                  w_h[:, par, m, :, :].bitcast(F32), ALU.subtract).then_inc(s["w_low"], 1)

            def tail(e, par):
                for k in range(G):
                    hold(dve, s[f"scattered{k}"], 16 * (e - 1))
                dve.tensor_copy(gate[:, par, :], rows[:, par, :, D])
                dve.tensor_scalar(token[:, par, :], rows[:, par, :, D + 1].bitcast(I32), 0, None, ALU.add)\
                    .then_inc(s["tails"], 1)

            def xt_copy(e, k):
                need(dve, s["x_high"], G * e + k + 1)
                dve.tensor_tensor(xt_l[:, :, k * P:(k + 1) * P],
                                  x_bank[k % 2][:, :].rearrange("p (k t) -> p k t", k=KD),
                                  xt_h[:, :, k * P:(k + 1) * P].bitcast(F32), ALU.subtract)\
                    .then_inc(s["x_low"], 1)

            def prepare(e, par):
                row_stats(e, par)
                norm(e, par)
                weights(e, par, 0)
                for k in range(G):
                    xt_copy(e, k)
                tail(e, par)
                weights(e, par, 1)

            def h_low(e, c):
                need(dve, s["h_high"], KD * e + c + 1)
                dve.tensor_tensor(ht_l[:, c, :], h[:, c % 2, :], ht_h[:, c, :].bitcast(F32), ALU.subtract)\
                    .then_inc(s["h_low"], 1)

            def finish(e, par, k):
                need(dve, s["o_done"], G * e + k + 1)
                need(dve, s["based"], G * e + k + 1)
                need(dve, s["tails"], e + 1)
                need(dve, s[f"scattered{k}"], 16 * e)
                dve.scalar_tensor_tensor(res[:, k, :], o_bank[k % 2][:, :], gate[:, par, k:k + 1],
                                         base[:, par, k, :], ALU.mult, ALU.add).then_inc(s["res_made"], 1)

            def work(e, par, more):
                if more:
                    row_stats(e + 1, 1 - par)
                h_low(e, 0)
                h_low(e, 1)
                if more:
                    norm(e + 1, 1 - par)
                h_low(e, 2)
                if more:
                    weights(e + 1, 1 - par, 0)
                h_low(e, 3)
                if more:
                    tail(e + 1, 1 - par)
                for k in range(G):
                    finish(e, par, k)
                    if more:
                        for n in ((0, 1), (2,), (3,), ())[k]:
                            xt_copy(e + 1, n)
                if more:
                    weights(e + 1, 1 - par, 1)
            run(dve, prepare, work)

        @block.tensor
        def _(pe):
            def turn(e, k):
                need(pe, s["normed"], G * e + k + 1)
                need(pe, s["x_low"], G * e + k - 1)
                for c in range(KD):
                    last = pe.transpose(x_bank[k % 2][:, c * P:(c + 1) * P], y[:, k, c * P:(c + 1) * P], ident[:, :])
                last.then_inc(s["x_turned"], 1)

            def prepare(e, par):
                for k in range(G):
                    turn(e, k)

            def work(e, par, more):
                need(pe, s["w_low"], 2 * e + 1)
                need(pe, s["x_low"], G * (e + 1))
                for c in range(KD):
                    need(pe, s["h_relu"], KD * e + c - 1)
                    for k in range(KD):
                        last = product(pe, h_bank[c % 2][:, :],
                                       [a[:, par, 0, k, c * P:(c + 1) * P] for a in (w_h, w_l)],
                                       [a[:, k, :] for a in (xt_h, xt_l)], k == 0, k == KD - 1)
                    last.then_inc(s["h_done"], 1)
                need(pe, s["w_low"], 2 * e + 2)
                for k in range(G):
                    need(pe, s["res_made"], G * e + k - 1)
                    for c in range(KD):
                        if k == 0:
                            need(pe, s["h_low"], KD * e + c + 1)
                        last = product(pe, o_bank[k % 2][:, :], [a[:, c, k * P:(k + 1) * P] for a in (ht_h, ht_l)],
                                       [a[:, par, 1, c, :] for a in (w_h, w_l)], c == 0, c == KD - 1)
                    last.then_inc(s["o_done"], 1)
                    if more:
                        for n in ((0, 1), (2,), (3,), ())[k]:
                            turn(e + 1, n)
            run(pe, prepare, work)


_INS = ['x', 'ctx_2048', 'L0_attn_Wqkv', 'L0_attn_bqkv', 'L0_attn_Wproj', 'L0_attn_bproj', 'L0_attn_mapping',
        'L0_xattn_Wq', 'L0_xattn_Wkv', 'L0_xattn_null_kv', 'L0_xattn_Wout', 'L0_xattn_ln_scale', 'L0_xattn_ln_bias',
        'L0_ffn_Wr', 'L0_ffn_br', 'L0_ffn_W1', 'L0_ffn_b1', 'L0_ffn_W2', 'L0_ffn_b2']


def kernel(**inputs):
    import numpy as _np
    import concourse.bacc as _bacc
    from concourse import mybir as _mybir
    from concourse.bass_utils import run_bass_kernel_spmd as _run

    nc = _bacc.Bacc("TRN2", target_bir_lowering=False, num_devices=1)
    arrays, args = {}, []
    for name in _INS:
        a = _np.ascontiguousarray(inputs[name])
        arrays[f"in_{name}_dram"] = a
        args.append(nc.dram_tensor(f"in_{name}_dram", a.shape, _mybir.dt.from_np(a.dtype), kind="ExternalInput").ap())
    args.append(nc.dram_tensor("out_0_dram", (B, M, D), F32, kind="ExternalOutput").ap())
    decoder_kernel(nc, *args)
    r = _run(nc, [arrays], core_ids=[0])
    return r.results[0]["out_0_dram"]
```

```python
import concourse.bass as bass
from concourse import mybir
from concourse.alu_op_type import AluOpType as ALU
from contextlib import ExitStack

F32 = mybir.dt.float32
F32R = mybir.dt.float32r
I32 = mybir.dt.int32
ACT = mybir.ActivationFunctionType
AX = mybir.AxisListType

P = 128
B, M, D = 2, 2048, 512
T = B * M
NT = T // P
G = 4
NG = NT // G
KD = D // P
H1, D1, SEG, DIL, BLK = 16, 32, 128, 4, 64
NSEG = M // SEG
NKEY = SEG // DIL
SCALE1 = float(D1) ** -0.5
EPS_SUM = 1e-6
EPS1 = 1e-5
H2, D2, CTX, LC = 16, 64, 1024, 154
KC = CTX // P
REM = LC - P
L2 = LC + 1
PW = 160
INNER = H2 * D2
KI = INNER // P
SCALE2 = float(D2) ** -0.5
EPS2 = 1e-6
E = 8
CAP = T // E
ROW = D + 2
NOBODY = 2 * T


def need(eng, sem, value):
    if not isinstance(value, int) or value > 0:
        eng.wait_ge(sem, value)


def hold(eng, sem, value):
    if not isinstance(value, int) or value > 0:
        eng.wait_ge(sem, value)
        eng.nop(nofuse=True)


def product(pe, out, lhs, rhs, first, last):
    (lh, ll), (rh, rl) = lhs, rhs
    pe.matmul(out, lh, rh, start=first, stop=False)
    pe.matmul(out, lh, rl, start=False, stop=False)
    return pe.matmul(out, ll, rh, start=False, stop=last)


def decoder_kernel(nc, x, ctx, wqkv, bqkv, wproj, bproj, mapping, wq2, wkv2, null_kv, wout, ln_scale, ln_bias,
                   wr, br, w1, b1, w2, b2, out):
    x_rows = x.rearrange("b t d -> (b t) d")
    x_tiles = x_rows.rearrange("(n p) d -> p n d", p=P)
    out_rows = out.rearrange("b t d -> (b t) d")
    out_tiles = out_rows.rearrange("(n p) d -> p n d", p=P)
    x1_dram = nc.dram_tensor("x1_scratch", (T, D), F32, kind="Internal").ap()
    x1_tiles = x1_dram.rearrange("(n p) d -> p n d", p=P)
    slots_dram = nc.dram_tensor("slot_rows", (2 * T, ROW), F32, kind="Internal").ap()
    slot_tiles = slots_dram.rearrange("(n p) d -> p n d", p=P)

    with ExitStack() as keep:
        def sb(name, shape, dt=F32, stack=keep):
            return stack.enter_context(nc.sbuf_tensor(name, shape, dt))

        taken = []

        def sem(name):
            taken.append(nc.alloc_semaphore(name=name))
            return taken[-1]

        def release_sems():
            nc.clear_and_free_semaphores(taken)
            nc.all_engine_barrier()
            taken.clear()

        bank = [keep.enter_context(nc.psum_tensor(f"bank{n}", [P, 512], F32)) for n in range(8)]

        ident = sb("ident", [P, P])
        upper = sb("upper", [P, P])
        ones = sb("ones", [P, P])
        head_mask = sb("head_mask", [P, 4])
        minus_half = sb("minus_half", [P, 4])
        rev = sb("rev", [P, E])
        token_int = sb("token_int", [P, NT], I32)
        token_f = sb("token_f", [P, NT])
        lns_b = sb("lns_b", [P, D])
        lnb_b = sb("lnb_b", [P, D])
        br_b = sb("br_b", [P, E])
        wr_sb = sb("wr_sb", [P, KD, E])
        keys_values = ExitStack()
        k2 = sb("k2", [P, B, KI, 2, L2], F32, keys_values)
        v2_main = sb("v2_main", [P, B, INNER], F32, keys_values)
        v2_rest = sb("v2_rest", [P, B, 4, 4 * D2], F32, keys_values)

        stage_a = ExitStack()
        with stage_a:
            wq_h = sb("wq_h", [P, KD, D], F32R, stage_a)
            wq_l = sb("wq_l", [P, KD, D], F32R, stage_a)
            wp_h = sb("wp_h", [P, KD, D], F32R, stage_a)
            wp_l = sb("wp_l", [P, KD, D], F32R, stage_a)
            bproj_b = sb("bproj_b", [P, D], F32, stage_a)
            bq_col = sb("bq_col", [P, KD], F32, stage_a)
            k1 = sb("k1", [P, KD, B * NSEG, NKEY], F32, stage_a)
            v1 = sb("v1", [P, B * NSEG, KD * D1], F32, stage_a)
            idx_all = sb("idx_all", [P, NT], I32, stage_a)
            head_pick = sb("head_pick", [P, 32], F32, stage_a)
            head_spread = sb("head_spread", [P, KD, P], F32R, stage_a)
            seg_tab = sb("seg_tab", [1, T // BLK], I32, stage_a)
            with ExitStack() as st:
                setup(nc, sem, lambda *a: sb(*a, stack=st), bank, x_rows, ctx, wqkv, bqkv, wproj, bproj, mapping, wkv2,
                      null_kv, ln_scale, ln_bias, wr, br, slot_tiles, ident, upper, ones, head_mask, minus_half, rev,
                      token_int, token_f, bproj_b, lns_b, lnb_b, br_b, wr_sb, k2, v2_main, v2_rest,
                      wq_h, wq_l, wp_h, wp_l, bq_col, k1, v1, idx_all, head_pick, head_spread, seg_tab)
            release_sems()
            with ExitStack() as st:
                self_attention(nc, sem, lambda *a: sb(*a, stack=st), bank, x_rows, x_tiles, x1_tiles, ident, head_mask,
                               minus_half, bproj_b, wq_h, wq_l, wp_h, wp_l, bq_col, k1, v1, idx_all, head_pick,
                               head_spread, seg_tab)
        release_sems()
        with ExitStack() as st:
            cross_attention(nc, sem, lambda *a: sb(*a, stack=st), bank, x1_tiles, out_tiles, slots_dram, wq2, wout,
                            ident, upper, ones, minus_half, rev, token_int, token_f, lns_b, lnb_b, br_b, wr_sb, k2,
                            v2_main, v2_rest)
        keys_values.close()
        release_sems()
        with ExitStack() as st:
            experts(nc, sem, lambda *a: sb(*a, stack=st), bank, slot_tiles, out_rows, w1, b1, w2, b2, ident,
                    minus_half)


def setup(nc, sem, sb, bank, x_rows, ctx, wqkv, bqkv, wproj, bproj, mapping, wkv2, null_kv, ln_scale, ln_bias, wr, br,
          slot_tiles, ident, upper, ones, head_mask, minus_half, rev, token_int, token_f, bproj_b, lns_b, lnb_b, br_b,
          wr_sb, k2, v2_main, v2_rest, wq_h, wq_l, wp_h, wp_l, bq_col, k1, v1, idx_all, head_pick, head_spread,
          seg_tab):
    CB = 256
    NC = 2 * INNER // CB
    KB, HB = NC // 2, CB // P
    raw = sb("raw", [P, 2, 2048])
    wc_h = sb("wc_h", [P, 2, 8, CB], F32R)
    wc_l = sb("wc_l", [P, 2, 8, CB], F32R)
    ctx_sb = sb("ctx_sb", [P, 3, CTX])
    ct_h = sb("ct_h", [P, KC, 3 * P], F32R)
    ct_l = sb("ct_l", [P, KC, 3 * P], F32R)
    xk = ctx_sb[:, 0:2, :].rearrange("p a (b d) -> p (a b) d", d=D)
    xkt = [(wp_h[:, :, :], wp_l[:, :, :]),
           tuple(a[:, :, :].rearrange("p k t -> p (k t)")[:, 0:KD * 512].rearrange("p (k t) -> p k t", k=KD)
                 for a in (ct_h, ct_l))]
    v_tmp = sb("v_tmp", [P, 2, D])
    v_last = v_tmp[:, :, :].rearrange("p a d -> p (a d)")
    bk_col = sb("bk_col", [P, KD])
    bv_b = sb("bv_b", [P, D])
    null_k = sb("null_k", [P, 1])
    map_raw = sb("map_raw", [P, NT], I32)
    kmap = sb("kmap", [P, 4], I32)
    kidx = sb("kidx", [P, B, 4], I32)
    seg_raw = sb("seg_raw", [1, T // BLK], I32)
    empty_row = sb("empty_row", [P, ROW])
    stats = sb("stats", [P, 4, 6])
    mv = sb("mv", [P, 4, 2])
    var_eps = sb("var_eps", [P, 4])
    rstd = sb("rstd", [P, 4])

    maps_loaded, biases_loaded = sem("maps_loaded"), sem("biases_loaded")
    ctx_loaded = [sem("ctx_loaded0"), sem("ctx_loaded1"), sem("ctx_loaded_rest")]
    raw_loaded = [sem("raw_loaded0"), sem("raw_loaded1")]
    raw_high, raw_low = sem("raw_high"), sem("raw_low")
    keys_zeroed, spread_made = sem("keys_zeroed"), sem("spread_made")
    zeroed, masks, tables = sem("zeroed"), sem("masks"), sem("tables")
    ctx_zeroed, null_k_loaded, null_v_loaded = sem("ctx_zeroed"), sem("null_k_loaded"), sem("null_v_loaded")
    prefilled, empty_made, rest_placed = sem("prefilled"), sem("empty_made"), sem("rest_placed")
    turned, turned_high, turned_low = sem("turned"), sem("turned_high"), sem("turned_low")
    kv_done, block_done, kv_evac = sem("kv_done"), sem("block_done"), sem("kv_evac")
    xk_loaded, xk_stats, xk_aggr, xk_eps = sem("xk_loaded"), sem("xk_stats"), sem("xk_aggr"), sem("xk_eps")
    xk_rstd, xk_norm, v_done, v_biased = sem("xk_rstd"), sem("xk_norm"), sem("v_done"), sem("v_biased")
    v_copied, v_copied_act = sem("v_copied"), sem("v_copied_act")

    units = []
    for n in range(NC):
        units.append((wkv2[:, n * CB:(n + 1) * CB], 8, wc_h[:, n % 2, :, :], wc_l[:, n % 2, :, :]))
    for part in range(2):
        units.append((wqkv[:, (part + 1) * D:(part + 2) * D], 4,
                      *(a[:, part, :, :].rearrange("p k n -> p (k n)").rearrange("p (k n) -> p k n", k=4)
                        for a in (wc_h, wc_l))))
    wkv_a = [(units[NC + part][2], units[NC + part][3]) for part in range(2)]
    units.append((wqkv[:, 0:D], 4, wq_h[:, :, :], wq_l[:, :, :]))
    units.append((wproj[:, :], 4, wp_h[:, :, :], wp_l[:, :, :]))
    NU = len(units)
    CR = 3 * 2
    CTX_COLS = 2 * P + 32 * B
    XB = 2

    block = nc.Block()
    with block as block:
        @block.sync
        def _(sp):
            def load(u):
                src, chunks, _, _ = units[u]
                need(sp, raw_low, u - 1)
                sp.dma_start(raw[:, u % 2, :].rearrange("p (k n) -> p k n", k=chunks),
                             src.rearrange("(k p) n -> p k n", p=P)).then_inc(raw_loaded[u % 2], 16)

            for b in range(B):
                sp.dma_start(ctx_sb[:, b, :], ctx[b, 0:P, :]).then_inc(ctx_loaded[b], 16)
            load(0)
            sp.wait_ge(ctx_zeroed, 1)
            for b in range(B):
                sp.dma_start(ctx_sb[32 * b:32 * b + REM, 2, :], ctx[b, P:LC, :]).then_inc(ctx_loaded[2], 16)
            with nc.allow_non_contiguous_dma(reason="small tables by column"):
                sp.dma_start(kmap[:, :], mapping.rearrange("(n p f) -> p n f", p=P, f=DIL)[:, :, 0])\
                    .then_inc(maps_loaded, 16)
                for b in range(B):
                    sp.dma_start(map_raw[:, b * 16:(b + 1) * 16],
                                 mapping.rearrange("(n p) -> p n", p=P)).then_inc(maps_loaded, 16)
                    sp.dma_start(seg_raw[0:1, b * 32:(b + 1) * 32],
                                 mapping.rearrange("(a n f) -> a n f", a=1, f=BLK)[:, :, 0]).then_inc(maps_loaded, 16)
            load(1)
            with nc.allow_non_contiguous_dma(reason="small biases by column"):
                sp.dma_start(bq_col[:, :], bqkv[0:D].rearrange("(c p) -> p c", p=P)).then_inc(biases_loaded, 16)
                sp.dma_start(bk_col[:, :], bqkv[D:2 * D].rearrange("(c p) -> p c", p=P)).then_inc(biases_loaded, 16)
                sp.dma_start(bv_b[:, :], bqkv[2 * D:3 * D].partition_broadcast(P)).then_inc(biases_loaded, 16)
                sp.dma_start(bproj_b[:, :], bproj.partition_broadcast(P)).then_inc(biases_loaded, 16)
                sp.dma_start(lns_b[:, :], ln_scale.partition_broadcast(P)).then_inc(biases_loaded, 16)
                sp.dma_start(lnb_b[:, :], ln_bias.partition_broadcast(P)).then_inc(biases_loaded, 16)
                sp.dma_start(br_b[:, :], br.partition_broadcast(P)).then_inc(biases_loaded, 16)
                sp.dma_start(wr_sb[:, :, :], wr.rearrange("(k p) e -> p k e", p=P)).then_inc(biases_loaded, 16)
                for s in range(2):
                    sp.dma_start(null_k[s * D2:(s + 1) * D2, :], null_kv[0, :].rearrange("(d a) -> d a", a=1))\
                        .then_inc(null_k_loaded, 16)
                sp.wait_ge(zeroed, 1)
                for b in range(B):
                    for h in range(4):
                        sp.dma_start(v2_rest[4 * REM + h:4 * REM + h + 1, b, :, h * D2:(h + 1) * D2],
                                      null_kv[1:2, :].rearrange("a (o d) -> a o d", o=1).to_broadcast([1, 4, D2]))\
                            .then_inc(null_v_loaded, 16)
            for u in range(2, NU):
                load(u)
            sp.wait_ge(kv_evac, KB * HB + KB * 3)
            sp.wait_ge(zeroed, 1)
            for b in range(B):
                for h in range(4):
                    sp.dma_start(v2_rest[h:h + 4 * (REM - 1) + 1:4, b, :, h * D2:(h + 1) * D2],
                                 v_last[32 * b:32 * b + REM, :].rearrange("p (g h d) -> p g h d", g=4, h=4)
                                 [:, :, h, :]).then_inc(rest_placed, 16)
            sp.wait_ge(empty_made, 2)
            sp.dma_start(slot_tiles[:, 0:NT, :],
                         empty_row[:, :].rearrange("p (a d) -> p a d", a=1).to_broadcast([P, NT, ROW]))\
                .then_inc(prefilled, 16)
            sp.wait_ge(prefilled, 16)
            sp.wait_ge(rest_placed, 16 * 4 * B)

        @block.gpsimd
        def _(pool):
            pool.memset(ctx_sb[:, 2, :], 0.0).then_inc(ctx_zeroed, 1)
            pool.memset(ident[:, :], 0.0).then_inc(masks, 1)
            pool.memset(upper[:, :], 1.0).then_inc(masks, 1)
            pool.memset(head_mask[:, :], 1.0).then_inc(masks, 1)
            pool.memset(ones[:, :], 1.0).then_inc(masks, 1)
            pool.memset(minus_half[:, :], -0.5).then_inc(masks, 1)
            pool.wait_ge(masks, 5)
            pool.affine_select(out=ident[:, :], in_=ident[:, :], compare_op=ALU.not_equal, fill=1.0, base=0,
                               pattern=[[-1, P]], channel_multiplier=1).then_inc(masks, 1)
            pool.affine_select(out=upper[:, :], in_=upper[:, :], compare_op=ALU.is_ge, fill=0.0, base=0,
                               pattern=[[1, P]], channel_multiplier=-1).then_inc(masks, 1)
            pool.affine_select(out=head_mask[:, :], in_=head_mask[:, :], compare_op=ALU.is_ge, fill=0.0, base=0,
                               pattern=[[-32, 4]], channel_multiplier=1).then_inc(masks, 1)
            pool.wait_ge(masks, 8)
            pool.affine_select(out=head_mask[:, :], in_=head_mask[:, :], compare_op=ALU.is_ge, fill=0.0, base=31,
                               pattern=[[32, 4]], channel_multiplier=-1).then_inc(masks, 1)
            pool.iota(token_int[:, :], pattern=[[P, NT]], base=0, channel_multiplier=1).then_inc(masks, 1)
            pool.memset(v_tmp[:, 0, :], 0.0).then_inc(masks, 1)
            pool.wait_ge(masks, 11)
            spread = v_tmp[:, 0, :].rearrange("p (c h d) -> p c h d", c=4, h=4)
            pool.affine_select(out=spread, in_=spread, compare_op=ALU.not_equal, fill=1.0, base=0,
                               pattern=[[-32, 4], [-8, 4], [0, 32]], channel_multiplier=1).then_inc(masks, 1)
            pool.memset(k2[:, :, :, :, :], 0.0).then_inc(keys_zeroed, 1)
            pool.wait_ge(tables, 1)
            for b in range(B):
                pool.wait_ge(turned, CR + 4 * b)
                for n in range(4):
                    pool.indirect_dma_start(out=xk[:, n, :], out_offset=None, in_=x_rows,
                                            in_offset=bass.IndirectOffsetOnAxis(ap=kidx[:, b, n:n + 1], axis=0))\
                        .then_inc(xk_loaded, 16)
                pool.wait_ge(xk_eps, b + 1)
                pool.tensor_tensor(rstd[:, :], var_eps[:, :], minus_half[:, :], ALU.pow).then_inc(xk_rstd, 1)

        @block.scalar
        def _(act):
            def split(u):
                if 2 <= u < NC + 2:
                    act.wait_ge(block_done, u - 1)
                act.wait_ge(raw_loaded[u % 2], 16 * (u // 2 + 1))
                act.activation(units[u][2], raw[:, u % 2, :].rearrange("p (k n) -> p k n", k=units[u][1]), ACT.Copy)\
                    .then_inc(raw_high, 1)

            def turn(r):
                act.wait_ge(turned, r + 1)
                if r < CR:
                    dst = ct_h[:, 4 * (r % 2):4 * (r % 2) + 4, (r // 2) * P:(r // 2 + 1) * P]
                else:
                    dst = xkt[(r - CR) // 4][0][:, :, ((r - CR) % 4) * P:((r - CR) % 4 + 1) * P]
                act.activation(dst, bank[r % 2][:, :].rearrange("p (k t) -> p k t", k=4), ACT.Copy)\
                    .then_inc(turned_high, 1)

            for r in range(4):
                turn(r)
            split(0)
            for r in range(4, CR):
                turn(r)
            m = 0
            for n in range(NC):
                split(n + 1)
                for c in range(HB if n < KB else 3):
                    act.wait_ge(kv_done, m + 1)
                    src = bank[2 + m % 3]
                    if n < KB:
                        act.wait_ge(keys_zeroed, 1)
                        for s in range(2):
                            rows = slice(s * D2, (s + 1) * D2)
                            act.activation(k2[rows, :, HB * n + c, s, 0:P],
                                           src[rows, 0:2 * P].rearrange("p (b k) -> p b k", b=B), ACT.Copy,
                                           scale=SCALE2)
                            last = act.activation(
                                k2[rows, :, HB * n + c, s, P:LC],
                                src[rows, 2 * P:2 * P + 64].rearrange("p (b k) -> p b k", b=B)[:, :, 0:REM],
                                ACT.Copy, scale=SCALE2)
                    elif c < 2:
                        last = act.activation(v2_main[:, c, (n - KB) * CB:(n - KB + 1) * CB], src[:, 0:CB], ACT.Copy)
                    else:
                        act.wait_ge(spread_made, 1)
                        last = act.activation(v_last[0:64, (n - KB) * CB:(n - KB + 1) * CB], src[0:64, 0:CB], ACT.Copy)
                    last.then_inc(kv_evac, 1)
                    m += 1
                if n == XB:
                    for k in range(4):
                        turn(CR + k)
            act.wait_ge(null_k_loaded, 32)
            for s in range(2):
                rows = slice(s * D2, (s + 1) * D2)
                act.activation(k2[rows, :, :, s, LC:L2],
                               null_k[rows, 0:1].rearrange("p (a b c) -> p a b c", a=1, b=1)
                               .to_broadcast([D2, B, KI, 1]), ACT.Copy, scale=SCALE2)
            split(NC + 1)
            act.wait_ge(biases_loaded, 16 * 8)
            for b in range(B):
                for c in range(KD):
                    act.wait_ge(kv_done, m + 1)
                    act.activation(k1[:, c, b * NSEG:b * NSEG + NSEG, :],
                                   bank[2 + m % 3][:, :].rearrange("p (s k) -> p s k", s=NSEG), ACT.Identity,
                                   bias=bk_col[:, c:c + 1]).then_inc(kv_evac, 1)
                    m += 1
                    if b == 0:
                        turn(CR + 4 + c)
                for n in range(4):
                    i = 4 * b + n
                    act.wait_ge(v_biased, i + 1)
                    for s in range(4):
                        for h in (2, 3):
                            last = act.activation(
                                v1[32 * h:32 * h + 32, b * NSEG + 4 * n + s, :].rearrange("p (c d) -> p c d", c=KD),
                                v_tmp[32 * s:32 * s + 32, i % 2, :].rearrange("p (c h d) -> p c h d", c=KD, h=4)
                                [:, :, h, :], ACT.Copy)
                    last.then_inc(v_copied_act, 1)
                if b == 0:
                    split(NC + 2)
                    split(NC + 3)
            act.wait_ge(null_v_loaded, 16 * 4 * B)

        @block.vector
        def _(dve):
            dve.memset(v2_rest[:, :, :, :], 0.0).then_inc(zeroed, 1)
            dve.memset(empty_row[:, :], 0.0).then_inc(empty_made, 1)
            dve.wait_ge(empty_made, 1)
            dve.memset(empty_row[:, D + 1:D + 2].bitcast(I32), NOBODY).then_inc(empty_made, 1)
            def split(u):
                dve.wait_ge(raw_high, u + 1)
                dve.tensor_tensor(units[u][3], raw[:, u % 2, :].rearrange("p (k n) -> p k n", k=units[u][1]),
                                  units[u][2].bitcast(F32), ALU.subtract)\
                    .then_inc(raw_low, 1)

            def turn(r):
                dve.wait_ge(turned_high, r + 1)
                if r < CR:
                    cols = (slice(None), slice(4 * (r % 2), 4 * (r % 2) + 4), slice((r // 2) * P, (r // 2 + 1) * P))
                    high, low = ct_h[cols], ct_l[cols]
                else:
                    cols = (slice(None), slice(None), slice(((r - CR) % 4) * P, ((r - CR) % 4 + 1) * P))
                    high, low = (a[cols] for a in xkt[(r - CR) // 4])
                dve.tensor_tensor(low, bank[r % 2][:, :].rearrange("p (k t) -> p k t", k=4), high.bitcast(F32),
                                  ALU.subtract).then_inc(turned_low, 1)

            def norm(b):
                dve.wait_ge(xk_loaded, 64 * (b + 1))
                for n in range(4):
                    last = dve.bn_stats(stats[:, n, :], xk[:, n, :])
                last.then_inc(xk_stats, 1)
                dve.wait_ge(xk_stats, b + 1)
                for n in range(4):
                    last = dve.bn_aggr(mv[:, n, :], stats[:, n, :])
                last.then_inc(xk_aggr, 1)
                dve.wait_ge(xk_aggr, b + 1)
                dve.tensor_scalar(var_eps[:, :], mv[:, :, 1], EPS1, None, ALU.add).then_inc(xk_eps, 1)
                dve.wait_ge(xk_rstd, b + 1)
                for n in range(4):
                    dve.tensor_scalar(xk[:, n, :], xk[:, n, :], mv[:, n, 0:1], rstd[:, n:n + 1], ALU.subtract,
                                      ALU.mult).then_inc(xk_norm, 1)

            for r in range(4):
                turn(r)
            split(0)
            for r in range(4, CR):
                turn(r)
            dve.wait_ge(maps_loaded, 16 * (2 * B + 1))
            for b in range(B):
                last = dve.tensor_scalar(kidx[:, b, :], kmap[:, :], M - 1, b * M, ALU.min, ALU.add)
            last.then_inc(tables, 1)
            for b in range(B):
                dve.tensor_scalar(idx_all[:, 16 * b:16 * b + 16], map_raw[:, 16 * b:16 * b + 16], M - 1, b * M,
                                  ALU.min, ALU.add)
            dve.tensor_scalar(seg_raw[:, :], seg_raw[:, :], 7, None, ALU.arith_shift_right).then_inc(tables, 1)
            dve.wait_ge(tables, 2)
            for b in range(B):
                dve.tensor_scalar(seg_tab[:, 32 * b:32 * b + 32], seg_raw[:, 32 * b:32 * b + 32], NSEG - 1, b * NSEG,
                                  ALU.min, ALU.add)
            for e in range(E):
                dve.memset(rev[:, e:e + 1], float(E - e))
            dve.wait_ge(masks, 10)
            dve.tensor_copy(token_f[:, :], token_int[:, :])
            dve.tensor_copy(head_pick[:, :].rearrange("p (h d) -> p h d", h=4),
                            head_mask[:, :].rearrange("p (h d) -> p h d", d=1).to_broadcast([P, 4, 8]))
            dve.wait_ge(masks, 12)
            dve.tensor_copy(head_spread[:, :, :].rearrange("p c m -> p (c m)"), v_tmp[:, 0, :])\
                .then_inc(spread_made, 1)
            for u in range(1, NC + 2):
                split(u)
                if u == XB:
                    norm(0)
                if u == XB + 1:
                    for k in range(4):
                        turn(CR + k)
                if u == XB + 3:
                    norm(1)
            for n in range(4):
                turn(CR + 4 + n)
            dve.wait_ge(biases_loaded, 16 * 8)
            dve.wait_ge(rest_placed, 16 * 4 * B)
            for b in range(B):
                for n in range(4):
                    i = 4 * b + n
                    dve.wait_ge(v_done, i + 1)
                    need(dve, v_copied, i - 1)
                    need(dve, v_copied_act, i - 1)
                    dve.tensor_tensor(v_tmp[:, i % 2, :], bank[5 + i % 2][:, :], bv_b[:, :], ALU.add)\
                        .then_inc(v_biased, 1)
                    dve.wait_ge(v_biased, i + 1)
                    for s in range(4):
                        for h in (0, 1):
                            last = dve.tensor_copy(
                                v1[32 * h:32 * h + 32, b * NSEG + 4 * n + s, :].rearrange("p (c d) -> p c d", c=KD),
                                v_tmp[32 * s:32 * s + 32, i % 2, :].rearrange("p (c h d) -> p c h d", c=KD, h=4)
                                [:, :, h, :])
                    last.then_inc(v_copied, 1)
                if b == 0:
                    split(NC + 2)
                    split(NC + 3)

        @block.tensor
        def _(pe):
            pe.wait_ge(masks, 9)

            def turn(r, src):
                need(pe, turned_low, r - 1)
                for k in range(4):
                    last = pe.transpose(bank[r % 2][:, k * P:(k + 1) * P], src(k), ident[:, :])
                last.then_inc(turned, 1)

            for r in range(CR):
                pe.wait_ge(ctx_loaded[r // 2], 16 if r < 4 else 32)
                turn(r, lambda k, r=r: ctx_sb[:, r // 2, (4 * (r % 2) + k) * P:(4 * (r % 2) + k + 1) * P])
            def turn_keys(b, n):
                pe.wait_ge(xk_norm, 4 * b + n + 1)
                turn(CR + 4 * b + n, lambda k: xk[:, n, k * P:(k + 1) * P])

            pe.wait_ge(turned_low, CR)
            m = 0
            for n in range(NC):
                pe.wait_ge(raw_low, n + 1)
                for c in range(HB if n < KB else 3):
                    need(pe, kv_evac, m - 2)
                    for k in range(KC):
                        if n < KB:
                            w = [a[:, n % 2, k, c * P:(c + 1) * P] for a in (wc_h, wc_l)]
                            last = product(pe, bank[2 + m % 3][:, 0:CTX_COLS], w,
                                           [a[:, k, 0:CTX_COLS] for a in (ct_h, ct_l)], k == 0, k == KC - 1)
                        else:
                            t = [a[:, k, c * P:(c + 1) * P] for a in (ct_h, ct_l)]
                            last = product(pe, bank[2 + m % 3][:, 0:CB], t,
                                           [a[:, n % 2, k, :] for a in (wc_h, wc_l)], k == 0, k == KC - 1)
                    last.then_inc(kv_done, 1)
                    m += 1
                pe.wait_ge(kv_done, m)
                pe.sem_inc(block_done, 1)
                if n == XB:
                    for k in range(4):
                        turn_keys(0, k)
            for b in range(B):
                xkt_h, xkt_l = xkt[b]
                pe.wait_ge(turned_low, CR + 4 * b + 4)
                pe.wait_ge(raw_low, NC + 1)
                for c in range(KD):
                    need(pe, kv_evac, m - 2)
                    for k in range(KD):
                        w = [a[:, k, c * P:(c + 1) * P] for a in wkv_a[0]]
                        last = product(pe, bank[2 + m % 3][:, :], w, [a[:, k, :] for a in (xkt_h, xkt_l)], k == 0,
                                       k == KD - 1)
                    last.then_inc(kv_done, 1)
                    m += 1
                    if b == 0:
                        turn_keys(1, c)
                pe.wait_ge(raw_low, NC + 2)
                for n in range(4):
                    i = 4 * b + n
                    need(pe, v_biased, i - 1)
                    for k in range(KD):
                        t = [a[:, k, n * P:(n + 1) * P] for a in (xkt_h, xkt_l)]
                        last = product(pe, bank[5 + i % 2][:, :], t,
                                       [a[:, k, :] for a in wkv_a[1]], k == 0, k == KD - 1)
                    last.then_inc(v_done, 1)


def self_attention(nc, sem, sb, bank, x_rows, x_tiles, x1_tiles, ident, head_mask, minus_half, bproj_b, wq_h, wq_l,
                   wp_h, wp_l, bq_col, k1, v1, idx_all, head_pick, head_spread, seg_tab):
    idx = sb("a_idx", [P, G], I32)
    xg = sb("a_xg", [P, G, D])
    xt_h = sb("a_xt_h", [P, KD, G * P], F32R)
    xt_l = sb("a_xt_l", [P, KD, G * P], F32R)
    qt = sb("a_qt", [P, KD, G * P])
    k_block = sb("a_k_block", [P, 4, KD, 4, NKEY])
    v_block = sb("a_v_block", [P, 4, KD, 4, D1])
    prob = sb("a_prob", [P, G, D])
    top = sb("a_top", [P, G, 2 * KD])
    total, recip = sb("a_total", [P, P]), sb("a_recip", [P, P])
    recip_h, recip_l = sb("a_recip_h", [P, P], F32R), sb("a_recip_l", [P, P], F32R)
    recip_t = sb("a_recip_t", [P, D])
    mixed = sb("a_mixed", [P, D])
    at_h = sb("a_at_h", [P, 2, KD, P], F32R)
    at_l = sb("a_at_l", [P, 2, KD, P], F32R)
    xr = sb("a_xr", [P, G, D])
    stats = sb("a_stats", [P, G, 6])
    mv = sb("a_mv", [P, G, 2])
    var_eps = sb("a_var_eps", [P, G])
    rstd = sb("a_rstd", [P, G])

    names = ("slot_tables gathered0 gathered1 gathered2 gathered3 stats_done aggr_done eps_done rstd_done normed "
             "x_turned x_high x_low q_done q_evac k_ready v_ready s_done s_top s_shifted s_exp a_done sum_done "
             "sum_eps sum_recip recip_high recip_low recip_spread recip_evac a_norm a_high a_low proj_done x1_made "
             "res_biased").split()
    s = {n: sem("a_" + n) for n in names}
    xr_loaded = [sem(f"a_xr_loaded{t}") for t in range(G)]
    x1_stored = [sem(f"a_x1_stored{t}") for t in range(G)]
    x_bank, q_bank, s_bank, sum_bank, a_bank, o_bank, r_bank = (bank[0], bank[1:3], bank[3], bank[4], bank[5],
                                                                bank[6], bank[7])

    def run(eng, step):
        for i in (-1, 0):
            step(i)
        with eng.Fori(1, NG - 2) as i:
            step(i)
        for i in (NG - 2, NG - 1, NG):
            step(i)

    def there(i):
        return not isinstance(i, int) or 0 <= i < NG

    def tiled(n):
        return not isinstance(n, int) or 0 <= n < NT

    def normed_in(i, t):
        return there(i + 2) if t else there(i + 1) and not (isinstance(i, int) and i < 0)

    block = nc.Block()
    with block as block:
        @block.sync
        def _(sp):
            def step(i):
                for t in range(G):
                    n = G * i + t
                    k = (t + 2) % G
                    if tiled(n - 2):
                        need(sp, s["x1_made"], n - 1)
                        sp.dma_start(x1_tiles[:, n - 2, :], xr[:, k, :]).then_inc(x1_stored[k], 16)
                    if tiled(n + 2):
                        need(sp, x1_stored[k], 16 * (i if t < 2 else i + 1))
                        sp.dma_start(xr[:, k, :], x_tiles[:, n + 2, :]).then_inc(xr_loaded[k], 16)
            step(-2)
            run(sp, step)
            for t in range(G):
                sp.wait_ge(x1_stored[t], 16 * NG)

        @block.gpsimd
        def _(pool):
            def spread(dst, src):
                return pool.tensor_tensor(dst, src, head_mask[:, :].rearrange("p (a h d) -> p a h d", a=1, d=1)
                                          .to_broadcast([P, KD, 4, 32]), ALU.mult)

            def segment(n, j):
                return pool.value_load(seg_tab[0:1, bass.ds(2 * n + j, 1)], min_val=0, max_val=B * NSEG - 1)

            def values(n, t):
                hold(pool, s["a_done"], n - 1)
                for j in range(2):
                    g = segment(n, j)
                    ins = spread(v_block[:, 2 * (t % 2) + j, :, :, :],
                                 v1[:, bass.ds(g, 1), :].rearrange("p a (c d) -> p c a d", c=KD)
                                 .to_broadcast([P, KD, 4, D1]))
                ins.then_inc(s["v_ready"], 1)

            def keys(n, t):
                hold(pool, s["s_done"], n - 1)
                for j in range(2):
                    g = segment(n, j)
                    ins = spread(k_block[:, 2 * (t % 2) + j, :, :, :],
                                 k1[:, :, bass.ds(g, 1), :].to_broadcast([P, KD, 4, NKEY]))
                ins.then_inc(s["k_ready"], 1)

            def step(i):
                for t in range(G):
                    n = G * i + t
                    m, k = n + 7, (t + 3) % G
                    early = isinstance(n, int) and n < 0
                    if tiled(n + 1) and not early:
                        values(n + 1, t + 1)
                    if tiled(n + 2) and not early:
                        keys(n + 2, t)
                    if tiled(n):
                        hold(pool, xr_loaded[t], 16 * (i + 1))
                        pool.tensor_tensor(xr[:, t, :], xr[:, t, :], bproj_b[:, :], ALU.add)\
                            .then_inc(s["res_biased"], 1)
                    if there(i + 2):
                        hold(pool, s["x_turned"], G * (i + 1) + t + 1)
                        gather(n + 8, t)
                    if normed_in(i, t):
                        power(m, k)

            def gather(m, k):
                hold(pool, s["slot_tables"], m + 1)
                pool.indirect_dma_start(out=xg[:, k, :], out_offset=None, in_=x_rows,
                                        in_offset=bass.IndirectOffsetOnAxis(ap=idx[:, k:k + 1], axis=0))\
                    .then_inc(s[f"gathered{k}"], 16)

            def power(m, k):
                hold(pool, s["eps_done"], m + 1)
                pool.tensor_tensor(rstd[:, k:k + 1], var_eps[:, k:k + 1], minus_half[:, 0:1], ALU.pow)\
                    .then_inc(s["rstd_done"], 1)

            for k in range(G):
                gather(k, k)
            keys(0, 0)
            keys(1, 1)
            values(0, 0)
            for k in range(G):
                power(k, k)
            run(pool, step)

        @block.scalar
        def _(act):
            def expo(n, t):
                need(act, s["s_shifted"], n + 1)
                act.activation(prob[:, t % G, :], prob[:, t % G, :], ACT.Exp, scale=SCALE1).then_inc(s["s_exp"], 1)

            def q_copy(i, c):
                need(act, s["q_done"], KD * i + c + 1)
                act.activation(qt[:, c, :], q_bank[c % 2][:, :], ACT.Identity, bias=bq_col[:, c:c + 1])\
                    .then_inc(s["q_evac"], 1)

            def xt_copy(i, k):
                need(act, s["x_turned"], G * i + k + 1)
                act.activation(xt_h[:, :, k * P:(k + 1) * P], x_bank[:, :].rearrange("p (k t) -> p k t", k=KD),
                               ACT.Copy).then_inc(s["x_high"], 1)

            def step(i):
                for t in range(G):
                    n = G * i + t
                    if t == 0 and there(i + 1):
                        xt_copy(i + 1, 0)
                    if tiled(n):
                        need(act, s["sum_recip"], n + 1)
                        act.activation(recip_h[:, :], recip[:, :], ACT.Copy).then_inc(s["recip_high"], 1)
                    if t < 3 and tiled(n + 1):
                        expo(n + 1, t + 1)
                    if there(i + 1):
                        if t == 1:
                            xt_copy(i + 1, 2)
                        elif t > 1:
                            q_copy(i + 1, 2 * (t - 2))
                    if tiled(n):
                        need(act, s["recip_spread"], n + 1)
                        act.activation(recip_t[:, :], r_bank[:, :], ACT.Copy).then_inc(s["recip_evac"], 1)
                        need(act, s["a_norm"], n + 1)
                        act.activation(at_h[:, t % 2, :, :], mixed[:, :].rearrange("p (c t) -> p c t", c=KD),
                                       ACT.Copy).then_inc(s["a_high"], 1)
                    if there(i + 1):
                        if t < 2:
                            xt_copy(i + 1, 2 * t + 1)
                        else:
                            q_copy(i + 1, 2 * (t - 2) + 1)
                    if t == 3 and tiled(n + 1):
                        expo(n + 1, t + 1)
            run(act, step)

        @block.vector
        def _(dve):
            def table(m, k):
                dve.tensor_scalar(idx[:, k:k + 1], idx_all[:, bass.ds(m, 1)], 0, None, ALU.add)\
                    .then_inc(s["slot_tables"], 1)

            def row_stats(m, k, group):
                need(dve, s[f"gathered{k}"], 16 * (group + 1))
                dve.bn_stats(stats[:, k, :], xg[:, k, :]).then_inc(s["stats_done"], 1)
                hold(dve, s["stats_done"], m + 1)
                dve.bn_aggr(mv[:, k, :], stats[:, k, :]).then_inc(s["aggr_done"], 1)
                need(dve, s["aggr_done"], m + 1)
                dve.tensor_scalar(var_eps[:, k:k + 1], mv[:, k, 1:2], EPS1, None, ALU.add).then_inc(s["eps_done"], 1)

            def norm(m, k):
                need(dve, s["rstd_done"], m + 1)
                dve.tensor_scalar(xg[:, k, :], xg[:, k, :], mv[:, k, 0:1], rstd[:, k:k + 1], ALU.subtract,
                                  ALU.mult).then_inc(s["normed"], 1)

            def shift(n, t):
                s3 = s_bank[:, :].rearrange("p (c q) -> p c q", q=BLK)
                need(dve, s["s_done"], n + 1)
                dve.tensor_reduce(top[:, t % G, :], s3, AX.X, ALU.max).then_inc(s["s_top"], 1)
                need(dve, s["s_top"], n + 1)
                dve.tensor_tensor(prob[:, t % G, :].rearrange("p (c q) -> p c q", q=BLK), s3,
                                  top[:, t % G, :].rearrange("p (c q) -> p c q", q=1)
                                  .to_broadcast([P, 2 * KD, BLK]), ALU.subtract).then_inc(s["s_shifted"], 1)

            def xt_copy(i, k):
                need(dve, s["x_high"], G * i + k + 1)
                dve.tensor_tensor(xt_l[:, :, k * P:(k + 1) * P], x_bank[:, :].rearrange("p (k t) -> p k t", k=KD),
                                  xt_h[:, :, k * P:(k + 1) * P].bitcast(F32), ALU.subtract)\
                    .then_inc(s["x_low"], 1)

            def step(i):
                for t in range(G):
                    n = G * i + t
                    m, k = n + 7, (t + 3) % G
                    if there(i + 2):
                        need(dve, s[f"gathered{t}"], 16 * (i + 2))
                        table(n + 8, t)
                    if tiled(n - 2):
                        need(dve, s["proj_done"], n - 1)
                        need(dve, s["res_biased"], n - 1)
                        r = (t + 2) % G
                        dve.tensor_tensor(xr[:, r, :], o_bank[:, :], xr[:, r, :], ALU.add).then_inc(s["x1_made"], 1)
                    if t == 0 and there(i + 1):
                        xt_copy(i + 1, 0)
                    if tiled(n):
                        need(dve, s["sum_done"], n + 1)
                        dve.tensor_scalar(total[:, :], sum_bank[:, 0:P], EPS_SUM, None, ALU.add)\
                            .then_inc(s["sum_eps"], 1)
                        need(dve, s["sum_eps"], n + 1)
                        dve.reciprocal(recip[:, :], total[:, :]).then_inc(s["sum_recip"], 1)
                        need(dve, s["recip_high"], n + 1)
                        dve.tensor_tensor(recip_l[:, :], recip[:, :], recip_h[:, :].bitcast(F32), ALU.subtract)\
                            .then_inc(s["recip_low"], 1)
                    if t < 3 and tiled(n + 1):
                        shift(n + 1, t + 1)
                    if t == 1 and there(i + 1):
                        xt_copy(i + 1, 2)
                    if tiled(n):
                        need(dve, s["a_done"], n + 1)
                        need(dve, s["recip_evac"], n + 1)
                        dve.tensor_tensor(mixed[:, :], a_bank[:, :], recip_t[:, :], ALU.mult).then_inc(s["a_norm"], 1)
                    if normed_in(i, t):
                        row_stats(m, k, i + 2 if t else i + 1)
                    if tiled(n):
                        need(dve, s["a_high"], n + 1)
                        dve.tensor_tensor(at_l[:, t % 2, :, :], mixed[:, :].rearrange("p (c t) -> p c t", c=KD),
                                          at_h[:, t % 2, :, :].bitcast(F32), ALU.subtract).then_inc(s["a_low"], 1)
                    if t < 2 and there(i + 1):
                        xt_copy(i + 1, 2 * t + 1)
                    if normed_in(i, t):
                        norm(m, k)
                    if t == 3 and tiled(n + 1):
                        shift(n + 1, t + 1)

            for k in range(G):
                table(k, k)
            for k in range(G):
                row_stats(k, k, 0)
            for k in range(G):
                norm(k, k)
            run(dve, step)

        @block.tensor
        def _(pe):
            def sums(n, t):
                need(pe, s["s_exp"], n + 1)
                need(pe, s["sum_eps"], n)
                for c in range(KD):
                    last = pe.matmul(sum_bank[32 * c:32 * c + 32, 0:P], head_pick[:, :],
                                     prob[:, t, c * P:(c + 1) * P], start=True, stop=True)
                last.then_inc(s["sum_done"], 1)

            def scores(n, t):
                need(pe, s["k_ready"], n + 1)
                need(pe, s["s_shifted"], n)
                for c in range(KD):
                    for j in range(2):
                        o = c * P + BLK * j
                        last = pe.matmul(s_bank[:, o:o + BLK], k_block[:, 2 * (t % 2) + j, c, :, :],
                                         qt[:, c, (t % G) * P + BLK * j:(t % G) * P + BLK * (j + 1)], start=True,
                                         stop=True)
                last.then_inc(s["s_done"], 1)

            def values(n, t):
                need(pe, s["v_ready"], n + 1)
                need(pe, s["a_norm"], n)
                for c in range(KD):
                    for j in range(2):
                        o = c * P + BLK * j
                        last = pe.matmul(a_bank[:, o:o + BLK], v_block[:, 2 * (t % 2) + j, c, :, :],
                                         prob[:, t, o:o + BLK], start=True, stop=True)
                last.then_inc(s["a_done"], 1)

            def turn_x(i, k):
                need(pe, s["normed"], G * i + k + 1)
                need(pe, s["x_low"], G * i + k)
                for c in range(KD):
                    last = pe.transpose(x_bank[:, c * P:(c + 1) * P], xg[:, k, c * P:(c + 1) * P], ident[:, :])
                last.then_inc(s["x_turned"], 1)

            def spread_recip(n):
                need(pe, s["recip_low"], n + 1)
                need(pe, s["recip_evac"], n)
                for c in range(KD):
                    pe.matmul(r_bank[:, c * P:(c + 1) * P], head_spread[:, c, :], recip_h[:, :], start=True,
                              stop=False)
                    last = pe.matmul(r_bank[:, c * P:(c + 1) * P], head_spread[:, c, :], recip_l[:, :],
                                     start=False, stop=True)
                last.then_inc(s["recip_spread"], 1)

            def queries(i, c):
                need(pe, s["x_low"], G * (i + 1))
                need(pe, s["q_evac"], KD * i + c - 1)
                for k in range(KD):
                    last = product(pe, q_bank[c % 2][:, :], [a[:, k, c * P:(c + 1) * P] for a in (wq_h, wq_l)],
                                   [a[:, k, :] for a in (xt_h, xt_l)], k == 0, k == KD - 1)
                last.then_inc(s["q_done"], 1)

            def project(n, t, first, end):
                if first == 0:
                    need(pe, s["a_low"], n + 1)
                    need(pe, s["x1_made"], n)
                for c in range(first, end):
                    last = product(pe, o_bank[:, :], [a[:, t % 2, c, :] for a in (at_h, at_l)],
                                   [a[:, c, :] for a in (wp_h, wp_l)], c == 0, c == KD - 1)
                if end == KD:
                    last.then_inc(s["proj_done"], 1)

            def step(i):
                for t in range(G):
                    n = G * i + t
                    if t == 0 and there(i + 1):
                        turn_x(i + 1, 0)
                    if tiled(n):
                        sums(n, t)
                    if t < 3 and tiled(n + 1):
                        scores(n + 1, t + 1)
                    if tiled(n):
                        values(n, t)
                    if there(i + 1):
                        if t == 1:
                            turn_x(i + 1, 2)
                        elif t > 1:
                            queries(i + 1, 2 * (t - 2))
                    if tiled(n):
                        spread_recip(n)
                    if t == 3 and there(i + 1):
                        queries(i + 1, 3)
                    if tiled(n - 1):
                        project(n - 1, t + 1, 0, 1)
                    if t == 3 and tiled(n + 1):
                        need(pe, s["q_evac"], KD * (i + 2))
                        scores(n + 1, t + 1)
                    if tiled(n - 1):
                        project(n - 1, t + 1, 1, KD)
                    if t == 2 and there(i + 1):
                        queries(i + 1, 1)
                    if t < 2 and there(i + 1):
                        turn_x(i + 1, 2 * t + 1)
            run(pe, step)


def cross_attention(nc, sem, sb, bank, x1_tiles, out_tiles, slots_dram, wq2, wout, ident, upper, ones, minus_half, rev,
                    token_int, token_f, lns_b, lnb_b, br_b, wr_sb, k2, v2_main, v2_rest):
    wq_h, wq_l = sb("b_wq_h", [P, KD, INNER], F32R), sb("b_wq_l", [P, KD, INNER], F32R)
    wo_h, wo_l = sb("b_wo_h", [P, KI, D], F32R), sb("b_wo_l", [P, KI, D], F32R)
    xn = sb("b_xn", [P, G, D])
    xt_h, xt_l = sb("b_xt_h", [P, KD, G * P], F32R), sb("b_xt_l", [P, KD, G * P], F32R)
    qt = sb("b_qt", [P, KI, G * P])
    prob = sb("b_prob", [P, 2, 4, PW, 4])
    raw = prob[:, :, :, :, :].rearrange("p a g k h -> p (a g k h)")[:, 0:2 * 2048].rearrange("p (a n) -> p a n", a=2)
    pt = sb("b_pt", [P, 4 + H2, P])
    ot_h, ot_l = sb("b_ot_h", [P, KI, P], F32R), sb("b_ot_l", [P, KI, P], F32R)
    xr = sb("b_xr", [P, D])
    x2 = sb("b_x2", [P, 2, D])
    y = sb("b_y", [P, D])
    yt = sb("b_yt", [P, KD, P])
    rows = sb("b_rows", [P, G, ROW])
    neg_top, total, recip = sb("b_neg_top", [P, 2, H2]), sb("b_total", [P, 2, H2]), sb("b_recip", [P, 2, H2])
    kinds = ("x", "w", "y")
    stats = {k: sb(f"b_{k}_stats", [P, 6]) for k in kinds}
    mv = {k: sb(f"b_{k}_mv", [P, 2]) for k in kinds}
    var_eps = {k: sb(f"b_{k}_var", [P, 1]) for k in kinds}
    rstd = {k: sb(f"b_{k}_rstd", [P, 1]) for k in kinds}
    logit = sb("b_logit", [P, G, E])
    p_e, q_e = sb("b_p_e", [P, G, E]), sb("b_q_e", [P, G, E])
    onehot = sb("b_onehot", [P, G, E])
    before = sb("b_before", [P, G + 1, E])
    c4 = {k: sb(f"b_{k}", [P, G]) for k in ("top4", "sum4", "rec4", "gate4", "rank4", "pos4", "keep4", "slot4")}
    counts = sb("b_counts", [P, 2, G, E])
    slot_idx = sb("b_slot_idx", [P, G], I32)

    names = ("raw_high raw_low padded x_loaded0 x_loaded1 x_loaded2 x_loaded3 x_normed x_turned x_high x_low q_done "
             "q_evac s_done s_max s_exp s_recip s_scaled pt_turned pt_evac pt_evac_act o_done ot_high ot_low w_done "
             "w_normed xr_loaded xr_biased w_scaled x2_made y_normed y_turned y_evac l_done l_evac rows_loaded "
             "route_step route_exp counted counts_read routed scattered rows_free").split()
    s = {n: sem("b_" + n) for n in names}
    raw_loaded = [sem("b_raw_loaded0"), sem("b_raw_loaded1")]
    x2_stored = [sem("b_x2_stored0"), sem("b_x2_stored1")]
    ln = {k: {n: sem(f"b_{k}_{n}") for n in ("stats", "aggr", "eps", "rstd")} for k in kinds}
    pt_bank, s_bank, q_bank, o_bank, w_bank, x_bank = bank[0:2], bank[2:4], bank[4], bank[5], bank[6], bank[7]
    ot_bank = (o_bank, x_bank)
    NB = NG // B
    PS = H2 // 2
    QUERIES = {(2, 1): 0, (2, 3): 1, (2, 5): 2, (2, 7): 3, (3, 0): 4, (3, 1): 5, (3, 3): 6, (3, 5): 7}
    RS1, RS2 = 10, 13

    units = [(wq2[:, n * 512:(n + 1) * 512], wq_h[:, :, n * 512:(n + 1) * 512], wq_l[:, :, n * 512:(n + 1) * 512])
             for n in range(2)]
    units += [(wout[n * 512:(n + 1) * 512, :], wo_h[:, 4 * n:4 * n + 4, :], wo_l[:, 4 * n:4 * n + 4, :])
              for n in range(2)]
    NU = len(units)

    def run(eng, step):
        for i in (-2, -1, 0):
            step(i, 0, 0)
        with eng.Fori(1, NB - 1) as i:
            step(i, 0, 0)
        step(NB - 1, 0, 1)
        with eng.Fori(NB, NG - 2) as i:
            step(i, 1, 1)
        for i in (NG - 2, NG - 1, NG):
            step(i, 1, 1)

    def there(i):
        return not isinstance(i, int) or 0 <= i < NG

    def tiled(n):
        return not isinstance(n, int) or 0 <= n < NT

    def capped(v, most):
        return min(v, most) if isinstance(v, int) else v

    block = nc.Block()
    with block as block:
        @block.sync
        def _(sp):
            def load_weights():
                for u, (src, _, _) in enumerate(units):
                    need(sp, s["raw_low"], u - 1)
                    sp.dma_start(raw[:, u % 2, :].rearrange("p (k n) -> p k n", k=4),
                                 src.rearrange("(k p) n -> p k n", p=P)).then_inc(raw_loaded[u % 2], 16)

            def step(i, *_):
                if isinstance(i, int) and i == -1:
                    load_weights()
                for t in range(G):
                    n = G * i + t
                    if tiled(n - 2):
                        need(sp, s["x2_made"], n - 1)
                        sp.dma_start(out_tiles[:, n - 2, :], x2[:, t % 2, :]).then_inc(x2_stored[t % 2], 16)
                    if t == 2 and there(i - 1):
                        need(sp, x2_stored[0], 32 * i)
                        need(sp, x2_stored[1], 32 * i)
                        need(sp, s["rows_free"], i)
                        sp.dma_start(rows[:, :, 0:D], out_tiles[:, bass.ds(G * (i - 1), G), :])\
                            .then_inc(s["rows_loaded"], 16)
                    if there(i + 2):
                        need(sp, s["x_turned"], G * (i + 1) + t + 1)
                        sp.dma_start(xn[:, t, :], x1_tiles[:, G * (i + 2) + t, :]).then_inc(s[f"x_loaded{t}"], 16)
                    if tiled(n):
                        need(sp, s["x2_made"], n)
                        sp.dma_start(xr[:, :], x1_tiles[:, n, :]).then_inc(s["xr_loaded"], 16)
            run(sp, step)
            for par in range(2):
                sp.wait_ge(x2_stored[par], 16 * NT // 2)

        @block.gpsimd
        def _(pool):
            def power(kind, count):
                hold(pool, ln[kind]["eps"], count)
                pool.tensor_tensor(rstd[kind][:, :], var_eps[kind][:, :], minus_half[:, 0:1], ALU.pow)\
                    .then_inc(ln[kind]["rstd"], 1)

            def step(i, *_):
                for t in range(G):
                    n = G * i + t
                    if tiled(n - 2):
                        power("y", n - 1)
                    if tiled(n - 1):
                        hold(pool, s["xr_loaded"], 16 * n)
                        pool.tensor_tensor(xr[:, :], xr[:, :], lnb_b[:, :], ALU.add).then_inc(s["xr_biased"], 1)
                    if tiled(n - 1):
                        power("w", n)
                        x2t = x2[:, (t + 1) % 2, :]
                        hold(pool, s["w_normed"], n)
                        pool.tensor_tensor(x2t, x2t, lns_b[:, :], ALU.mult).then_inc(s["w_scaled"], 1)
                        hold(pool, s["w_scaled"], n)
                        hold(pool, s["xr_biased"], n)
                        pool.tensor_tensor(x2t, x2t, xr[:, :], ALU.add).then_inc(s["x2_made"], 1)
                    if there(i + 2 if t else i + 1):
                        power("x", n + 8)
                    if t == 3 and there(i - 1):
                        hold(pool, s["routed"], i)
                        for k in range(G):
                            pool.indirect_dma_start(out=slots_dram, out_offset=bass.IndirectOffsetOnAxis(
                                ap=slot_idx[:, k:k + 1], axis=0), in_=rows[:, k, :], in_offset=None)\
                                .then_inc(s["scattered"], 16)
                        hold(pool, s["scattered"], 64 * i)
                        pool.sem_inc(s["rows_free"], 1)
            pool.sem_inc(s["rows_free"], 1)
            run(pool, step)
            pool.wait_ge(s["scattered"], 64 * NG)

        @block.scalar
        def _(act):
            def split(u):
                act.wait_ge(raw_loaded[u % 2], 16 * (u // 2 + 1))
                act.activation(units[u][1], raw[:, u % 2, :].rearrange("p (k n) -> p k n", k=4), ACT.Copy)\
                    .then_inc(s["raw_high"], 1)

            def expo(n, t, j):
                need(act, s["s_max"], PS * n + j + 1)
                for h in range(2):
                    last = act.activation(prob[:, t % 2, j // 2, 0:L2, 2 * (j % 2) + h],
                                          s_bank[j % 2][:, h * L2:(h + 1) * L2], ACT.Exp,
                                          bias=neg_top[:, t % 2, 2 * j + h:2 * j + h + 1],
                                          accum_out=total[:, t % 2, 2 * j + h:2 * j + h + 1])
                last.then_inc(s["s_exp"], 1)

            def q_copy(i, c):
                need(act, s["q_done"], KI * i + c + 1)
                src = w_bank if isinstance(i, int) and i == 0 and c % 2 else q_bank
                act.activation(qt[:, c, :], src[:, :], ACT.Copy).then_inc(s["q_evac"], 1)

            def pt_copy(n, t, u):
                if u == 1:
                    need(act, s["o_done"], 2 * n)
                need(act, s["pt_turned"], 5 * n + u + 1)
                act.activation(pt[:, 4 * u:4 * u + 4, :],
                               pt_bank[(5 * t + u) % 2][:, :].rearrange("p (c t) -> p c t", c=4), ACT.Copy)\
                    .then_inc(s["pt_evac_act"], 1)

            def xt_copy(i, k):
                need(act, s["x_turned"], G * i + k + 1)
                act.activation(xt_h[:, :, k * P:(k + 1) * P], x_bank[:, :].rearrange("p (k t) -> p k t", k=KD),
                               ACT.Copy).then_inc(s["x_high"], 1)

            def ot_copy(n, u):
                need(act, s["o_done"], 2 * n + u + 1)
                act.activation(ot_h[:, 4 * u:4 * u + 4, :], ot_bank[u][:, :].rearrange("p (c t) -> p c t", c=4),
                               ACT.Copy).then_inc(s["ot_high"], 1)

            def step(i, *_):
                for t in range(G):
                    n = G * i + t
                    if isinstance(i, int) and i == -1:
                        if t == 3:
                            act.wait_ge(s["padded"], 1)
                    if t < 2 and there(i + 1):
                        xt_copy(i + 1, 2 * t)
                    if tiled(n):
                        pt_copy(n, t, 1)
                    for j in range(PS):
                        if j == 4 and tiled(n):
                            ot_copy(n, 0)
                        if tiled(n + 1):
                            expo(n + 1, t + 1, j)
                        if (t, j) in QUERIES and there(i + 1):
                            q_copy(i + 1, QUERIES[t, j])
                        if (t, j) in ((2, 3), (2, 5)) and isinstance(i, int) and i == -1:
                            split(2 + j // 5)
                        if j == 2 and tiled(n):
                            pt_copy(n, t, 3)
                        if j == 2 and t < 2 and there(i + 1):
                            xt_copy(i + 1, 2 * t + 1)
                            if isinstance(i, int) and i == -1:
                                split(t)
                    if tiled(n):
                        ot_copy(n, 1)
                    if t == 1 and there(i - 1):
                        need(act, s["route_step"], (RS1 + RS2) * (i - 1) + 2)
                        act.activation(p_e[:, :, :], q_e[:, :, :], ACT.Exp).then_inc(s["route_exp"], 1)
            run(act, step)

        @block.vector
        def _(dve):
            dve.memset(before[:, :, :], 0.0)

            def split(u):
                dve.wait_ge(s["raw_high"], u + 1)
                dve.tensor_tensor(units[u][2], raw[:, u % 2, :].rearrange("p (k n) -> p k n", k=4),
                                  units[u][1].bitcast(F32), ALU.subtract).then_inc(s["raw_low"], 1)

            def norm_stats(kind, count, src, eps):
                dve.bn_stats(stats[kind][:, :], src).then_inc(ln[kind]["stats"], 1)
                hold(dve, ln[kind]["stats"], count)
                dve.bn_aggr(mv[kind][:, :], stats[kind][:, :]).then_inc(ln[kind]["aggr"], 1)
                need(dve, ln[kind]["aggr"], count)
                dve.tensor_scalar(var_eps[kind][:, :], mv[kind][:, 1:2], eps, None, ALU.add)\
                    .then_inc(ln[kind]["eps"], 1)

            def norm(kind, count, dst, src):
                need(dve, ln[kind]["rstd"], count)
                return dve.tensor_scalar(dst, src, mv[kind][:, 0:1], rstd[kind][:, :], ALU.subtract, ALU.mult)

            def pt_copy(n, t, u):
                if u == 0:
                    need(dve, s["o_done"], 2 * n)
                need(dve, s["pt_turned"], 5 * n + u + 1)
                dve.tensor_copy(pt[:, 4 * u:4 * u + 4, :],
                                pt_bank[(5 * t + u) % 2][:, :].rearrange("p (c t) -> p c t", c=4))\
                    .then_inc(s["pt_evac"], 1)

            def xt_copy(i, k):
                need(dve, s["x_high"], G * i + k + 1)
                dve.tensor_tensor(xt_l[:, :, k * P:(k + 1) * P], x_bank[:, :].rearrange("p (k t) -> p k t", k=KD),
                                  xt_h[:, :, k * P:(k + 1) * P].bitcast(F32), ALU.subtract)\
                    .then_inc(s["x_low"], 1)

            def scale(n, t, g):
                need(dve, s["s_exp"], PS * n + 2 * g + 2)
                heads = recip[:, t % 2, 4 * g:4 * g + 4]
                dve.reciprocal(heads, total[:, t % 2, 4 * g:4 * g + 4]).then_inc(s["s_recip"], 1)
                need(dve, s["s_recip"], 4 * n + g + 1)
                p = prob[:, t % 2, g, 0:L2, :]
                dve.tensor_tensor(p, p, heads.rearrange("p (k h) -> p k h", k=1).to_broadcast([P, L2, 4]), ALU.mult)\
                    .then_inc(s["s_scaled"], 1)

            def ot_copy(n, u):
                need(dve, s["ot_high"], 2 * n + u + 1)
                dve.tensor_tensor(ot_l[:, 4 * u:4 * u + 4, :], ot_bank[u][:, :].rearrange("p (c t) -> p c t", c=4),
                                  ot_h[:, 4 * u:4 * u + 4, :].bitcast(F32), ALU.subtract).then_inc(s["ot_low"], 1)

            def router(i, first, steps):
                for k, op in enumerate(steps):
                    if first + k:
                        need(dve, s["route_step"], (RS1 + RS2) * i + first + k)
                    op().then_inc(s["route_step"], 1)

            def b8(a):
                return a.rearrange("p (t e) -> p t e", e=1).to_broadcast([P, G, E])

            def route_experts(i):
                revb = rev[:, :].rearrange("p (t e) -> p t e", t=1).to_broadcast([P, G, E])
                need(dve, s["l_evac"], G * (i + 1))
                router(i, 0, [
                    lambda: dve.tensor_reduce(c4["top4"][:, :], logit[:, :, :], AX.X, ALU.max),
                    lambda: dve.tensor_tensor(q_e[:, :, :], logit[:, :, :], b8(c4["top4"][:, :]), ALU.subtract),
                ])
                need(dve, s["route_exp"], i + 1)
                router(i, 2, [
                    lambda: dve.tensor_reduce(c4["sum4"][:, :], p_e[:, :, :], AX.X, ALU.add),
                    lambda: dve.reciprocal(c4["rec4"][:, :], c4["sum4"][:, :]),
                    lambda: dve.tensor_tensor(p_e[:, :, :], p_e[:, :, :], b8(c4["rec4"][:, :]), ALU.mult),
                    lambda: dve.tensor_reduce(c4["gate4"][:, :], p_e[:, :, :], AX.X, ALU.max),
                    lambda: dve.tensor_tensor(q_e[:, :, :], p_e[:, :, :], b8(c4["gate4"][:, :]), ALU.is_ge),
                    lambda: dve.tensor_tensor(q_e[:, :, :], q_e[:, :, :], revb, ALU.mult),
                    lambda: dve.tensor_reduce(c4["rank4"][:, :], q_e[:, :, :], AX.X, ALU.max),
                    lambda: dve.tensor_tensor(onehot[:, :, :], revb, b8(c4["rank4"][:, :]), ALU.is_equal),
                ])

            def route_slots(i):
                need(dve, s["counts_read"], i + 1)
                need(dve, s["rows_free"], i + 1)
                cum, tot = counts[:, 0, :, :], counts[:, 1, :, :]
                pos, keep, slot = c4["pos4"][:, :], c4["keep4"][:, :], c4["slot4"][:, :]
                spare = token_f[:, bass.ds(G * i, G)]
                steps = [lambda k=k: dve.tensor_tensor(before[:, k + 1, :], before[:, k, :], tot[:, k, :], ALU.add)
                         for k in range(G)]
                steps += [
                    lambda: dve.tensor_tensor(q_e[:, :, :], cum, before[:, 0:G, :], ALU.add),
                    lambda: dve.tensor_tensor(q_e[:, :, :], q_e[:, :, :], onehot[:, :, :], ALU.mult),
                    lambda: dve.tensor_reduce(pos, q_e[:, :, :], AX.X, ALU.add),
                    lambda: dve.tensor_scalar(keep, pos, float(CAP), None, ALU.is_lt),
                    lambda: dve.tensor_scalar(slot, c4["rank4"][:, :], -float(CAP), float(CAP * E - T), ALU.mult,
                                              ALU.add),
                    lambda: dve.tensor_tensor(slot, slot, pos, ALU.add),
                    lambda: dve.tensor_tensor(slot, slot, spare, ALU.subtract),
                    lambda: dve.tensor_tensor(slot, slot, keep, ALU.mult),
                    lambda: dve.tensor_copy(before[:, 0, :], before[:, G, :]),
                ]
                assert len(steps) == RS2
                router(i, RS1, steps)
                need(dve, s["route_step"], (RS1 + RS2) * (i + 1))
                dve.scalar_tensor_tensor(slot_idx[:, :], slot, float(T), spare, ALU.add, ALU.add)
                need(dve, s["rows_loaded"], 16 * (i + 1))
                dve.tensor_copy(rows[:, :, D:D + 1], c4["gate4"][:, :].rearrange("p (t a) -> p t a", a=1))
                dve.tensor_scalar(rows[:, :, D + 1:D + 2].bitcast(I32),
                                  token_int[:, bass.ds(G * i, G)].rearrange("p (t a) -> p t a", a=1), 0, None,
                                  ALU.add).then_inc(s["routed"], 1)

            def step(i, *_):
                for t in range(G):
                    n = G * i + t
                    if isinstance(i, int) and i == -1:
                        if t == 2:
                            split(2)
                            split(3)
                            dve.wait_ge(s["raw_low"], NU)
                            dve.memset(prob[:, :, :, L2:PW, :], 0.0).then_inc(s["padded"], 1)

                    def top(j):
                        if tiled(n + 1):
                            need(dve, s["s_done"], PS * (n + 1) + j + 1)
                            dve.tensor_reduce(neg_top[:, (t + 1) % 2, 2 * j:2 * j + 2],
                                              s_bank[j % 2][:, 0:2 * L2].rearrange("p (h k) -> p h k", h=2), AX.X,
                                              ALU.max, negate=True).then_inc(s["s_max"], 1)

                    m, k = n + 7, (t + 3) % G
                    if t < 2 and there(i + 1):
                        xt_copy(i + 1, 2 * t)
                    if tiled(n):
                        pt_copy(n, t, 0)
                    top(0)
                    if tiled(n - 2):
                        need(dve, s["x2_made"], n - 1)
                        norm_stats("y", n - 1, x2[:, t % 2, :], EPS1)
                        need(dve, s["y_turned"], n - 2)
                        norm("y", n - 1, y[:, :], x2[:, t % 2, :]).then_inc(s["y_normed"], 1)
                    if tiled(n):
                        pt_copy(n, t, 2)
                    top(1)
                    if tiled(n - 2):
                        need(dve, s["y_turned"], n - 1)
                        need(dve, s["l_done"], n - 2)
                        dve.tensor_copy(yt[:, :, :], x_bank[:, :].rearrange("p (c t) -> p c t", c=KD))\
                            .then_inc(s["y_evac"], 1)
                    top(2)
                    if tiled(n - 1):
                        need(dve, s["w_done"], n)
                        norm_stats("w", n, w_bank[:, :], EPS2)
                    if tiled(n + 1):
                        scale(n + 1, t + 1, 0)
                    if t < 2 and there(i + 1):
                        xt_copy(i + 1, 2 * t + 1)
                        if isinstance(i, int) and i == -1:
                            split(t)
                    top(3)
                    if tiled(n):
                        pt_copy(n, t, 4)
                    if tiled(n - 1):
                        need(dve, x2_stored[(t + 1) % 2], 16 * (2 * i + (t - 3) // 2 + 1))
                        norm("w", n, x2[:, (t + 1) % 2, :], w_bank[:, :]).then_inc(s["w_normed"], 1)
                    top(4)
                    if tiled(n):
                        ot_copy(n, 0)
                    if tiled(n + 1):
                        scale(n + 1, t + 1, 1)
                    top(5)
                    if there(i + 2 if t else i + 1):
                        need(dve, s[f"x_loaded{k}"], 16 * ((i + 2 if t else i + 1) + 1))
                        norm_stats("x", m + 1, xn[:, k, :], EPS1)
                    if t == 2 and there(i - 1):
                        need(dve, s["counted"], i)
                        need(dve, s["l_done"], capped(n - 1, NT))
                        dve.tensor_copy(counts[:, :, :, :].rearrange("p a t e -> p (a t e)"),
                                        w_bank[:, 64:64 + 2 * G * E]).then_inc(s["counts_read"], 1)
                    if tiled(n - 2):
                        need(dve, s["l_done"], n - 1)
                        dve.tensor_tensor(logit[:, (t + 2) % 4, :], w_bank[:, 0:E], br_b[:, :], ALU.add)\
                            .then_inc(s["l_evac"], 1)
                    top(6)
                    if tiled(n + 1):
                        scale(n + 1, t + 1, 2)
                    top(7)
                    if there(i + 2 if t else i + 1):
                        norm("x", m + 1, xn[:, k, :], xn[:, k, :]).then_inc(s["x_normed"], 1)
                    if tiled(n + 1):
                        scale(n + 1, t + 1, 3)
                    if tiled(n):
                        ot_copy(n, 1)
                    if t == 1 and there(i - 1):
                        route_experts(i - 1)
                    if t == 2 and there(i - 1):
                        route_slots(i - 1)
            run(dve, step)

        @block.tensor
        def _(pe):
            def turn_p(n, t, u):
                if u == 0:
                    need(pe, s["s_scaled"], 4 * (n + 1))
                evac, value = ((s["pt_evac_act"], 2 * n), (s["pt_evac"], 3 * n), (s["pt_evac"], 3 * n + 1),
                               (s["pt_evac_act"], 2 * n + 1), (s["pt_evac"], 3 * n + 2))[u]
                need(pe, evac, value)
                for k in range(4):
                    src = prob[:, t % 2, k, P:PW, :].rearrange("p k h -> p (k h)") if u == 0 else \
                        prob[:, t % 2, u - 1, 0:P, k]
                    last = pe.transpose(pt_bank[(5 * t + u) % 2][:, k * P:(k + 1) * P], src, ident[:, :])
                last.then_inc(s["pt_turned"], 1)

            def scores(n, t, b, j):
                need(pe, s["s_exp"], PS * n + j - 1)
                if t % G == 0:
                    need(pe, s["q_evac"], 2 * n + j + 1)
                pe.matmul(s_bank[j % 2][:, 0:2 * L2], qt[:, j, (t % G) * P:(t % G + 1) * P],
                          k2[:, b, j, :, :].rearrange("p h k -> p (h k)"), start=True, stop=True)\
                    .then_inc(s["s_done"], 1)

            def values(n, b, g):
                need(pe, s["pt_evac"], 3 * n + 1)
                evac, value = ((s["pt_evac_act"], 2 * n + 1), (s["pt_evac"], 3 * n + 2),
                               (s["pt_evac_act"], 2 * n + 2), (s["pt_evac"], 3 * n + 3))[g]
                need(pe, evac, value)
                for c in range(2):
                    o = (2 * (g % 2) + c) * P
                    pe.matmul(ot_bank[g // 2][:, o:o + P], v2_rest[:, b, g, c * P:(c + 1) * P], pt[:, g, :], start=True,
                              stop=False)
                    for h in range(2):
                        head = 4 * g + 2 * c + h
                        last = pe.matmul(ot_bank[g // 2][h * D2:(h + 1) * D2, o:o + P],
                                         v2_main[:, b, head * D2:(head + 1) * D2], pt[:, 4 + head, :], start=False,
                                         stop=True)
                if g % 2:
                    last.then_inc(s["o_done"], 1)

            def queries(i, c):
                need(pe, s["x_low"], G * (i + 1))
                if isinstance(i, int) and i == 0:
                    need(pe, s["raw_low"], 1 + c // 4)
                first = isinstance(i, int) and i == 0
                need(pe, s["q_evac"], c - 1 if first else KI * i + c)
                for k in range(KD):
                    last = product(pe, (w_bank if first and c % 2 else q_bank)[:, :],
                                   [a[:, k, c * P:(c + 1) * P] for a in (wq_h, wq_l)],
                                   [a[:, k, :] for a in (xt_h, xt_l)], k == 0, k == KD - 1)
                last.then_inc(s["q_done"], 1)

            def output(n, first, last_chunk, counts=0):
                if isinstance(n, int) and n == 0:
                    need(pe, s["raw_low"], NU)
                need(pe, s["ot_low"], 2 * n + first // 4 + 1)
                if first == 0:
                    need(pe, s["w_normed"], n)
                    need(pe, s["l_evac"], n - 1)
                    need(pe, s["counts_read"], counts)
                for c in range(first, last_chunk):
                    last = product(pe, w_bank[:, :], [a[:, c, :] for a in (ot_h, ot_l)],
                                   [a[:, c, :] for a in (wo_h, wo_l)], c == 0, c == KI - 1)
                if last_chunk == KI:
                    last.then_inc(s["w_done"], 1)

            def step(i, b, after):
                for t in range(G):
                    n = G * i + t

                    def sc(j):
                        if tiled(n + 1):
                            scores(n + 1, t + 1, b if t < 3 else after, j)
                        if (t, j) in QUERIES and there(i + 1):
                            queries(i + 1, QUERIES[t, j])

                    def turn_x(k):
                        if t < 2 and there(i + 1):
                            need(pe, s["x_normed"], G * (i + 1) + k + 1)
                            need(pe, s["x_low"], G * (i + 1) + k)
                            need(pe, s["ot_low"], 2 * n)
                            need(pe, s["y_evac"], n - 2 + k % 2)
                            for c in range(KD):
                                last = pe.transpose(x_bank[:, c * P:(c + 1) * P], xn[:, k, c * P:(c + 1) * P],
                                                    ident[:, :])
                            last.then_inc(s["x_turned"], 1)

                    def x_read(more):
                        if there(i + 1):
                            need(pe, s["x_low"], G * (i + 1) + (2 * t + more if t < 2 else G))

                    if tiled(n - 1):
                        output(n - 1, 0, 4, i if t == 3 else 0)
                    turn_x(2 * t)
                    if tiled(n):
                        turn_p(n, t, 0)
                        turn_p(n, t, 1)
                    sc(0)
                    if tiled(n - 1):
                        output(n - 1, 4, 6)
                    if tiled(n):
                        turn_p(n, t, 2)
                    sc(1)
                    if tiled(n - 1):
                        output(n - 1, 6, 8)
                    if tiled(n - 2):
                        need(pe, s["y_normed"], n - 1)
                        need(pe, s["ot_low"], capped(2 * n, 2 * NT))
                        x_read(1)
                        for k in range(KD):
                            last = pe.transpose(x_bank[:, k * P:(k + 1) * P], y[:, k * P:(k + 1) * P], ident[:, :])
                        last.then_inc(s["y_turned"], 1)
                    sc(2)
                    if tiled(n):
                        turn_p(n, t, 3)
                        need(pe, s["ot_low"], 2 * n - 1)
                        values(n, b, 0)
                    turn_x(2 * t + 1)
                    sc(3)
                    if tiled(n):
                        turn_p(n, t, 4)
                        values(n, b, 1)
                    sc(4)
                    if tiled(n):
                        need(pe, s["y_evac"], n - 1)
                        x_read(2)
                        values(n, b, 2)
                    sc(5)
                    routed = t == 2 and there(i - 1)
                    if routed or tiled(n - 2):
                        need(pe, s["w_normed"], capped(n, NT))
                    if routed:
                        need(pe, s["route_step"], (RS1 + RS2) * (i - 1) + RS1)
                        oh = onehot[:, :, :].rearrange("p t e -> p (t e)")
                        pe.matmul(w_bank[:, 64:64 + G * E], upper[:, :], oh, start=True, stop=True)
                        pe.matmul(w_bank[:, 64 + G * E:64 + 2 * G * E], ones[:, :], oh, start=True, stop=True)\
                            .then_inc(s["counted"], 1)
                    if tiled(n - 2):
                        need(pe, s["y_evac"], n - 1)
                        for k in range(KD):
                            last = pe.matmul(w_bank[:, 0:E], yt[:, k, :], wr_sb[:, k, :], start=k == 0,
                                             stop=k == KD - 1)
                        last.then_inc(s["l_done"], 1)
                    sc(6)
                    sc(7)
                    if tiled(n):
                        values(n, b, 3)
            run(pe, step)


def experts(nc, sem, sb, bank, slot_tiles, out_rows, w1, b1, w2, b2, ident, minus_half):
    raw = sb("c_raw", [P, 2, 2048])
    w_h = sb("c_w_h", [P, 2, 2, KD, D], F32R)
    w_l = sb("c_w_l", [P, 2, 2, KD, D], F32R)
    b1_col = sb("c_b1", [P, 2, KD])
    b2_b = sb("c_b2", [P, 2, D])
    rows = sb("c_rows", [P, 2, G, ROW])
    gate, token = sb("c_gate", [P, 2, G]), sb("c_token", [P, 2, G], I32)
    y = sb("c_y", [P, G, D])
    base = sb("c_base", [P, 2, G, D])
    xt_h, xt_l = sb("c_xt_h", [P, KD, G * P], F32R), sb("c_xt_l", [P, KD, G * P], F32R)
    h = sb("c_h", [P, 2, G * P])
    ht_h, ht_l = sb("c_ht_h", [P, KD, G * P], F32R), sb("c_ht_l", [P, KD, G * P], F32R)
    res = sb("c_res", [P, G, D])
    stats, mv = sb("c_stats", [P, G, 6]), sb("c_mv", [P, G, 2])
    var_eps, rstd, gain = sb("c_var", [P, G]), sb("c_rstd", [P, G]), sb("c_gain", [P, G])

    names = ("w_loaded0 w_loaded1 w_high w_low b_loaded0 b_loaded1 rows_loaded0 rows_loaded1 stats_done aggr_done "
             "eps_done rstd_done gain_done normed scaled based tails x_turned x_high x_low h_done h_relu h_high h_low "
             "o_done res_made scattered0 scattered1 scattered2 scattered3").split()
    s = {n: sem("c_" + n) for n in names}
    h_bank, x_bank, o_bank = bank[0:2], bank[2:4], bank[4:6]

    def run(eng, prepare, work):
        def pair(p, last):
            for k in range(2):
                work(2 * p + k, k, not (last and k))
        prepare(0, 0)
        pair(0, False)
        with eng.Fori(1, E // 2 - 1) as p:
            pair(p, False)
        pair(E // 2 - 1, True)

    def times(e, par):
        return (e - par) // 2 if isinstance(e, int) else (e - par) >> 1

    block = nc.Block()
    with block as block:
        @block.sync
        def _(sp):
            def load(e, par):
                need(sp, s["based"], G * (e - 1))
                need(sp, s["normed"], G * (e - 1))
                need(sp, s["tails"], e - 1)
                sp.dma_start(rows[:, par, :, :], slot_tiles[:, bass.ds(G * e, G), :])\
                    .then_inc(s[f"rows_loaded{par}"], 16)
                for m, w in enumerate((w1, w2)):
                    need(sp, s["w_low"], 2 * e + m - 1)
                    sp.dma_start(raw[:, m, :].rearrange("p (k n) -> p k n", k=KD),
                                 w[bass.ds(e, 1), :, :].rearrange("a (k p) n -> p (a k) n", p=P))\
                        .then_inc(s[f"w_loaded{m}"], 16)
                need(sp, s["h_relu"], KD * (e - 1))
                need(sp, s["scaled"], G * (e - 1))
                with nc.allow_non_contiguous_dma(reason="a bias by column"):
                    sp.dma_start(b1_col[:, par, :], b1[bass.ds(e, 1), :].rearrange("a (c p) -> p (a c)", p=P))\
                        .then_inc(s[f"b_loaded{par}"], 16)
                sp.dma_start(b2_b[:, par, :], b2[bass.ds(e, 1), :].to_broadcast([P, D]))\
                    .then_inc(s[f"b_loaded{par}"], 16)

            def work(e, par, more):
                if more:
                    load(e + 1, 1 - par)
            run(sp, load, work)

        @block.gpsimd
        def _(pool):
            def prepare(e, par):
                hold(pool, s["eps_done"], e + 1)
                pool.tensor_tensor(rstd[:, :], var_eps[:, :], minus_half[:, :], ALU.pow).then_inc(s["rstd_done"], 1)
                for k in range(G):
                    hold(pool, s["scaled"], G * e + k + 1)
                    pool.tensor_tensor(base[:, par, k, :], base[:, par, k, :], rows[:, par, k, 0:D], ALU.add)\
                        .then_inc(s["based"], 1)

            def work(e, par, more):
                if more:
                    prepare(e + 1, 1 - par)
                for k in range(G):
                    hold(pool, s["res_made"], G * e + k + 1)
                    pool.indirect_dma_start(
                        out=out_rows, out_offset=bass.IndirectOffsetOnAxis(ap=token[:, par, k:k + 1], axis=0),
                        in_=res[:, k, :], in_offset=None, bounds_check=T - 1, oob_is_err=False)\
                        .then_inc(s[f"scattered{k}"], 16)
            run(pool, prepare, work)
            for k in range(G):
                pool.wait_ge(s[f"scattered{k}"], 16 * E)

        @block.scalar
        def _(act):
            def weights(e, par, m):
                need(act, s[f"w_loaded{m}"], 16 * (e + 1))
                act.activation(w_h[:, par, m, :, :], raw[:, m, :].rearrange("p (k n) -> p k n", k=KD), ACT.Copy)\
                    .then_inc(s["w_high"], 1)

            def scale_bias(e, par):
                hold(act, s[f"rows_loaded{par}"], 16 * (times(e, par) + 1))
                hold(act, s[f"b_loaded{par}"], 32 * (times(e, par) + 1))
                hold(act, s["res_made"], G * (e - 1))
                for k in range(G):
                    act.activation(base[:, par, k, :], b2_b[:, par, :], ACT.Copy, scale=rows[:, par, k, D:D + 1])\
                        .then_inc(s["scaled"], 1)

            def xt_copy(e, k):
                need(act, s["x_turned"], G * e + k + 1)
                act.activation(xt_h[:, :, k * P:(k + 1) * P],
                               x_bank[k % 2][:, :].rearrange("p (k t) -> p k t", k=KD), ACT.Copy)\
                    .then_inc(s["x_high"], 1)

            def prepare(e, par):
                weights(e, par, 0)
                for k in range(G):
                    xt_copy(e, k)
                weights(e, par, 1)
                scale_bias(e, par)

            def work(e, par, more):
                hold(act, s[f"b_loaded{par}"], 32 * (times(e, par) + 1))
                for c in range(KD):
                    need(act, s["h_done"], KD * e + c + 1)
                    need(act, s["h_low"], KD * e + c - 1)
                    act.activation(h[:, c % 2, :], h_bank[c % 2][:, :], ACT.Relu, bias=b1_col[:, par, c:c + 1])\
                        .then_inc(s["h_relu"], 1)
                    need(act, s["h_relu"], KD * e + c + 1)
                    act.activation(ht_h[:, c, :], h[:, c % 2, :], ACT.Copy).then_inc(s["h_high"], 1)
                    if c == 1 and more:
                        weights(e + 1, 1 - par, 0)
                if more:
                    scale_bias(e + 1, 1 - par)
                    for k in range(G):
                        xt_copy(e + 1, k)
                    weights(e + 1, 1 - par, 1)
            run(act, prepare, work)

        @block.vector
        def _(dve):
            def row_stats(e, par):
                need(dve, s[f"rows_loaded{par}"], 16 * (times(e, par) + 1))
                for k in range(G):
                    last = dve.bn_stats(stats[:, k, :], rows[:, par, k, 0:D])
                last.then_inc(s["stats_done"], 1)
                hold(dve, s["stats_done"], e + 1)
                for k in range(G):
                    last = dve.bn_aggr(mv[:, k, :], stats[:, k, :])
                last.then_inc(s["aggr_done"], 1)
                need(dve, s["aggr_done"], e + 1)
                dve.tensor_scalar(var_eps[:, :], mv[:, :, 1], EPS1, None, ALU.add).then_inc(s["eps_done"], 1)

            def norm(e, par):
                need(dve, s["rstd_done"], e + 1)
                dve.tensor_tensor(gain[:, :], rstd[:, :], rows[:, par, :, D], ALU.mult).then_inc(s["gain_done"], 1)
                need(dve, s["gain_done"], e + 1)
                need(dve, s["x_turned"], G * e)
                for k in range(G):
                    dve.tensor_scalar(y[:, k, :], rows[:, par, k, 0:D], mv[:, k, 0:1], gain[:, k:k + 1],
                                      ALU.subtract, ALU.mult).then_inc(s["normed"], 1)

            def weights(e, par, m):
                need(dve, s["w_high"], 2 * e + m + 1)
                dve.tensor_tensor(w_l[:, par, m, :, :], raw[:, m, :].rearrange("p (k n) -> p k n", k=KD),
                                  w_h[:, par, m, :, :].bitcast(F32), ALU.subtract).then_inc(s["w_low"], 1)

            def tail(e, par):
                for k in range(G):
                    hold(dve, s[f"scattered{k}"], 16 * (e - 1))
                dve.tensor_copy(gate[:, par, :], rows[:, par, :, D])
                dve.tensor_scalar(token[:, par, :], rows[:, par, :, D + 1].bitcast(I32), 0, None, ALU.add)\
                    .then_inc(s["tails"], 1)

            def xt_copy(e, k):
                need(dve, s["x_high"], G * e + k + 1)
                dve.tensor_tensor(xt_l[:, :, k * P:(k + 1) * P],
                                  x_bank[k % 2][:, :].rearrange("p (k t) -> p k t", k=KD),
                                  xt_h[:, :, k * P:(k + 1) * P].bitcast(F32), ALU.subtract)\
                    .then_inc(s["x_low"], 1)

            def prepare(e, par):
                row_stats(e, par)
                norm(e, par)
                weights(e, par, 0)
                for k in range(G):
                    xt_copy(e, k)
                tail(e, par)
                weights(e, par, 1)

            def h_low(e, c):
                need(dve, s["h_high"], KD * e + c + 1)
                dve.tensor_tensor(ht_l[:, c, :], h[:, c % 2, :], ht_h[:, c, :].bitcast(F32), ALU.subtract)\
                    .then_inc(s["h_low"], 1)

            def finish(e, par, k):
                need(dve, s["o_done"], G * e + k + 1)
                need(dve, s["based"], G * e + k + 1)
                need(dve, s["tails"], e + 1)
                need(dve, s[f"scattered{k}"], 16 * e)
                dve.scalar_tensor_tensor(res[:, k, :], o_bank[k % 2][:, :], gate[:, par, k:k + 1],
                                         base[:, par, k, :], ALU.mult, ALU.add).then_inc(s["res_made"], 1)

            def work(e, par, more):
                if more:
                    row_stats(e + 1, 1 - par)
                h_low(e, 0)
                h_low(e, 1)
                if more:
                    norm(e + 1, 1 - par)
                h_low(e, 2)
                if more:
                    weights(e + 1, 1 - par, 0)
                h_low(e, 3)
                if more:
                    tail(e + 1, 1 - par)
                for k in range(G):
                    finish(e, par, k)
                    if more:
                        for n in ((0, 1), (2,), (3,), ())[k]:
                            xt_copy(e + 1, n)
                if more:
                    weights(e + 1, 1 - par, 1)
            run(dve, prepare, work)

        @block.tensor
        def _(pe):
            def turn(e, k):
                need(pe, s["normed"], G * e + k + 1)
                need(pe, s["x_low"], G * e + k - 1)
                for c in range(KD):
                    last = pe.transpose(x_bank[k % 2][:, c * P:(c + 1) * P], y[:, k, c * P:(c + 1) * P], ident[:, :])
                last.then_inc(s["x_turned"], 1)

            def prepare(e, par):
                for k in range(G):
                    turn(e, k)

            def work(e, par, more):
                need(pe, s["w_low"], 2 * e + 1)
                need(pe, s["x_low"], G * (e + 1))
                for c in range(KD):
                    need(pe, s["h_relu"], KD * e + c - 1)
                    for k in range(KD):
                        last = product(pe, h_bank[c % 2][:, :],
                                       [a[:, par, 0, k, c * P:(c + 1) * P] for a in (w_h, w_l)],
                                       [a[:, k, :] for a in (xt_h, xt_l)], k == 0, k == KD - 1)
                    last.then_inc(s["h_done"], 1)
                need(pe, s["w_low"], 2 * e + 2)
                for k in range(G):
                    need(pe, s["res_made"], G * e + k - 1)
                    for c in range(KD):
                        if k == 0:
                            need(pe, s["h_low"], KD * e + c + 1)
                        last = product(pe, o_bank[k % 2][:, :], [a[:, c, k * P:(k + 1) * P] for a in (ht_h, ht_l)],
                                       [a[:, par, 1, c, :] for a in (w_h, w_l)], c == 0, c == KD - 1)
                    last.then_inc(s["o_done"], 1)
                    if more:
                        for n in ((0, 1), (2,), (3,), ())[k]:
                            turn(e + 1, n)
            run(pe, prepare, work)


_INS = ['x', 'ctx_2048', 'L0_attn_Wqkv', 'L0_attn_bqkv', 'L0_attn_Wproj', 'L0_attn_bproj', 'L0_attn_mapping',
        'L0_xattn_Wq', 'L0_xattn_Wkv', 'L0_xattn_null_kv', 'L0_xattn_Wout', 'L0_xattn_ln_scale', 'L0_xattn_ln_bias',
        'L0_ffn_Wr', 'L0_ffn_br', 'L0_ffn_W1', 'L0_ffn_b1', 'L0_ffn_W2', 'L0_ffn_b2']


def kernel(**inputs):
    import numpy as _np
    import concourse.bacc as _bacc
    from concourse import mybir as _mybir
    from concourse.bass_utils import run_bass_kernel_spmd as _run

    nc = _bacc.Bacc("TRN2", target_bir_lowering=False, num_devices=1)
    arrays, args = {}, []
    for name in _INS:
        a = _np.ascontiguousarray(inputs[name])
        arrays[f"in_{name}_dram"] = a
        args.append(nc.dram_tensor(f"in_{name}_dram", a.shape, _mybir.dt.from_np(a.dtype), kind="ExternalInput").ap())
    args.append(nc.dram_tensor("out_0_dram", (B, M, D), F32, kind="ExternalOutput").ap())
    decoder_kernel(nc, *args)
    r = _run(nc, [arrays], core_ids=[0])
    return r.results[0]["out_0_dram"]
```
